# Optimizing a Trainium2 kernel written in Bass

```python
import numpy as np
import jax
import jax.numpy as jnp

def _softmax(x, axis=-1):
    return jax.nn.softmax(x, axis=axis)

def _gelu(x):
    return jax.nn.gelu(x, approximate=True)

def _silu(x):
    return jax.nn.silu(x)

def _sigmoid(x):
    return jax.nn.sigmoid(x)

def _layernorm(x, axis=-1, eps=1e-05):
    m = jnp.mean(x, axis=axis, keepdims=True)
    v = jnp.var(x, axis=axis, keepdims=True)
    return (x - m) / jnp.sqrt(v + eps)

def _scatter_add(tgt, idx, src, axis=0):
    return tgt.at[idx].add(src)

def _segment_sum(src, seg, n):
    return jax.ops.segment_sum(src, seg, n)
kernel_name = 'mk_macaron_d2_jaxref_r8_976b86'

def setup_inputs(seed: int=0):
    np.random.seed(seed)
    _w = jnp.asarray

    def _L0_attn_setup():
        import jax, jax.numpy as jnp
        import numpy as np
        B, S, IN, H = (8, 256, 128, 128)
        W_SCALE = 0.02
        LN_EPS = 1e-05

        def _reference_tuple_inner(x, Wi, bi, Wf, bf, Wg, bg, Wo, bo, Weg, beg, gamma, beta):
            Bsz, Slen, In = x.shape
            Hs = Wi.shape[1]
            Wix, Wih = (Wi[:In], Wi[In:])
            Wfx, Wfh = (Wf[:In], Wf[In:])
            Wgx, Wgh = (Wg[:In], Wg[In:])
            Wox, Woh = (Wo[:In], Wo[In:])
            xi = jnp.einsum('bsi,ih->bsh', x, Wix) + bi
            xf = jnp.einsum('bsi,ih->bsh', x, Wfx) + bf
            xg = jnp.einsum('bsi,ih->bsh', x, Wgx) + bg
            xo = jnp.einsum('bsi,ih->bsh', x, Wox) + bo

            def step(carry, inp):
                h, c, n = carry
                xi_t, xf_t, xg_t, xo_t = inp
                i_t = jax.nn.sigmoid(xi_t + h @ Wih)
                f_t = jax.nn.sigmoid(xf_t + h @ Wfh)
                g_t = jnp.tanh(xg_t + h @ Wgh)
                o_t = jax.nn.sigmoid(xo_t + h @ Woh)
                c_t = f_t * c + i_t * g_t
                n_t = f_t * n + i_t * jnp.exp(g_t @ Weg + beg)
                h_t = o_t * (c_t / n_t)
                return ((h_t, c_t, n_t), h_t)
            zeros = jnp.zeros((Bsz, Hs), x.dtype)
            carry0 = (zeros, zeros, zeros)
            inps = (jnp.swapaxes(xi, 0, 1), jnp.swapaxes(xf, 0, 1), jnp.swapaxes(xg, 0, 1), jnp.swapaxes(xo, 0, 1))
            (h_f, c_f, n_f), hs = jax.lax.scan(step, carry0, inps)
            output = jnp.swapaxes(hs, 0, 1)
            y = output + x
            mu = jnp.mean(y, axis=-1, keepdims=True)
            var = jnp.mean(jnp.square(y - mu), axis=-1, keepdims=True)
            out = (y - mu) * jax.lax.rsqrt(var + LN_EPS) * gamma + beta
            return (out, h_f, c_f, n_f)
        key = jax.random.key(seed)
        ks = jax.random.split(key, 8)
        x = jax.random.normal(ks[0], (B, S, IN), dtype=jnp.float32)

        def w(k, shape):
            return jax.random.normal(k, shape, dtype=jnp.float32) * W_SCALE
        return {'x': x, 'Wi': w(ks[1], (IN + H, H)), 'bi': jnp.zeros((H,), jnp.float32), 'Wf': w(ks[2], (IN + H, H)), 'bf': jnp.zeros((H,), jnp.float32), 'Wg': w(ks[3], (IN + H, H)), 'bg': jnp.zeros((H,), jnp.float32), 'Wo': w(ks[4], (IN + H, H)), 'bo': jnp.zeros((H,), jnp.float32), 'Weg': w(ks[5], (H, H)), 'beg': jnp.zeros((H,), jnp.float32), 'gamma': jnp.ones((H,), jnp.float32), 'beta': jnp.zeros((H,), jnp.float32)}
    _L0_attn_in = _L0_attn_setup()

    def _L0_ffn_setup():
        import jax, jax.numpy as jnp
        import numpy as np
        DIM = 128
        DEPTH = 6
        HEADS = 16
        DIM_HEAD = 64
        WINDOW = 32
        INNER = HEADS * DIM_HEAD
        DIM_INNER = int(DIM * 4 * 2 / 3)
        QK_SCALE = 8.0

        def shift_tokens(t):
            a, s = jnp.split(t, 2, -1)
            s = jnp.pad(s, ((0, 0), (1, 0), (0, 0)))[:, :-1]
            return jnp.concatenate([a, s], -1)

        def l2norm(t):
            return t / jnp.maximum(jnp.linalg.norm(t, axis=-1, keepdims=True), 1e-12)

        def rotate_half(x):
            x1, x2 = jnp.split(x, 2, -1)
            return jnp.concatenate([-x2, x1], -1)

        def rotary_tables(n):
            half = jnp.arange(0, DIM_HEAD, 2, dtype=jnp.float32)
            inv_freq = 1.0 / 10000.0 ** (half / DIM_HEAD)
            t = jnp.arange(n, dtype=jnp.float32)
            freqs = t[:, None] * inv_freq[None, :]
            freqs = jnp.concatenate([freqs, freqs], -1)
            base_scale = (half + 0.4 * DIM_HEAD) / (1.4 * DIM_HEAD)
            power = (t - n // 2) / (WINDOW // 2)
            scale = base_scale[None, :] ** power[:, None]
            scale = jnp.concatenate([scale, scale], -1)
            return (freqs, scale)

        def local_attention(q, k, v):
            b, h, n, d = q.shape
            w = WINDOW
            nw = n // w
            bq = q.reshape(b, h, nw, w, d)
            bk = k.reshape(b, h, nw, w, d)
            bv = v.reshape(b, h, nw, w, d)

            def look(t):
                p = jnp.pad(t, ((0, 0), (0, 0), (1, 0), (0, 0), (0, 0)))
                return jnp.concatenate([p[:, :, :nw], p[:, :, 1:]], axis=3)
            bk2, bv2 = (look(bk), look(bv))
            seq = jnp.arange(n).reshape(nw, w)
            seq_p = jnp.pad(seq, ((1, 0), (0, 0)), constant_values=-1)
            jt = jnp.concatenate([seq_p[:nw], seq_p[1:]], axis=1)
            it = seq[:, :, None]
            jb = jt[:, None, :]
            mask = (it < jb) | (it > jb + w) | (jb == -1)
            sim = jnp.einsum('bhwie,bhwje->bhwij', bq, bk2) * QK_SCALE
            sim = jnp.where(mask, -jnp.finfo(sim.dtype).max, sim)
            attn = jax.nn.softmax(sim, -1)
            out = jnp.einsum('bhwij,bhwje->bhwie', attn, bv2)
            return out.reshape(b, h, n, d)

        def attn_layer(x, Wqkv, qs, ksc, Wo):
            b, n, _ = x.shape
            qkv = x @ Wqkv
            q, k, v = jnp.split(qkv, 3, -1)
            sh = lambda t: t.reshape(b, n, HEADS, DIM_HEAD).transpose(0, 2, 1, 3)
            q, k, v = (sh(q), sh(k), sh(v))
            q = l2norm(q) * qs
            k = l2norm(k) * ksc
            freqs, scale = rotary_tables(n)
            cos, sin = (jnp.cos(freqs), jnp.sin(freqs))
            q = q * cos * scale + rotate_half(q) * sin * scale
            inv = 1.0 / scale
            k = k * cos * inv + rotate_half(k) * sin * inv
            out = local_attention(q, k, v)
            out = out.transpose(0, 2, 1, 3).reshape(b, n, INNER)
            return out @ Wo

        def ffn_layer(x, g, bln, W1, b1, W2, b2):
            mu = x.mean(-1, keepdims=True)
            var = ((x - mu) ** 2).mean(-1, keepdims=True)
            xn = (x - mu) / jnp.sqrt(var + 1e-05) * g + bln
            hg = xn @ W1 + b1
            a, gate = jnp.split(hg, 2, -1)
            return a * jax.nn.gelu(gate, approximate=False) @ W2 + b2
        key = jax.random.key(seed)
        ks = jax.random.split(key, 8)
        B, N = (2, 256)
        init = lambda k, shape: jax.random.normal(k, shape, jnp.float32) * 0.02
        return {'x': jax.random.normal(ks[0], (B, N, DIM), jnp.float32), 'Wqkv': init(ks[1], (DEPTH, DIM, 3 * INNER)), 'q_scale': jnp.ones((DEPTH, DIM_HEAD), jnp.float32), 'k_scale': jnp.ones((DEPTH, DIM_HEAD), jnp.float32), 'Wo': init(ks[2], (DEPTH, INNER, DIM)), 'ln_g': jnp.ones((DEPTH, DIM), jnp.float32), 'ln_b': jnp.zeros((DEPTH, DIM), jnp.float32), 'W1': init(ks[3], (DEPTH, DIM, 2 * DIM_INNER)), 'b1': jnp.zeros((DEPTH, 2 * DIM_INNER), jnp.float32), 'W2': init(ks[4], (DEPTH, DIM_INNER, DIM)), 'b2': jnp.zeros((DEPTH, DIM), jnp.float32)}
    _L0_ffn_in = _L0_ffn_setup()

    def _L1_attn_setup():
        import jax, jax.numpy as jnp
        import numpy as np
        D = 128
        K_LOW1 = D // 4
        K_LOW2 = D // 4

        def mix_precision_matmul(x, w):
            d = x.shape[-1]
            w1 = w[:K_LOW1]
            wh = w[K_LOW1:d - K_LOW2]
            w2 = w[d - K_LOW2:]
            y1 = jnp.matmul(x[..., :K_LOW1].astype(jnp.float16), w1.astype(jnp.float16)).astype(jnp.float32)
            yh = jnp.matmul(x[..., K_LOW1:d - K_LOW2], wh)
            y2 = jnp.matmul(x[..., d - K_LOW2:].astype(jnp.float16), w2.astype(jnp.float16)).astype(jnp.float32)
            return y1 + yh + y2
        key = jax.random.key(seed)
        k1, k2, k3, k4 = jax.random.split(key, 4)
        B, N, d = (8, 256, D)
        x = jax.random.normal(k1, (B, N, d), dtype=jnp.float32)
        weight_qkv = jax.random.normal(k2, (d, 3 * d), dtype=jnp.float32) * d ** (-0.5)
        out_w = jax.random.normal(k3, (d, d), dtype=jnp.float32) * d ** (-0.5)
        out_b = jax.random.normal(k4, (d,), dtype=jnp.float32) * 0.01
        return {'x': x, 'weight_qkv': weight_qkv, 'out_w': out_w, 'out_b': out_b}
    _L1_attn_in = _L1_attn_setup()

    def _L1_ffn_setup():
        import jax, jax.numpy as jnp
        import numpy as np
        B, S, D, DO = (4, 256, 128, 128)
        E, K = (20, 2)
        key = jax.random.key(seed)
        ks = jax.random.split(key, 6)
        sc_d = 1.0 / np.sqrt(D)
        sc_h = 1.0 / np.sqrt(D // 4)
        return {'x': jax.random.normal(ks[0], (B, S, D), jnp.float32), 'wg1': jax.random.normal(ks[1], (D, D // 4), jnp.float32) * sc_d, 'bg1': jnp.zeros((D // 4,), jnp.float32), 'wg2': jax.random.normal(ks[2], (D // 4, 2 * E), jnp.float32) * sc_h, 'bg2': jnp.zeros((2 * E,), jnp.float32), 'We': jax.random.normal(ks[3], (E, D, DO), jnp.float32) * sc_d, 'be': jnp.zeros((E, DO), jnp.float32)}
    _L1_ffn_in = _L1_ffn_setup()
    _d = {'L0_attn_x': _L0_attn_in['x'], 'L0_attn_Wi': _L0_attn_in['Wi'], 'L0_attn_bi': _L0_attn_in['bi'], 'L0_attn_Wf': _L0_attn_in['Wf'], 'L0_attn_bf': _L0_attn_in['bf'], 'L0_attn_Wg': _L0_attn_in['Wg'], 'L0_attn_bg': _L0_attn_in['bg'], 'L0_attn_Wo': _L0_attn_in['Wo'], 'L0_attn_bo': _L0_attn_in['bo'], 'L0_attn_Weg': _L0_attn_in['Weg'], 'L0_attn_beg': _L0_attn_in['beg'], 'L0_attn_gamma': _L0_attn_in['gamma'], 'L0_attn_beta': _L0_attn_in['beta'], 'L0_ffn_Wqkv': _L0_ffn_in['Wqkv'], 'L0_ffn_q_scale': _L0_ffn_in['q_scale'], 'L0_ffn_k_scale': _L0_ffn_in['k_scale'], 'L0_ffn_Wo': _L0_ffn_in['Wo'], 'L0_ffn_ln_g': _L0_ffn_in['ln_g'], 'L0_ffn_ln_b': _L0_ffn_in['ln_b'], 'L0_ffn_W1': _L0_ffn_in['W1'], 'L0_ffn_b1': _L0_ffn_in['b1'], 'L0_ffn_W2': _L0_ffn_in['W2'], 'L0_ffn_b2': _L0_ffn_in['b2'], 'L1_attn_weight_qkv': _L1_attn_in['weight_qkv'], 'L1_attn_out_w': _L1_attn_in['out_w'], 'L1_attn_out_b': _L1_attn_in['out_b'], 'L1_ffn_wg1': _L1_ffn_in['wg1'], 'L1_ffn_bg1': _L1_ffn_in['bg1'], 'L1_ffn_wg2': _L1_ffn_in['wg2'], 'L1_ffn_bg2': _L1_ffn_in['bg2'], 'L1_ffn_We': _L1_ffn_in['We'], 'L1_ffn_be': _L1_ffn_in['be']}
    _x0 = _d['L0_attn_x']
    _d['L0_attn_x'] = jax.random.normal(jax.random.fold_in(jax.random.key(seed), 1), (2, 1024, 128), dtype=_x0.dtype)
    del _x0
    return _d

def reference(L0_attn_x, L0_attn_Wi, L0_attn_bi, L0_attn_Wf, L0_attn_bf, L0_attn_Wg, L0_attn_bg, L0_attn_Wo, L0_attn_bo, L0_attn_Weg, L0_attn_beg, L0_attn_gamma, L0_attn_beta, L0_ffn_Wqkv, L0_ffn_q_scale, L0_ffn_k_scale, L0_ffn_Wo, L0_ffn_ln_g, L0_ffn_ln_b, L0_ffn_W1, L0_ffn_b1, L0_ffn_W2, L0_ffn_b2, L1_attn_weight_qkv, L1_attn_out_w, L1_attn_out_b, L1_ffn_wg1, L1_ffn_bg1, L1_ffn_wg2, L1_ffn_bg2, L1_ffn_We, L1_ffn_be):

    def _L0_attn_ref(x, Wi, bi, Wf, bf, Wg, bg, Wo, bo, Weg, beg, gamma, beta):
        import jax, jax.numpy as jnp
        import numpy as np
        B, S, IN, H = (8, 256, 128, 128)
        W_SCALE = 0.02
        LN_EPS = 1e-05

        def _reference_tuple_inner(x, Wi, bi, Wf, bf, Wg, bg, Wo, bo, Weg, beg, gamma, beta):
            Bsz, Slen, In = x.shape
            Hs = Wi.shape[1]
            Wix, Wih = (Wi[:In], Wi[In:])
            Wfx, Wfh = (Wf[:In], Wf[In:])
            Wgx, Wgh = (Wg[:In], Wg[In:])
            Wox, Woh = (Wo[:In], Wo[In:])
            xi = jnp.einsum('bsi,ih->bsh', x, Wix) + bi
            xf = jnp.einsum('bsi,ih->bsh', x, Wfx) + bf
            xg = jnp.einsum('bsi,ih->bsh', x, Wgx) + bg
            xo = jnp.einsum('bsi,ih->bsh', x, Wox) + bo

            def step(carry, inp):
                h, c, n = carry
                xi_t, xf_t, xg_t, xo_t = inp
                i_t = jax.nn.sigmoid(xi_t + h @ Wih)
                f_t = jax.nn.sigmoid(xf_t + h @ Wfh)
                g_t = jnp.tanh(xg_t + h @ Wgh)
                o_t = jax.nn.sigmoid(xo_t + h @ Woh)
                c_t = f_t * c + i_t * g_t
                n_t = f_t * n + i_t * jnp.exp(g_t @ Weg + beg)
                h_t = o_t * (c_t / n_t)
                return ((h_t, c_t, n_t), h_t)
            zeros = jnp.zeros((Bsz, Hs), x.dtype)
            carry0 = (zeros, zeros, zeros)
            inps = (jnp.swapaxes(xi, 0, 1), jnp.swapaxes(xf, 0, 1), jnp.swapaxes(xg, 0, 1), jnp.swapaxes(xo, 0, 1))
            (h_f, c_f, n_f), hs = jax.lax.scan(step, carry0, inps)
            output = jnp.swapaxes(hs, 0, 1)
            y = output + x
            mu = jnp.mean(y, axis=-1, keepdims=True)
            var = jnp.mean(jnp.square(y - mu), axis=-1, keepdims=True)
            out = (y - mu) * jax.lax.rsqrt(var + LN_EPS) * gamma + beta
            return (out, h_f, c_f, n_f)
        return _reference_tuple_inner(x, Wi, bi, Wf, bf, Wg, bg, Wo, bo, Weg, beg, gamma, beta)[0]

    def _L0_ffn_ref(x, Wqkv, q_scale, k_scale, Wo, ln_g, ln_b, W1, b1, W2, b2):
        import jax, jax.numpy as jnp
        import numpy as np
        DIM = 128
        DEPTH = 6
        HEADS = 16
        DIM_HEAD = 64
        WINDOW = 32
        INNER = HEADS * DIM_HEAD
        DIM_INNER = int(DIM * 4 * 2 / 3)
        QK_SCALE = 8.0

        def shift_tokens(t):
            a, s = jnp.split(t, 2, -1)
            s = jnp.pad(s, ((0, 0), (1, 0), (0, 0)))[:, :-1]
            return jnp.concatenate([a, s], -1)

        def l2norm(t):
            return t / jnp.maximum(jnp.linalg.norm(t, axis=-1, keepdims=True), 1e-12)

        def rotate_half(x):
            x1, x2 = jnp.split(x, 2, -1)
            return jnp.concatenate([-x2, x1], -1)

        def rotary_tables(n):
            half = jnp.arange(0, DIM_HEAD, 2, dtype=jnp.float32)
            inv_freq = 1.0 / 10000.0 ** (half / DIM_HEAD)
            t = jnp.arange(n, dtype=jnp.float32)
            freqs = t[:, None] * inv_freq[None, :]
            freqs = jnp.concatenate([freqs, freqs], -1)
            base_scale = (half + 0.4 * DIM_HEAD) / (1.4 * DIM_HEAD)
            power = (t - n // 2) / (WINDOW // 2)
            scale = base_scale[None, :] ** power[:, None]
            scale = jnp.concatenate([scale, scale], -1)
            return (freqs, scale)

        def local_attention(q, k, v):
            b, h, n, d = q.shape
            w = WINDOW
            nw = n // w
            bq = q.reshape(b, h, nw, w, d)
            bk = k.reshape(b, h, nw, w, d)
            bv = v.reshape(b, h, nw, w, d)

            def look(t):
                p = jnp.pad(t, ((0, 0), (0, 0), (1, 0), (0, 0), (0, 0)))
                return jnp.concatenate([p[:, :, :nw], p[:, :, 1:]], axis=3)
            bk2, bv2 = (look(bk), look(bv))
            seq = jnp.arange(n).reshape(nw, w)
            seq_p = jnp.pad(seq, ((1, 0), (0, 0)), constant_values=-1)
            jt = jnp.concatenate([seq_p[:nw], seq_p[1:]], axis=1)
            it = seq[:, :, None]
            jb = jt[:, None, :]
            mask = (it < jb) | (it > jb + w) | (jb == -1)
            sim = jnp.einsum('bhwie,bhwje->bhwij', bq, bk2) * QK_SCALE
            sim = jnp.where(mask, -jnp.finfo(sim.dtype).max, sim)
            attn = jax.nn.softmax(sim, -1)
            out = jnp.einsum('bhwij,bhwje->bhwie', attn, bv2)
            return out.reshape(b, h, n, d)

        def attn_layer(x, Wqkv, qs, ksc, Wo):
            b, n, _ = x.shape
            qkv = x @ Wqkv
            q, k, v = jnp.split(qkv, 3, -1)
            sh = lambda t: t.reshape(b, n, HEADS, DIM_HEAD).transpose(0, 2, 1, 3)
            q, k, v = (sh(q), sh(k), sh(v))
            q = l2norm(q) * qs
            k = l2norm(k) * ksc
            freqs, scale = rotary_tables(n)
            cos, sin = (jnp.cos(freqs), jnp.sin(freqs))
            q = q * cos * scale + rotate_half(q) * sin * scale
            inv = 1.0 / scale
            k = k * cos * inv + rotate_half(k) * sin * inv
            out = local_attention(q, k, v)
            out = out.transpose(0, 2, 1, 3).reshape(b, n, INNER)
            return out @ Wo

        def ffn_layer(x, g, bln, W1, b1, W2, b2):
            mu = x.mean(-1, keepdims=True)
            var = ((x - mu) ** 2).mean(-1, keepdims=True)
            xn = (x - mu) / jnp.sqrt(var + 1e-05) * g + bln
            hg = xn @ W1 + b1
            a, gate = jnp.split(hg, 2, -1)
            return a * jax.nn.gelu(gate, approximate=False) @ W2 + b2
        for i in range(DEPTH):
            x = attn_layer(shift_tokens(x), Wqkv[i], q_scale[i], k_scale[i], Wo[i]) + x
            x = ffn_layer(shift_tokens(x), ln_g[i], ln_b[i], W1[i], b1[i], W2[i], b2[i]) + x
        return x

    def _L1_attn_ref(x, weight_qkv, out_w, out_b):
        import jax, jax.numpy as jnp
        import numpy as np
        D = 128
        K_LOW1 = D // 4
        K_LOW2 = D // 4

        def mix_precision_matmul(x, w):
            d = x.shape[-1]
            w1 = w[:K_LOW1]
            wh = w[K_LOW1:d - K_LOW2]
            w2 = w[d - K_LOW2:]
            y1 = jnp.matmul(x[..., :K_LOW1].astype(jnp.float16), w1.astype(jnp.float16)).astype(jnp.float32)
            yh = jnp.matmul(x[..., K_LOW1:d - K_LOW2], wh)
            y2 = jnp.matmul(x[..., d - K_LOW2:].astype(jnp.float16), w2.astype(jnp.float16)).astype(jnp.float32)
            return y1 + yh + y2
        d = x.shape[-1]
        qkv = mix_precision_matmul(x, weight_qkv)
        q, k, v = jnp.split(qkv, 3, axis=-1)
        q = q / jnp.sqrt(jnp.asarray(d, dtype=q.dtype))
        qk = jnp.einsum('bqd,bkd->bqk', q, k)
        s = jax.nn.softmax(qk, axis=-1)
        y = jnp.einsum('bqk,bkd->bqd', s, v)
        return jnp.matmul(y, out_w.T) + out_b

    def _L1_ffn_ref(x, wg1, bg1, wg2, bg2, We, be):
        import jax, jax.numpy as jnp
        import numpy as np
        B, S, D, DO = (4, 256, 128, 128)
        E, K = (20, 2)
        Bv, Sv, Dv = x.shape
        xf = x.reshape(-1, Dv)
        h = jax.nn.gelu(xf @ wg1 + bg1, approximate=False)
        logits = (xf @ 0.0 + (h @ wg2 + bg2))[:, :E] if False else (h @ wg2 + bg2)[:, :E]
        probs = jax.nn.softmax(logits, axis=-1)
        top_vals, top_idx = jax.lax.top_k(probs, K)
        N = xf.shape[0]
        gates = jnp.zeros((N, E), xf.dtype).at[jnp.arange(N)[:, None], top_idx].set(top_vals)

        def body(y, eb):
            We_e, be_e, g_e = eb
            return (y + g_e[:, None] * (xf @ We_e + be_e), None)
        y0 = jnp.zeros((N, be.shape[-1]), xf.dtype)
        y, _ = jax.lax.scan(body, y0, (We, be, gates.T))
        return y.reshape(Bv, Sv, -1)
    x = L0_attn_x
    x = x + 0.5 * _L0_ffn_ref(_layernorm(x, axis=-1), L0_ffn_Wqkv, L0_ffn_q_scale, L0_ffn_k_scale, L0_ffn_Wo, L0_ffn_ln_g, L0_ffn_ln_b, L0_ffn_W1, L0_ffn_b1, L0_ffn_W2, L0_ffn_b2)
    x = x + _L0_attn_ref(_layernorm(x, axis=-1), L0_attn_Wi, L0_attn_bi, L0_attn_Wf, L0_attn_bf, L0_attn_Wg, L0_attn_bg, L0_attn_Wo, L0_attn_bo, L0_attn_Weg, L0_attn_beg, L0_attn_gamma, L0_attn_beta)
    x = x + 0.5 * _L0_ffn_ref(_layernorm(x, axis=-1), L0_ffn_Wqkv, L0_ffn_q_scale, L0_ffn_k_scale, L0_ffn_Wo, L0_ffn_ln_g, L0_ffn_ln_b, L0_ffn_W1, L0_ffn_b1, L0_ffn_W2, L0_ffn_b2)
    x = x + 0.5 * _L1_ffn_ref(_layernorm(x, axis=-1), L1_ffn_wg1, L1_ffn_bg1, L1_ffn_wg2, L1_ffn_bg2, L1_ffn_We, L1_ffn_be)
    x = x + _L1_attn_ref(_layernorm(x, axis=-1), L1_attn_weight_qkv, L1_attn_out_w, L1_attn_out_b)
    x = x + 0.5 * _L1_ffn_ref(_layernorm(x, axis=-1), L1_ffn_wg1, L1_ffn_bg1, L1_ffn_wg2, L1_ffn_bg2, L1_ffn_We, L1_ffn_be)
    return x

_drawn_inputs = setup_inputs


def setup_inputs(seed=0):
    import zlib

    import numpy as np

    out = dict(_drawn_inputs(seed))
    spreads = {'L0_attn_bi': (0.0, 2.0),
     'L0_attn_bf': (0.0, 2.0),
     'L0_attn_bg': (0.0, 0.402),
     'L0_attn_bo': (0.0, 2.0),
     'L0_attn_beg': (0.0, 0.8),
     'L0_attn_gamma': (1.0, 0.2),
     'L0_attn_beta': (0.0, 0.426),
     'L0_ffn_q_scale': (1.0, 0.6),
     'L0_ffn_k_scale': (1.0, 0.6),
     'L0_ffn_ln_g': (1.0, 0.6),
     'L0_ffn_ln_b': (0.0, 0.8),
     'L0_ffn_b1': (0.0, 0.8),
     'L0_ffn_b2': (0.0, 0.1),
     'L1_ffn_bg1': (0.0, 1.691),
     'L1_ffn_bg2': (0.0, 0.963),
     'L1_ffn_be': (0.0, 0.8)}
    factors = {'L0_attn_Wi': 23.517,
     'L0_attn_Wf': 8.0,
     'L0_attn_Wo': 8.0,
     'L0_attn_Weg': 8.0,
     'L0_ffn_W1': 3.54,
     'L0_ffn_W2': 3.45,
     'L1_attn_out_b': 35.035}
    for name, (base, spread) in spreads.items():
        noise = np.random.default_rng([zlib.crc32(name.encode()), seed]).standard_normal(out[name].shape)
        drawn = base * np.exp(spread * noise) if base else spread * noise
        out[name] = jnp.asarray(drawn.astype(out[name].dtype))
    for name, factor in factors.items():
        out[name] = (out[name] * factor).astype(out[name].dtype)
    return out
```

```python
from contextlib import ExitStack

import numpy as np

import concourse.bass as bass
from concourse import mybir

F32 = mybir.dt.float32
F16 = mybir.dt.float16
BF16 = mybir.dt.bfloat16
I32 = mybir.dt.int32
ALU = mybir.AluOpType
ACT = mybir.ActivationFunctionType
AX = mybir.AxisListType

P = 128
B, T = 2, 1024
NT = T // P
DEPTH, HEADS, DH, WIN = 6, 16, 64, 32
PAIRS = HEADS // 2
NW = P // WIN
KEYS = 2 * WIN
INNER = HEADS * DH
FF = int(P * 4 * 2 / 3)
FFC = [(0, 128), (128, 128), (256, FF - 256)]
PAD = WIN + 1
GT = 512
NG = T // GT
QK_SCALE = 8.0
RSQRT_SEED = 1597463007.0
NEWTON = 12
NEG = -1e30
LV = 9
CH = 16

EXPERTS, TOPK, GH = 20, 2, 32


def rope_tables():
    half = np.arange(0, DH, 2, dtype=np.float32)
    inv_freq = (np.float32(1.0) / np.float32(10000.0) ** (half / np.float32(DH))).astype(np.float32)
    t = np.arange(T, dtype=np.float32)
    freqs = t[:, None] * inv_freq[None, :]
    freqs = np.concatenate([freqs, freqs], -1)
    base = ((half + np.float32(0.4 * DH)) / np.float32(1.4 * DH)).astype(np.float32)
    power = ((t - T // 2) / np.float32(WIN // 2)).astype(np.float32)
    scale = (base[None, :] ** power[:, None]).astype(np.float32)
    scale = np.concatenate([scale, scale], -1)
    sign = np.where(np.arange(DH) < DH // 2, -1, 1).astype(np.float32)
    cos, sin = np.cos(freqs), np.sin(freqs) * sign
    inv = (np.float32(1.0) / scale).astype(np.float32)
    four = np.stack([cos * scale * np.float32(QK_SCALE), sin * scale * np.float32(QK_SCALE), cos * inv, sin * inv])
    return np.ascontiguousarray(four.reshape(4, NT, P, DH).transpose(2, 0, 1, 3)).astype(np.float32)


def band_mask():
    i = (np.arange(P) % WIN)[:, None, None]
    j = np.arange(KEYS)[None, None, :]
    seen = np.broadcast_to((j >= i) & (j <= i + WIN), (P, NT, KEYS)).copy()
    seen[:WIN, 0, :WIN] = False
    return np.where(seen, 0.0, NEG).astype(np.float32)


def rsqrt_steps(dve, done, at, v, y, t, least, add):
    k = 0

    def step(instruction):
        nonlocal k
        k += 1
        instruction.then_inc(done, 1)
        dve.wait_ge(done, at + k)

    step(dve.tensor_scalar(v, v, add, least, ALU.add, ALU.max))
    step(dve.tensor_scalar(y.bitcast(I32), v.bitcast(I32), 1, None, ALU.logical_shift_right))
    step(dve.tensor_scalar(y.bitcast(I32), y.bitcast(I32), -1.0, RSQRT_SEED, ALU.mult, ALU.add))
    for _ in range(3):
        step(dve.tensor_tensor(t, y, y, ALU.mult))
        step(dve.scalar_tensor_tensor(out=t, in0=t, scalar=-0.5, in1=v, op0=ALU.mult, op1=ALU.mult))
        step(dve.scalar_tensor_tensor(out=y, in0=t, scalar=1.5, in1=y, op0=ALU.add, op1=ALU.mult))
    assert k == NEWTON


def is_zero(t):
    return isinstance(t, int) and t == 0


def settle(eng, c):
    eng.sem_inc(c.settled, 1)


def start_at_one(nc, sems):
    with nc.Block() as block:
        @block.sync
        def _(sp):
            for sem in sems:
                sp.sem_inc(sem, 1)


class Chip:
    pass


def scope(nc, ctx):
    def sb(name, shape, dt=F32):
        return ctx.enter_context(nc.sbuf_tensor(name, shape, dt))

    def ps(name, shape, dt=F32):
        return ctx.enter_context(nc.psum_tensor(name, shape, dt))

    held = []

    def sem(name):
        if not held:
            ctx.callback(give_back)
        held.append(nc.alloc_semaphore(name=name))
        return held[-1]

    def give_back():
        nc.clear_and_free_semaphores(held)
        nc.all_engine_barrier()

    return sb, ps, sem


def load_phase(nc, c, d):
    with ExitStack() as ctx:
        sb, ps, sem = scope(nc, ctx)
        xt = sb("xt", [P, B * NT, P])
        rows = sb("rows", [P, P])
        maskf = sb("maskf", [P, NT, KEYS])
        turned = [ps(f"ld_turned{i}", [P, 4, P]) for i in range(4)]
        turned_rows = ps("ld_turned_rows", [P, P])
        x_in, cleared, rows_in, mask_in, rest_in = sem("x_in"), sem("cleared"), sem("rows_in"), sem("mask_in"), sem("rest_in")
        ident_done, x_turned, rows_turned, copied, swapped = (
            sem("ident_done"), sem("x_turned"), sem("rows_turned"), sem("copied"), sem("swapped"))
        single = ["L0_attn_bi", "L0_attn_bf", "L0_attn_bo", "L0_attn_bg", "L0_attn_beg", "L0_attn_gamma", "L0_attn_beta", "L1_attn_out_b"]
        c.col = {name: DEPTH * LV + i for i, name in enumerate(single)}

        with nc.Block() as block:
            @block.gpsimd
            def _(pool):
                pool.memset(c.ident[:, :], 0.0).then_inc(ident_done, 1)
                pool.memset(rows[:, :], 0.0).then_inc(cleared, 1)
                pool.wait_ge(ident_done, 1)
                pool.affine_select(out=c.ident[:, :], in_=c.ident[:, :], compare_op=ALU.not_equal, fill=1.0,
                                   base=0, pattern=[[-1, P]], channel_multiplier=1).then_inc(ident_done, 1)
                pool.wait_ge(ident_done, 2)
                settle(pool, c)
                pool.tensor_copy(c.identb[:, :], c.ident[:, :]).then_inc(copied, 1)
                pool.memset(c.xA[:, :, 0:PAD], 0.0).then_inc(cleared, 1)
                pool.memset(c.xB[:, :, 0:PAD], 0.0).then_inc(cleared, 1)
                pool.memset(c.xA[:, :, PAD + T:], 0.0).then_inc(cleared, 1)
                pool.memset(c.ones[:, :], 1.0).then_inc(cleared, 1)

            @block.sync
            def _(sp):
                for b in range(B):
                    sp.dma_start(xt[:, b * NT:(b + 1) * NT, :],
                                 d["L0_attn_x"][b].rearrange("(t p) f -> p t f", p=P)).then_inc(x_in, 16)
                sp.dma_start(maskf[:, :, :], d["mask"]).then_inc(mask_in, 16)
                sp.dma_start(c.rope[:, :, :, :], d["rope"]).then_inc(rest_in, 16)
                sp.dma_start(c.Wqkv[:, :], d["L0_ffn_Wqkv"][0]).then_inc(rest_in, 16)
                sp.dma_start(c.Wo[:, :, :], d["L0_ffn_Wo"][0].rearrange("(j p) n -> p j n", p=P)).then_inc(rest_in, 16)
                sp.wait_ge(rest_in, 16 * 5)

            @block.scalar
            def _(act):
                act.wait_ge(cleared, 1)
                with nc.allow_non_contiguous_dma(reason="short vectors"):
                    n = 0
                    layered = [("L0_ffn_ln_g", 0, 0, P), ("L0_ffn_ln_b", 1, 0, P), ("L0_ffn_b2", 2, 0, P)]
                    layered += [("L0_ffn_b1", 3 + i, s, w) for i, (s, w) in enumerate(FFC)]
                    layered += [("L0_ffn_b1", 6 + i, FF + s, w) for i, (s, w) in enumerate(FFC)]
                    for name, row, s, w in layered:
                        act.dma_start(rows[row:DEPTH * LV:LV, 0:w], d[name][:, s:s + w]).then_inc(rows_in, 16)
                        n += 1
                    for name in single:
                        act.dma_start(rows[c.col[name]:c.col[name] + 1, :],
                                      d[name].rearrange("(a f) -> a f", a=1)).then_inc(rows_in, 16)
                        n += 1
                    c.n_rows_in = n
                    act.dma_start(c.qks[:, 0, :], d["L0_ffn_q_scale"].rearrange("l f -> (l f)").partition_broadcast(P)).then_inc(rest_in, 16)
                    act.dma_start(c.qks[:, 1, :], d["L0_ffn_k_scale"].rearrange("l f -> (l f)").partition_broadcast(P)).then_inc(rest_in, 16)
                act.wait_ge(mask_in, 16)
                act.copy(c.mask[:, :, :], maskf[:, :, :]).then_inc(copied, 1)
                act.wait_ge(x_turned, 4)
                for g in range(4):
                    b, t = g // 2, (g % 2) * 4
                    act.copy(c.X[:, b, PAD + t * P:PAD + (t + 4) * P], turned[g][:, :, :].rearrange("f t p -> f (t p)")).then_inc(copied, 1)
                act.wait_ge(rows_turned, 1)
                act.copy(c.cols[:, :], turned_rows[:, :]).then_inc(copied, 1)

            @block.vector
            def _(dve):
                dve.wait_ge(rest_in, 16 * 5)
                for i in range(2):
                    halves = [c.qks[:, j, :].rearrange("p (l a d) -> p l a d", a=2, d=DH // 2) for j in (i, 2 + i)]
                    for a in range(2):
                        dve.tensor_copy(halves[1][:, :, a, :], halves[0][:, :, 1 - a, :]).then_inc(swapped, 1)

            @block.tensor
            def _(pe):
                pe.wait_ge(ident_done, 2)
                pe.wait_ge(x_in, 16 * B)
                for g in range(4):
                    for j in range(4):
                        last = pe.transpose(turned[g][:, j, :], xt[:, g * 4 + j, :], c.ident[:, :])
                    last.then_inc(x_turned, 1)
                pe.wait_ge(rows_in, 16 * (9 + len(single)))
                pe.transpose(turned_rows[:, :], rows[:, :], c.ident[:, :]).then_inc(rows_turned, 1)


def norm_phase(nc, c, name, src, dst, affine=None):
    NGR = B * NG
    with ExitStack() as ctx:
        sb, ps, sem = scope(nc, ctx)
        stats = sb(name + "stats", [P, NGR, 4, 6])
        mv = sb(name + "mv", [P, NGR, 4, 2])
        var = sb(name + "var", [P, NGR * 4])
        rstd = sb(name + "rstd", [P, NGR * 4])
        tmp = sb(name + "tmp", [P, NGR * 4])
        xn = sb(name + "xn", [P, NGR, 4, P])
        tok = [ps(f"{name}tok{g}", [P, 4, P]) for g in range(NGR)]
        back = [ps(f"{name}back{g}", [P, 4 * P]) for g in range(NGR)]
        tok_ready, stat, aggr, var_ready, newton = sem(name + "tok_ready"), sem(name + "stat"), sem(name + "aggr"), sem(name + "var_ready"), sem(name + "newton")
        xn_ready, back_ready, out_done = sem(name + "xn_ready"), sem(name + "back_ready"), sem(name + "out_done")
        place = [(g // NG, PAD + (g % NG) * GT) for g in range(NGR)]

        with nc.Block() as block:
            @block.tensor
            def _(pe):
                for g, (b, s) in enumerate(place):
                    for j in range(4):
                        last = pe.transpose(tok[g][:, j, :], src[:, b, s + j * P:s + (j + 1) * P], c.ident[:, :])
                    last.then_inc(tok_ready, 1)
                for g in range(NGR):
                    pe.wait_ge(xn_ready, 4 * (g + 1))
                    for j in range(4):
                        last = pe.transpose(back[g][:, j * P:(j + 1) * P], xn[:, g, j, :], c.ident[:, :])
                    last.then_inc(back_ready, 1)

            @block.vector
            def _(dve):
                for g in range(NGR):
                    dve.wait_ge(tok_ready, g + 1)
                    for j in range(4):
                        dve.bn_stats(stats[:, g, j, :], tok[g][:, j, :]).then_inc(stat, 1)
                for g in range(NGR):
                    dve.wait_ge(stat, 4 * (g + 1))
                    for j in range(4):
                        dve.bn_aggr(mv[:, g, j, :], stats[:, g, j, :]).then_inc(aggr, 1)
                dve.wait_ge(aggr, 4 * NGR)
                dve.tensor_copy(var[:, :], mv[:, :, :, 1].rearrange("p g j -> p (g j)")).then_inc(var_ready, 1)
                dve.wait_ge(var_ready, 1)
                rsqrt_steps(dve, newton, 0, var[:, :], rstd[:, :], tmp[:, :], 0.0, 1e-5)
                for g in range(NGR):
                    for j in range(4):
                        dve.tensor_scalar(xn[:, g, j, :], tok[g][:, j, :], mv[:, g, j, 0:1],
                                          rstd[:, g * 4 + j:g * 4 + j + 1], ALU.subtract, ALU.mult).then_inc(xn_ready, 1)

            @block.scalar
            def _(act):
                for g, (b, s) in enumerate(place):
                    act.wait_ge(back_ready, g + 1)
                    if affine:
                        gain, offset = (c.cols[:, c.col[x]:c.col[x] + 1] for x in affine)
                        act.activation(dst[:, b, s:s + GT], back[g][:, :], ACT.Identity, bias=offset, scale=gain).then_inc(out_done, 1)
                    else:
                        act.copy(dst[:, b, s:s + GT], back[g][:, :]).then_inc(out_done, 1)


def attention_phase(nc, c, layer, nm):
    s = c.sems[nm]
    base = layer * (B * NT)
    qk, vo, sc = c.qk_ps, c.vo_ps, c.sc_ps
    t1, t2, sq, pr = c.t1, c.t2, c.sq, c.probs

    def slots(emit):
        emit((0, 0), None)
        emit((1, 0), (0, 0))

        def steady(t):
            emit((0, t), (1, t - 1))
            emit((1, t), (0, t))
        return steady, lambda: emit(None, (1, NT - 1))

    def run(eng, stages):
        def emit(one, two):
            stages(None if one is None else (one[0], one[1], base + 2 * one[1] + one[0], not is_zero(one[1])),
                   None if two is None else (two[0], two[1], base + 2 * two[1] + two[0], not is_zero(two[1])))
        steady, last = slots(emit)
        with eng.Fori(1, NT) as t:
            steady(t)
        last()

    def qview(psum):
        return psum.rearrange("p (h d) -> p h d", d=DH)

    def swapped(psum):
        return psum.rearrange("p (h a d) -> p h a d", a=2, d=DH // 2)[:, :, ::-1, :]

    with nc.Block() as block:
        @block.gpsimd
        def _(pool):
            def stages(one, two):
                if one:
                    b, t, n, later = one
                    if later:
                        pool.wait_ge(s.v_done, 2 * (n - 1))
                    at = PAD - WIN + t * P
                    pool.tensor_copy(c.xs[b][0:64, :], c.xA[0:64, b, bass.ds(at, WIN + P)]).then_inc(s.xs_ready, 1)
                    pool.wait_ge(s.xs_ready, 2 * n + 1)
                    settle(pool, c)
                    pool.tensor_copy(c.xs[b][64:P, :], c.xA[64:P, b, bass.ds(at - 1, WIN + P)]).then_inc(s.xs_ready, 1)
                    pool.wait_ge(s.xs_ready, 2 * n + 2)
                    settle(pool, c)
                    if not later:
                        pool.memset(c.KT[b][:, :, 0:WIN], 0.0).then_inc(s.k_moved, 1)
                if one:
                    b, t, n, later = one
                    for i in range(2):
                        pool.wait_ge(s.t_ready, 4 * n + 2 * i + 2)
                        part = slice(i * INNER, (i + 1) * INNER)
                        pool.tensor_tensor(t1[:, part], t1[:, part], t2[:, part], ALU.add).then_inc(s.rot_sum, 1)
                    pool.wait_ge(s.newton, NEWTON * (n + 1))
                    for i in range(2):
                        pool.wait_ge(s.rot_sum, 2 * n + i + 1)
                        part = slice(i * INNER, (i + 1) * INNER)
                        pool.tensor_tensor(qview(t1[:, part]), qview(t1[:, part]),
                                           c.rnorm[:, i * HEADS:(i + 1) * HEADS].unsqueeze(2).to_broadcast([P, HEADS, DH]),
                                           ALU.mult).then_inc(s.rot_ready, 1)
            run(pool, stages)

        @block.tensor
        def _(pe):
            def stages(one, two):
                if two:
                    b, t, n, later = two
                    if later or b:
                        pe.wait_ge(s.x_done, n)
                    pe.wait_ge(s.kq_ready, 2 * n + 2)
                    for h in range(2):
                        pe.matmul(sc[:, h * 512:(h + 1) * 512], c.identb[:, :],
                                  c.mask[:, t, :].unsqueeze(1).to_broadcast([P, 8, KEYS]), start=True, stop=False,
                                  skip_group_check=True)
                    for w in range(NW):
                        for pair in range(PAIRS):
                            for par in range(2):
                                col = par * 512 + pair * KEYS
                                rows = slice(64 * par, 64 * par + 64)
                                last = pe.matmul(sc[WIN * w:WIN * w + WIN, col:col + KEYS],
                                                 c.QT[rows, pair, WIN * w:WIN * w + WIN],
                                                 c.KT[b][rows, pair, WIN * w:WIN * w + KEYS],
                                                 start=False, stop=True, skip_group_check=True)
                    last.then_inc(s.scored, 1)
                if one:
                    b, t, n, later = one
                    pe.wait_ge(s.xs_ready, 2 * n + 2)
                    if later or b:
                        pe.wait_ge(s.kq_ready, 2 * n)
                    for i in range(4):
                        last = pe.matmul(qk[:, i * 512:(i + 1) * 512], c.xs[b][:, WIN:WIN + P],
                                         c.Wqkv[:, i * 512:(i + 1) * 512], start=True, stop=True)
                        if i % 2:
                            last.then_inc(s.qk_done, 1)
                if two:
                    b, t, n, later = two
                    for i in range(2):
                        if i == 0 and (later or b):
                            pe.wait_ge(s.o_ready, n)
                        if i == 1:
                            pe.wait_ge(s.v_ready, 2 * n + 1)
                        for j in range(2):
                            w = 2 * i + j
                            for par in range(2):
                                last = pe.matmul(vo[64 * par:64 * par + 64, j * 512:(j + 1) * 512],
                                                 c.xs[b][:, WIN * w:WIN * w + KEYS],
                                                 c.Wqkv[:, 2 * INNER:3 * INNER].rearrange("p (k a d) -> p a k d", a=2, d=DH)[:, par],
                                                 start=True, stop=True)
                        last.then_inc(s.v_done, 1)
                    pe.wait_ge(s.exp_done, n + 1)
                    for k in range(PAIRS):
                        last = pe.transpose(sc[:, k * P:(k + 1) * P], pr[:, 2 * k:2 * k + 2, :].rearrange("p a j -> p (a j)"),
                                            c.ident[:, :])
                    last.then_inc(s.p_turned, 1)
                    pe.wait_ge(s.pt_ready, n + 1)
                    pe.wait_ge(s.v_ready, 2 * n + 2)
                    settle(pe, c)
                    for w in range(NW):
                        for k in range(PAIRS):
                            for par in range(2):
                                rows = slice(64 * par, 64 * par + 64)
                                last = pe.matmul(vo[WIN * w:WIN * w + WIN, par * 512 + k * DH:par * 512 + (k + 1) * DH],
                                                 c.PT[rows, k * P + WIN * w:k * P + WIN * w + WIN],
                                                 c.Vw[rows, w, k * DH:(k + 1) * DH], start=True, stop=True)
                    last.then_inc(s.pv_done, 1)
                if one:
                    b, t, n, later = one
                    for i in range(2):
                        pe.wait_ge(s.rot_ready, 2 * n + i + 1)
                        for k in range(PAIRS):
                            last = pe.transpose(qk[:, i * INNER + k * P:i * INNER + (k + 1) * P],
                                                t1[:, i * INNER + k * P:i * INNER + (k + 1) * P], c.ident[:, :])
                        last.then_inc(s.kq_turned, 1)
                if two:
                    b, t, n, later = two
                    pe.wait_ge(s.o_normed, n + 1)
                    for k in range(PAIRS):
                        last = pe.transpose(vo[:, k * P:(k + 1) * P], c.On[:, 2 * k:2 * k + 2, :].rearrange("p a d -> p (a d)"),
                                            c.ident[:, :])
                    last.then_inc(s.o_turned, 1)
                    pe.wait_ge(s.o_ready, n + 1)
                    for k in range(PAIRS):
                        last = pe.matmul(sc[:, 0:P], c.Wo[:, k, :], c.OT[:, k * P:(k + 1) * P],
                                         start=(k == 0), stop=(k == PAIRS - 1))
                    last.then_inc(s.wo_done, 1)
            run(pe, stages)

        @block.vector
        def _(dve):
            def stages(one, two):
                if two:
                    b, t, n, later = two
                    dve.wait_ge(s.scored, n + 1)
                    dve.tensor_reduce(c.mx[:, :], sc.rearrange("p (h j) -> p h j", j=KEYS), AX.X, ALU.max).then_inc(s.max_done, 1)
                    dve.wait_ge(s.max_done, n + 1)
                    if later or b:
                        dve.wait_ge(s.p_turned, n)
                    dve.tensor_tensor(pr[:, :, :].rearrange("p (k a) j -> p a k j", a=2),
                                      sc.rearrange("p (a k j) -> p a k j", a=2, j=KEYS),
                                      c.mx[:, :].rearrange("p (a k) -> p a k", a=2).unsqueeze(3).to_broadcast([P, 2, PAIRS, KEYS]),
                                      ALU.subtract).then_inc(s.centred, 1)
                if one:
                    b, t, n, later = one
                    for i in range(2):
                        dve.wait_ge(s.sq_done, 2 * n + i + 1)
                        if later or b:
                            dve.wait_ge(s.kq_turned, 2 * n)
                        part = slice(i * INNER, (i + 1) * INNER)
                        dve.tensor_tensor(qview(t1[:, part]), qview(qk[:, part]),
                                          c.rl[:, 2 * i, bass.ds(t * DH, DH)].unsqueeze(1).to_broadcast([P, HEADS, DH]),
                                          ALU.mult).then_inc(s.t_ready, 1)
                        table = c.rl[:, 2 * i + 1, bass.ds(t * DH, DH)].rearrange("p (a d) -> p a d", a=2)
                        dve.tensor_tensor(t2[:, part].rearrange("p (h a d) -> p h a d", a=2, d=DH // 2), swapped(qk[:, part]),
                                          table.unsqueeze(1).to_broadcast([P, HEADS, 2, DH // 2]),
                                          ALU.mult).then_inc(s.t_ready, 1)
                if two:
                    b, t, n, later = two
                    dve.wait_ge(s.exp_done, n + 1)
                    dve.tensor_reduce(c.rsum[:, :], pr[:, :, :], AX.X, ALU.add).then_inc(s.rsum_ready, 1)
                    dve.wait_ge(s.rsum_ready, 2 * n + 1)
                    dve.reciprocal(c.rsum[:, :], c.rsum[:, :]).then_inc(s.rsum_ready, 1)
                if one:
                    b, t, n, later = one
                    if later or b:
                        dve.wait_ge(s.rot_ready, 2 * n)
                    for i in range(2):
                        dve.wait_ge(s.sq_done, 2 * n + i + 1)
                        dve.tensor_reduce(c.ssq[:, i * HEADS:(i + 1) * HEADS], qview(sq[:, i * INNER:(i + 1) * INNER]),
                                          AX.X, ALU.add).then_inc(s.ssq_done, 1)
                    dve.wait_ge(s.ssq_done, 2 * n + 2)
                    rsqrt_steps(dve, s.newton, n * NEWTON, c.ssq[:, :], c.rnorm[:, :], c.ntmp[:, :], 1e-24, 0.0)
                if two:
                    b, t, n, later = two
                    dve.wait_ge(s.rsum_ready, 2 * n + 2)
                    dve.wait_ge(s.pv_done, n + 1)
                    dve.tensor_tensor(c.On[:, :, :].rearrange("p (k a) d -> p a k d", a=2),
                                      vo.rearrange("p (a k d) -> p a k d", a=2, d=DH),
                                      c.rsum[:, :].rearrange("p (k a) -> p a k", a=2).unsqueeze(3).to_broadcast([P, 2, PAIRS, DH]),
                                      ALU.mult).then_inc(s.o_normed, 1)
                    dve.wait_ge(s.wo_done, n + 1)
                    dve.tensor_tensor(c.xB[:, b, bass.ds(PAD + t * P, P)], sc[:, 0:P],
                                      c.xA[:, b, bass.ds(PAD + t * P, P)], ALU.add).then_inc(s.x_done, 1)
            for i in range(2):
                scale = c.qks[:, i, bass.ds(layer * DH, DH)]
                dve.tensor_tensor(c.rl[:, 2 * i, :].rearrange("p (t d) -> p t d", d=DH), c.rope[:, 2 * i, :, :],
                                  scale.unsqueeze(1).to_broadcast([P, NT, DH]), ALU.mult).then_inc(s.table, 1)
                other = c.qks[:, 2 + i, bass.ds(layer * DH, DH)]
                dve.tensor_tensor(c.rl[:, 2 * i + 1, :].rearrange("p (t d) -> p t d", d=DH), c.rope[:, 2 * i + 1, :, :],
                                  other.unsqueeze(1).to_broadcast([P, NT, DH]), ALU.mult).then_inc(s.table, 1)
            dve.wait_ge(s.table, 4 * (layer + 1))
            settle(dve, c)
            run(dve, stages)

        @block.scalar
        def _(act):
            def stages(one, two):
                if one:
                    b, t, n, later = one
                    for i in range(2):
                        act.wait_ge(s.qk_done, 2 * n + i + 1)
                        if later or b:
                            act.wait_ge(s.ssq_done, 2 * n)
                        act.activation(sq[:, i * INNER:(i + 1) * INNER], qk[:, i * INNER:(i + 1) * INNER],
                                       ACT.Square).then_inc(s.sq_done, 1)
                if two:
                    b, t, n, later = two
                    act.wait_ge(s.centred, n + 1)
                    act.activation(pr[:, :, :], pr[:, :, :], ACT.Exp).then_inc(s.exp_done, 1)
                    for i in range(2):
                        act.wait_ge(s.v_done, 2 * n + i + 1)
                        if later or b:
                            act.wait_ge(s.pv_done, n)
                        act.copy(c.Vw[:, 2 * i:2 * i + 2, :].rearrange("p w k -> p (w k)"), vo).then_inc(s.v_ready, 1)
                    act.wait_ge(s.p_turned, n + 1)
                    act.copy(c.PT[:, :], sc).then_inc(s.pt_ready, 1)
                    act.wait_ge(s.o_turned, n + 1)
                    act.copy(c.OT[:, :], vo).then_inc(s.o_ready, 1)
                if one:
                    b, t, n, later = one
                    if later:
                        act.wait_ge(s.scored, n - 1)
                        act.copy(c.KT[b][:, :, 0:WIN], c.KT[b][:, :, P:P + WIN]).then_inc(s.k_moved, 1)
                    for i in range(2):
                        act.wait_ge(s.kq_turned, 2 * n + i + 1)
                        if i == 0:
                            if later or b:
                                act.wait_ge(s.scored, n)
                            dst = c.QT[:, :, :]
                        else:
                            act.wait_ge(s.k_moved, n + 1)
                            dst = c.KT[b][:, :, WIN:WIN + P]
                        act.copy(dst, qk[:, i * INNER:(i + 1) * INNER].rearrange("p (k m) -> p k m", m=P)).then_inc(s.kq_ready, 1)
            act.activation(c.scrap[:, :], c.ones[:, 0:1], ACT.Exp).then_inc(s.table_load, 1)
            run(act, stages)

        @block.sync
        def _(sp):
            W1, W2 = c.d["L0_ffn_W1"], c.d["L0_ffn_W2"]
            sp.dma_start(c.W1[:, :], W1[bass.ds(layer, 1)].rearrange("l p n -> p (l n)")).then_inc(s.w_in, 16)
            sp.dma_start(c.W2[:, 0:2, :], W2[bass.ds(layer, 1), 0:256, :].rearrange("l (j p) n -> p (l j) n", p=P)).then_inc(s.w_in, 16)
            w = FFC[2][1]
            sp.dma_start(c.W2[0:w, 2, :], W2[bass.ds(layer, 1), 256:FF, :].rearrange("l p n -> p (l n)")).then_inc(s.w_in, 16)
            sp.wait_ge(s.w_in, 16 * 3 * (layer + 1))
            settle(sp, c)


class TransformerSemaphores:
    def __init__(self, sem, nm):
        self.xs_ready, self.qk_done, self.sq_done, self.ssq_done = (
            sem(nm + "_xs_ready"), sem(nm + "_qk_done"), sem(nm + "_sq_done"), sem(nm + "_ssq_done"))
        self.newton, self.t_ready, self.rot_sum, self.rot_ready = (
            sem(nm + "_newton"), sem(nm + "_t_ready"), sem(nm + "_rot_sum"), sem(nm + "_rot_ready"))
        self.kq_turned, self.kq_ready, self.k_moved, self.scored = (
            sem(nm + "_kq_turned"), sem(nm + "_kq_ready"), sem(nm + "_k_moved"), sem(nm + "_scored"))
        self.max_done, self.centred, self.exp_done, self.rsum_ready = (
            sem(nm + "_max_done"), sem(nm + "_centred"), sem(nm + "_exp_done"), sem(nm + "_rsum_ready"))
        self.o_normed, self.o_turned, self.p_turned, self.pt_ready = (
            sem(nm + "_o_normed"), sem(nm + "_o_turned"), sem(nm + "_p_turned"), sem(nm + "_pt_ready"))
        self.v_done, self.v_ready, self.pv_done, self.o_ready = (
            sem(nm + "_v_done"), sem(nm + "_v_ready"), sem(nm + "_pv_done"), sem(nm + "_o_ready"))
        self.wo_done, self.x_done, self.table, self.table_load = (
            sem(nm + "_wo_done"), sem(nm + "_x_done"), sem(nm + "_table"), sem(nm + "_table_load"))
        self.w_in = sem(nm + "_w_in")
        self.f_xs, self.f_tok, self.f_stat, self.f_aggr = (
            sem(nm + "_f_xs"), sem(nm + "_f_tok"), sem(nm + "_f_stat"), sem(nm + "_f_aggr"))
        self.f_var, self.f_newton, self.f_xn, self.f_turned = (
            sem(nm + "_f_var"), sem(nm + "_f_newton"), sem(nm + "_f_xn"), sem(nm + "_f_turned"))
        self.f_xnT, self.f_h, self.f_gelu, self.f_prod = (
            sem(nm + "_f_xnT"), sem(nm + "_f_h"), sem(nm + "_f_gelu"), sem(nm + "_f_prod"))
        self.f_out, self.f_x, self.f_cols, self.f_next = (
            sem(nm + "_f_out"), sem(nm + "_f_x"), sem(nm + "_f_cols"), sem(nm + "_f_next"))
        self.f_load = sem(nm + "_f_load")


def ffn_phase(nc, c, layer, nm):
    s = c.sems[nm]
    base = layer * (B * NG)
    tok, back, outp = c.tok_ps, c.back_ps, c.out_ps
    H = c.h_ps

    def groups(eng, body):
        with eng.Fori(0, NG) as g:
            for b in range(B):
                body(b, g, base + 2 * g + b)

    with nc.Block() as block:
        @block.gpsimd
        def _(pool):
            def body(b, g, n):
                pool.wait_ge(s.f_tok, n + 1)
                at = PAD + g * GT
                pool.tensor_copy(c.fxs[0:64, :], c.xB[0:64, b, bass.ds(at, GT)]).then_inc(s.f_xs, 1)
                pool.wait_ge(s.f_xs, 2 * n + 1)
                settle(pool, c)
                pool.tensor_copy(c.fxs[64:P, :], c.xB[64:P, b, bass.ds(at - 1, GT)]).then_inc(s.f_xs, 1)
                pool.wait_ge(s.f_xs, 2 * n + 2)
            groups(pool, body)

        @block.tensor
        def _(pe):
            def body(b, g, n):
                pe.wait_ge(s.f_xs, 2 * n + 2)
                pe.wait_ge(s.f_xn, 4 * n + 1)
                for j in range(4):
                    last = pe.transpose(tok[:, j, :], c.fxs[:, j * P:(j + 1) * P], c.ident[:, :])
                last.then_inc(s.f_tok, 1)
                pe.wait_ge(s.f_xn, 4 * n + 4 + 1)
                pe.wait_ge(s.f_xnT, n + 1)
                for j in range(4):
                    last = pe.transpose(back[:, j * P:(j + 1) * P], c.fxn[:, j, :], c.ident[:, :])
                last.then_inc(s.f_turned, 1)
                pe.wait_ge(s.f_xnT, n + 1 + 1)
                for i, (at, w) in enumerate(FFC):
                    if i < 2:
                        pe.wait_ge(s.f_prod, 3 * n + 1)
                    else:
                        pe.wait_ge(s.f_prod, 3 * n + 1 + 1)
                    gate, lin = H[i % 2]
                    pe.matmul(gate[0:w, :], c.W1[:, FF + at:FF + at + w], c.fxnT[:, :], start=True, stop=True).then_inc(s.f_h, 1)
                    pe.matmul(lin[0:w, :], c.W1[:, at:at + w], c.fxnT[:, :], start=True, stop=True).then_inc(s.f_h, 1)
                pe.wait_ge(s.f_x, n + 1)
                for i, (at, w) in enumerate(FFC):
                    pe.wait_ge(s.f_prod, 3 * n + i + 1 + 1)
                    last = pe.matmul(outp, c.W2[0:w, i, :], c.fh[0:w, i, :], start=(i == 0), stop=(i == 2))
                last.then_inc(s.f_out, 1)
            groups(pe, body)

        @block.vector
        def _(dve):
            dve.tensor_copy(c.lcols[:, :], c.cols[:, bass.ds(layer * LV, LV)]).then_inc(s.f_cols, 1)
            dve.wait_ge(s.f_cols, layer + 1)
            settle(dve, c)

            def body(b, g, n):
                dve.wait_ge(s.f_tok, n + 1 + 1)
                for j in range(4):
                    dve.bn_stats(c.fstat[:, j, :], tok[:, j, :]).then_inc(s.f_stat, 1)
                dve.wait_ge(s.f_stat, 4 * n + 4)
                settle(dve, c)
                for j in range(4):
                    dve.bn_aggr(c.fmv[:, j, :], c.fstat[:, j, :]).then_inc(s.f_aggr, 1)
                dve.wait_ge(s.f_aggr, 4 * n + 4)
                dve.tensor_copy(c.fvar[:, :], c.fmv[:, :, 1]).then_inc(s.f_var, 1)
                dve.wait_ge(s.f_var, n + 1)
                rsqrt_steps(dve, s.f_newton, n * NEWTON, c.fvar[:, :], c.frstd[:, :], c.ftmp[:, :], 0.0, 1e-5)
                dve.wait_ge(s.f_turned, n + 1)
                for j in range(4):
                    dve.tensor_scalar(c.fxn[:, j, :], tok[:, j, :], c.fmv[:, j, 0:1], c.frstd[:, j:j + 1],
                                      ALU.subtract, ALU.mult).then_inc(s.f_xn, 1)
                dve.wait_ge(s.f_out, n + 1)
                for i, (at, w) in enumerate(FFC):
                    dve.wait_ge(s.f_h, 6 * n + 2 * i + 2 + 1)
                    dve.wait_ge(s.f_gelu, 3 * n + i + 1)
                    dve.scalar_tensor_tensor(out=c.fh[0:w, i, :], in0=H[i % 2][1][0:w, :], scalar=c.lcols[0:w, 3 + i:4 + i],
                                             in1=c.fg[0:w, i, :], op0=ALU.add, op1=ALU.mult).then_inc(s.f_prod, 1)
                dve.wait_ge(s.f_out, n + 1 + 1)
                at = PAD + g * GT
                dve.scalar_tensor_tensor(out=c.xA[:, b, bass.ds(at, GT)], in0=outp, scalar=c.lcols[:, 2:3],
                                         in1=c.xB[:, b, bass.ds(at, GT)], op0=ALU.add, op1=ALU.add).then_inc(s.f_x, 1)
            groups(dve, body)

        @block.scalar
        def _(act):
            act.activation(c.scrap[:, :], c.ones[:, 0:1], ACT.Gelu).then_inc(s.f_load, 1)
            act.wait_ge(s.f_cols, layer + 1)

            def body(b, g, n):
                act.wait_ge(s.f_turned, n + 1 + 1)
                act.wait_ge(s.f_h, 6 * n + 1)
                act.activation(c.fxnT[:, :], back, ACT.Identity, bias=c.lcols[:, 1:2], scale=c.lcols[:, 0:1]).then_inc(s.f_xnT, 1)
                act.wait_ge(s.f_prod, 3 * n + 1)
                for i, (at, w) in enumerate(FFC):
                    act.wait_ge(s.f_h, 6 * n + 2 * i + 1 + 1)
                    act.activation(c.fg[0:w, i, :], H[i % 2][0][0:w, :], ACT.Gelu, bias=c.lcols[0:w, 6 + i:7 + i]).then_inc(s.f_gelu, 1)
            groups(act, body)

        @block.sync
        def _(sp):
            nxt = sp.snap((layer + 1) % (DEPTH))
            sp.dma_start(c.Wqkv[:, :], c.d["L0_ffn_Wqkv"][bass.ds(nxt, 1)].rearrange("l p n -> p (l n)")).then_inc(s.f_next, 16)
            sp.dma_start(c.Wo[:, :, :], c.d["L0_ffn_Wo"][bass.ds(nxt, 1)].rearrange("l (j p) n -> p (l j) n", p=P)).then_inc(s.f_next, 16)
            sp.wait_ge(s.f_next, 32 * (layer + 1))
            settle(sp, c)


def residual_phase(nc, c, name, scale):
    with ExitStack() as ctx:
        _, _, sem = scope(nc, ctx)
        done = sem(name)
        with nc.Block() as block:
            @block.vector
            def _(dve):
                for b in range(B):
                    dve.scalar_tensor_tensor(out=c.X[:, b, PAD:PAD + T], in0=c.xA[:, b, PAD:PAD + T], scalar=scale, in1=c.X[:, b, PAD:PAD + T],
                                             op0=ALU.mult, op1=ALU.add).then_inc(done, 1)


def transformer(nc, c, nm, dump=None):
    norm_phase(nc, c, nm + "n", c.X, c.xA)
    with ExitStack() as ctx:
        sb, ps, sem = scope(nc, ctx)
        c.rl = sb("rl" + nm, [P, 4, NT * DH])
        with ExitStack() as low:
            sb, ps, _ = scope(nc, low)
            c.xs = [sb(f"xs{b}" + nm, [P, WIN + P]) for b in range(B)]
            c.t1, c.t2, c.sq = (sb(x + nm, [P, 2 * INNER]) for x in ("t1", "t2", "sq"))
            c.ssq, c.rnorm, c.ntmp = (sb(x + nm, [P, 2 * HEADS]) for x in ("ssq", "rnorm", "ntmp"))
            c.mx, c.rsum = (sb(x + nm, [P, HEADS]) for x in ("mx", "rsum"))
            c.QT = sb("QT" + nm, [P, PAIRS, P])
            c.Vw = sb("Vw" + nm, [P, NW, PAIRS * DH])
            c.On = sb("On" + nm, [P, HEADS, DH])
            c.probs = sb("probs" + nm, [P, HEADS, KEYS])
            c.PT, c.OT = (sb(x + nm, [P, PAIRS * P]) for x in ("PT", "OT"))
            c.fxs, c.fxnT = (sb(x + nm, [P, GT]) for x in ("fxs", "fxnT"))
            c.fxn = sb("fxn" + nm, [P, 4, P])
            c.fg, c.fh = (sb(x + nm, [P, 3, GT]) for x in ("fg", "fh"))
            c.fstat, c.fmv = sb("fstat" + nm, [P, 4, 6]), sb("fmv" + nm, [P, 4, 2])
            c.fvar, c.frstd, c.ftmp = (sb(x + nm, [P, 4]) for x in ("fvar", "frstd", "ftmp"))
            c.lcols = sb("lcols" + nm, [P, LV])
            bank = ps("banks" + nm, [P, 8 * 512])
            c.qk_ps, c.vo_ps, c.sc_ps = bank[:, 0:2048], bank[:, 2048:3072], bank[:, 3072:4096]
            part = lambda i: bank[:, i * 512:(i + 1) * 512]
            c.tok_ps = part(0).rearrange("p (j f) -> p j f", f=P)
            c.back_ps, c.out_ps = part(1), part(2)
            c.h_ps = [(part(3), part(4)), (part(5), part(6))]
            c.sems[nm] = s = TransformerSemaphores(sem, nm)
            start_at_one(nc, [s.f_tok, s.f_xn, s.f_xnT, s.f_h, s.f_prod, s.f_out, s.f_x, s.f_turned])
            with nc.Fori(0, c.depth) as layer:
                attention_phase(nc, c, layer, nm)
                ffn_phase(nc, c, layer, nm)
    residual_phase(nc, c, nm + "res", 0.5)


GATES = ("i", "f", "o", "g")


def recurrence_phase(nc, c):
    with ExitStack() as ctx:
        sb, ps, sem = scope(nc, ctx)
        Wg = sb("Wgates", [P, 4, 2, P])
        bias = sb("gate_bias", [1, 4, P])
        Weg = sb("Weg", [P, P])
        hbuf = [sb(f"hbuf{i}", [P, B, CH]) for i in range(2)]
        tg, es, sg, ex = sb("tg", [P, B]), sb("es", [P, 3, B]), sb("sg", [P, 3, B]), sb("ex", [P, B])
        cn, fcn = sb("cn", [P, 2, B]), sb("fcn", [P, 2, B])
        ig, oc, rn = sb("ig", [P, B]), sb("oc", [P, B]), sb("rn", [P, B])
        g_bank = [ps(f"g_bank{i}", [P, 512]) for i in range(2)]
        s_bank = [ps(f"s_bank{i}", [P, 512]) for i in range(2)]
        e_bank = ps("e_bank", [P, 512])
        w_in, zeroed = sem("r_w_in"), sem("r_zeroed")
        projected, g_done, s_done, e_done = sem("r_projected"), sem("r_g_done"), sem("r_s_done"), sem("r_e_done")
        tg_ready, es_ready, ex_ready, h_ready = sem("r_tg_ready"), sem("r_es_ready"), sem("r_ex_ready"), sem("r_h_ready")
        sg_done, fcn_done, ig_done, c_done, n_done, oc_done, rn_done, y_done = (
            sem("r_" + x) for x in ("sg_done", "fcn_done", "ig_done", "c_done", "n_done", "oc_done", "rn_done", "y_done"))
        CHUNKS = T // CH
        start_at_one(nc, [h_ready, y_done])

        with nc.Block() as block:
            @block.sync
            def _(sp):
                for i, g in enumerate(GATES):
                    sp.dma_start(Wg[:, i, :, :], c.d[f"L0_attn_W{g}"].rearrange("(a p) n -> p a n", p=P)).then_inc(w_in, 16)
                    sp.dma_start(bias[:, i, :], c.d[f"L0_attn_b{g}"].rearrange("(a n) -> a n", a=1)).then_inc(w_in, 16)
                sp.dma_start(Weg[:, :], c.d["L0_attn_Weg"]).then_inc(w_in, 16)
                sp.wait_ge(w_in, 16 * 9)

            @block.gpsimd
            def _(pool):
                pool.memset(cn[:, :, :], 0.0).then_inc(zeroed, 1)
                pool.memset(hbuf[1][:, :, :], 0.0).then_inc(zeroed, 1)

        with nc.Block() as block:
            @block.tensor
            def _(pe):
                def project(j, at, which):
                    gate, part = which // 2, which % 2
                    if GATES[gate] == "g":
                        out = g_bank[j][:, 0:CH * B].rearrange("p (s b) -> p b s", b=B)
                        first, last = part == 0, False
                    else:
                        out = s_bank[j][:, 0:CH * 3 * B].rearrange("p (s g b) -> p g b s", g=3, b=B)[:, gate]
                        first, last = which == 0, False
                    if part == 0:
                        lhsT, rhs = bias[0:1, gate, :], c.ones[0:1, 0:B * CH].rearrange("p (b s) -> p b s", b=B)
                    else:
                        lhsT, rhs = Wg[:, gate, 0, :], c.xA[:, :, bass.ds(at, CH)]
                    return pe.matmul(out, lhsT, rhs, start=first, stop=last, skip_group_check=True)

                for which in range(8):
                    project(0, PAD, which)
                with pe.Fori(0, CHUNKS // 2) as it:
                    for j in range(2):
                        for s in range(CH):
                            n = it * (2 * CH) + j * CH + s
                            h = hbuf[j][:, :, s - 1] if s else hbuf[1 - j][:, :, CH - 1]
                            pe.wait_ge(h_ready, n + 1)
                            pe.matmul(g_bank[j][:, s * B:(s + 1) * B], Wg[:, 3, 1, :], h, start=False, stop=True,
                                      skip_group_check=True).then_inc(g_done, 1)
                            for gate in range(3):
                                at = (s * 3 + gate) * B
                                last = pe.matmul(s_bank[j][:, at:at + B], Wg[:, gate, 1, :], h, start=False, stop=True,
                                                 skip_group_check=True)
                            last.then_inc(s_done, 1)
                            pe.wait_ge(tg_ready, n + 1)
                            pe.matmul(e_bank[:, 0:B], Weg[:, :], tg[:, :], start=True, stop=True).then_inc(e_done, 1)
                            if s % 2 == 1:
                                project(1 - j, it * (2 * CH) + (PAD + (j + 1) * CH), s // 2)

            @block.scalar
            def _(act):
                act.activation(c.scrap[:, :], c.ones[:, 0:1], ACT.Exp).then_inc(projected, 1)
                with act.Fori(0, CHUNKS // 2) as it:
                    for j in range(2):
                        for s in range(CH):
                            n = it * (2 * CH) + j * CH + s
                            act.wait_ge(g_done, n + 1)
                            act.activation(tg[:, :], g_bank[j][:, s * B:(s + 1) * B], ACT.Tanh).then_inc(tg_ready, 1)
                            act.wait_ge(s_done, n + 1)
                            act.activation(es[:, :, :].rearrange("p g b -> p (g b)"), s_bank[j][:, s * 3 * B:(s + 1) * 3 * B],
                                           ACT.Exp, scale=-1.0).then_inc(es_ready, 1)
                            act.wait_ge(e_done, n + 1)
                            act.activation(ex[:, :], e_bank[:, 0:B], ACT.Exp,
                                           bias=c.cols[:, c.col["L0_attn_beg"]:c.col["L0_attn_beg"] + 1]).then_inc(ex_ready, 1)

            @block.vector
            def _(dve):
                with dve.Fori(0, CHUNKS // 2) as it:
                    for j in range(2):
                        for s in range(CH):
                            n = it * (2 * CH) + j * CH + s
                            if s == CH // 2:
                                dve.wait_ge(y_done, it * 2 + j + 1)
                            dve.wait_ge(es_ready, n + 1)
                            dve.tensor_scalar(sg[:, :, :], es[:, :, :], 1.0, None, ALU.add).then_inc(sg_done, 1)
                            dve.wait_ge(sg_done, 2 * n + 1)
                            dve.reciprocal(sg[:, :, :], sg[:, :, :]).then_inc(sg_done, 1)
                            dve.wait_ge(sg_done, 2 * n + 2)
                            dve.tensor_tensor(fcn[:, :, :], cn[:, :, :], sg[:, 1:2, :].to_broadcast([P, 2, B]), ALU.mult).then_inc(fcn_done, 1)
                            dve.tensor_tensor(ig[:, :], sg[:, 0, :], tg[:, :], ALU.mult).then_inc(ig_done, 1)
                            dve.wait_ge(ig_done, n + 1)
                            dve.tensor_tensor(cn[:, 0, :], ig[:, :], fcn[:, 0, :], ALU.add).then_inc(c_done, 1)
                            dve.wait_ge(ex_ready, n + 1)
                            for b in range(B):
                                dve.scalar_tensor_tensor(out=cn[:, 1, b:b + 1], in0=ex[:, b:b + 1], scalar=sg[:, 0, b:b + 1],
                                                         in1=fcn[:, 1, b:b + 1], op0=ALU.mult, op1=ALU.add).then_inc(n_done, 1)
                            dve.wait_ge(c_done, n + 1)
                            dve.tensor_tensor(oc[:, :], sg[:, 2, :], cn[:, 0, :], ALU.mult).then_inc(oc_done, 1)
                            dve.wait_ge(n_done, 2 * n + 2)
                            dve.reciprocal(rn[:, :], cn[:, 1, :]).then_inc(rn_done, 1)
                            dve.wait_ge(rn_done, n + 1)
                            dve.tensor_tensor(hbuf[j][:, :, s], oc[:, :], rn[:, :], ALU.mult).then_inc(h_ready, 1)

            @block.gpsimd
            def _(pool):
                with pool.Fori(0, CHUNKS // 2) as it:
                    for j in range(2):
                        pool.wait_ge(h_ready, it * (2 * CH) + (j + 1) * CH + 1)
                        at = it * (2 * CH) + (PAD + j * CH)
                        pool.tensor_tensor(c.xB[:, :, bass.ds(at, CH)], hbuf[j][:, :, :], c.xA[:, :, bass.ds(at, CH)],
                                           ALU.add).then_inc(y_done, 1)


def experts_phase(nc, c, nm):
    E, N16 = EXPERTS, B * NT
    EP = E + 8 - TOPK
    with ExitStack() as ctx:
        sb, ps, sem = scope(nc, ctx)
        wg1, wg2, bg1 = sb("wg1" + nm, [P, GH]), sb("wg2" + nm, [GH, 2 * E]), sb("bg1" + nm, [GH, 1])
        bg2, We, be = sb("bg2" + nm, [P, 2 * E]), sb("We" + nm, [P, E, P]), sb("be" + nm, [E, P])
        hT = sb("hT" + nm, [GH, B, T])
        lg, pb, gates = sb("lg" + nm, [P, N16, E]), sb("pb" + nm, [P, N16, EP]), sb("gates" + nm, [P, N16, EP])
        mx, sm = sb("emx" + nm, [P, N16]), sb("esm" + nm, [P, N16])
        top, drop = sb("top" + nm, [P, N16, 8]), sb("drop" + nm, [P, N16, 8])
        gT = sb("gT" + nm, [E, B, T])
        xt = [sb(f"ext{b}" + nm, [P, P]) for b in range(B)]
        y = [[sb(f"ey{b}{i}" + nm, [P, P]) for i in range(2)] for b in range(B)]
        with ExitStack() as low:
            _, ps, sem = scope(nc, low)
            h_ps = [ps(f"eh{i}" + nm, [P, 512]) for i in range(4)]
            l_ps = ps("el" + nm, [P, 512])
            w_in, small_in, h_done, gelu, logits = (sem(nm + x) for x in ("w_in", "small_in", "h_done", "gelu", "logits"))
            soft, exped, topped = (sem(nm + x) for x in ("soft", "exped", "topped"))
            gt_turned, gt_ready, filled, loaded = sem(nm + "gt_turned"), sem(nm + "gt_ready"), sem(nm + "filled"), sem(nm + "loaded")
            with nc.Block() as block:
                @block.sync
                def _(sp):
                    with nc.allow_non_contiguous_dma(reason="a short vector to a column"):
                        sp.dma_start(bg1[:, :], c.d["L1_ffn_bg1"].rearrange("(p a) -> p a", a=1)).then_inc(small_in, 16)
                    sp.dma_start(wg1[:, :], c.d["L1_ffn_wg1"]).then_inc(small_in, 16)
                    sp.dma_start(wg2[:, :], c.d["L1_ffn_wg2"]).then_inc(small_in, 16)
                    sp.dma_start(bg2[:, :], c.d["L1_ffn_bg2"].partition_broadcast(P)).then_inc(small_in, 16)
                    sp.dma_start(be[:, :], c.d["L1_ffn_be"]).then_inc(small_in, 16)
                    sp.dma_start(We[:, :, :], c.d["L1_ffn_We"].rearrange("e p n -> p e n")).then_inc(w_in, 16)
                    sp.wait_ge(w_in, 16)
                    sp.wait_ge(small_in, 16 * 5)

                @block.gpsimd
                def _(pool):
                    pool.memset(pb[:, :, E:EP], -1.0).then_inc(filled, 1)
                    pool.memset(drop[:, :, TOPK:8], -1.0).then_inc(filled, 1)

                @block.tensor
                def _(pe):
                    pe.wait_ge(small_in, 16 * 5)
                    for g in range(4):
                        pe.matmul(h_ps[g][0:GH, :], wg1[:, :], c.xA[:, g // 2, PAD + (g % 2) * GT:PAD + (g % 2 + 1) * GT],
                                  start=True, stop=True).then_inc(h_done, 1)
                    for n in range(N16):
                        if n % 4 == 0:
                            pe.wait_ge(gelu, n // 4 + 1)
                        last = pe.matmul(l_ps[:, n * E:(n + 1) * E], hT[:, n // NT, (n % NT) * P:(n % NT + 1) * P], wg2[:, 0:E],
                                         start=True, stop=True)
                    last.then_inc(logits, 1)
                    for g in range(4):
                        pe.wait_ge(topped, N16 + 1)
                        for j in range(4):
                            last = pe.transpose(h_ps[g][0:E, j * P:(j + 1) * P], gates[:, 4 * g + j, 0:E], c.ident[:, :])
                        last.then_inc(gt_turned, 1)

                @block.scalar
                def _(act):
                    for g in range(4):
                        act.wait_ge(h_done, g + 1)
                        act.activation(hT[:, g // 2, (g % 2) * GT:(g % 2 + 1) * GT], h_ps[g][0:GH, :], ACT.Gelu, bias=bg1[:, :]).then_inc(gelu, 1)
                    act.wait_ge(soft, 3)
                    act.activation(pb[:, :, 0:E], lg[:, :, :], ACT.Exp).then_inc(exped, 1)
                    for g in range(4):
                        act.wait_ge(gt_turned, g + 1)
                        act.copy(gT[:, g // 2, (g % 2) * GT:(g % 2 + 1) * GT], h_ps[g][0:E, :]).then_inc(gt_ready, 1)

                @block.vector
                def _(dve):
                    k = 0

                    def step(instruction):
                        nonlocal k
                        k += 1
                        instruction.then_inc(soft, 1)
                        dve.wait_ge(soft, k)

                    def wide(a, w=E):
                        return a.unsqueeze(2).to_broadcast([P, N16, w])

                    dve.wait_ge(logits, 1)
                    dve.wait_ge(filled, 2)
                    step(dve.tensor_tensor(lg[:, :, :], l_ps[:, 0:N16 * E].rearrange("p (n e) -> p n e", e=E),
                                           bg2[:, 0:E].unsqueeze(1).to_broadcast([P, N16, E]), ALU.add))
                    step(dve.tensor_reduce(mx[:, :], lg[:, :, :], AX.X, ALU.max))
                    step(dve.tensor_tensor(lg[:, :, :], lg[:, :, :], wide(mx[:, :]), ALU.subtract))
                    dve.wait_ge(exped, 1)
                    step(dve.tensor_reduce(sm[:, :], pb[:, :, 0:E], AX.X, ALU.add))
                    step(dve.reciprocal(sm[:, :], sm[:, :]))
                    step(dve.tensor_tensor(pb[:, :, 0:E], pb[:, :, 0:E], wide(sm[:, :]), ALU.mult))
                    for n in range(N16):
                        last = dve.max(top[:, n, :], pb[:, n, 0:E])
                    step(last)
                    step(dve.tensor_copy(drop[:, :, 0:TOPK], top[:, :, 0:TOPK]))
                    for n in range(N16):
                        dve.match_replace(out=gates[:, n, :], in_to_replace=drop[:, n, :], in_values=pb[:, n, :],
                                          imm_value=0.0).then_inc(topped, 1)
                    dve.wait_ge(topped, N16)
                    dve.tensor_tensor(gates[:, :, 0:E], pb[:, :, 0:E], gates[:, :, 0:E], ALU.subtract).then_inc(topped, 1)

        with ExitStack() as low:
            _, ps, sem = scope(nc, low)
            z_ps, o_ps = ps("ez" + nm, [P, E * P]), ps("eo" + nm, [P, 512])
            x_taken, z_done, y_done, turned, added = (sem(nm + x) for x in ("x_taken", "z_done", "y_done", "turned", "added"))
            start_at_one(nc, [added, y_done])
            with nc.Block() as block:
                def tiles(eng, body):
                    with eng.Fori(0, NT) as t:
                        for b in range(B):
                            body(b, t, t * B + b)

                @block.gpsimd
                def _(pool):
                    def body(b, t, n):
                        pool.wait_ge(added, n + 1)
                        settle(pool, c)
                        pool.tensor_copy(xt[b][:, :], c.xA[:, b, bass.ds(PAD + t * P, P)]).then_inc(x_taken, 1)
                    tiles(pool, body)

                @block.tensor
                def _(pe):
                    def body(b, t, n):
                        pe.wait_ge(x_taken, n + 1)
                        for i in range(5):
                            pe.wait_ge(y_done, n * E + 0 + 1)
                            pe.matmul(z_ps[:, i * 512:(i + 1) * 512], xt[b][:, :],
                                      We[:, 4 * i:4 * i + 4, :].rearrange("p e n -> p (e n)"), start=True, stop=True).then_inc(z_done, 1)
                        pe.wait_ge(y_done, (n + 1) * E + 1)
                        for i in range(2):
                            pe.matmul(o_ps[:, 0:P], y[b][i][:, :], c.ident[:, :], start=(i == 0), stop=False)
                        pe.matmul(o_ps[:, 0:P], be[:, :], gT[:, b, bass.ds(t * P, P)], start=False, stop=True).then_inc(turned, 1)
                    tiles(pe, body)

                @block.vector
                def _(dve):
                    def body(b, t, n):
                        for e in range(E):
                            if e % 4 == 0:
                                dve.wait_ge(z_done, 5 * n + e // 4 + 1)
                            gate = c.gates_now[:, e:e + 1]
                            z = z_ps[:, e * P:(e + 1) * P]
                            acc = y[b][e % 2][:, :]
                            if e == 0:
                                dve.tensor_copy(c.gates_now[:, :], gates[:, bass.ds(b * NT + t, 1), 0:E].rearrange("p n e -> p (n e)")).then_inc(c.gates_sem, 1)
                                dve.wait_ge(c.gates_sem, n + 1)
                            if e < 2:
                                dve.tensor_scalar(acc, z, gate, None, ALU.mult).then_inc(y_done, 1)
                            else:
                                dve.wait_ge(y_done, n * E + e - 1 + 1)
                                dve.scalar_tensor_tensor(out=acc, in0=z, scalar=gate, in1=acc, op0=ALU.mult, op1=ALU.add).then_inc(y_done, 1)
                        dve.wait_ge(turned, n + 1)
                        at = PAD + t * P
                        dve.scalar_tensor_tensor(out=c.X[:, b, bass.ds(at, P)], in0=o_ps[:, 0:P], scalar=0.5,
                                                 in1=c.X[:, b, bass.ds(at, P)], op0=ALU.mult, op1=ALU.add).then_inc(added, 1)
                    c.gates_now = ctx.enter_context(nc.sbuf_tensor("gates_now" + nm, [P, E], F32))
                    c.gates_sem = sem(nm + "gates_taken")
                    tiles(dve, body)


def full_attention_phase(nc, c):
    BAND = P // 4
    with ExitStack() as ctx:
        sb, ps, sem = scope(nc, ctx)
        w, ow, owT = sb("w_qkv", [P, 3 * P]), sb("ow", [P, P]), sb("owT", [P, P])
        xh, wh = sb("xh", [P, B, T], F16), sb("wh", [P, 3 * P], F16)
        qT, kT = sb("qT", [P, B, T]), sb("kT", [P, B, T])
        V = sb("V", [P, B * NT, P])
        qs = [sb(f"qs{b}", [P, P]) for b in range(B)]
        pr = [sb(f"apr{b}", [P, T]) for b in range(B)]
        pT = [sb(f"apT{b}", [P, T]) for b in range(B)]
        yT = [sb(f"ayT{b}", [P, P]) for b in range(B)]
        mx, sm = [sb(f"amx{b}", [P, 1]) for b in range(B)], [sb(f"asm{b}", [P, 1]) for b in range(B)]
        bank = ps("a_banks", [P, 8 * 512])
        part = lambda i, n=1: bank[:, i * 512:(i + n) * 512]
        w_in, rounded, made, evacuated, turned_w = sem("fa_w_in"), sem("fa_rounded"), sem("fa_made"), sem("fa_evacuated"), sem("fa_turned_w")
        with nc.Block() as block:
            @block.sync
            def _(sp):
                sp.dma_start(w[:, :], c.d["L1_attn_weight_qkv"]).then_inc(w_in, 16)
                sp.dma_start(ow[:, :], c.d["L1_attn_out_w"]).then_inc(w_in, 16)

            @block.vector
            def _(dve):
                xa = c.xA[:, :, PAD:PAD + T]
                dve.tensor_copy(xh[:, :, :], xa).then_inc(rounded, 1)
                dve.wait_ge(w_in, 32)
                dve.tensor_copy(wh[:, :], w[:, :]).then_inc(rounded, 1)
                dve.wait_ge(rounded, 2)
                for lo in (0, P - BAND):
                    rows = slice(lo, lo + BAND)
                    dve.tensor_copy(c.xA[rows, :, PAD:PAD + T], xh[rows, :, :]).then_inc(rounded, 1)
                    dve.tensor_copy(w[rows, :], wh[rows, :]).then_inc(rounded, 1)

            @block.tensor
            def _(pe):
                pe.wait_ge(rounded, 6)
                for what in range(2):
                    for g in range(4):
                        pe.matmul(part(4 * what + g), w[:, what * P:(what + 1) * P],
                                  c.xA[:, g // 2, PAD + (g % 2) * GT:PAD + (g % 2 + 1) * GT], start=True, stop=True).then_inc(made, 1)
                for n in range(B * NT):
                    if n % 4 == 0:
                        pe.wait_ge(evacuated, n // 4 + 1)
                    at = PAD + (n % NT) * P
                    last = pe.matmul(part(n // 4)[:, (n % 4) * P:(n % 4 + 1) * P], c.xA[:, n // NT, at:at + P], w[:, 2 * P:3 * P],
                                     start=True, stop=True)
                    if n % 4 == 3:
                        last.then_inc(made, 1)
                pe.wait_ge(evacuated, 8)
                pe.transpose(part(4)[:, 0:P], ow[:, :], c.ident[:, :]).then_inc(turned_w, 1)

            @block.scalar
            def _(act):
                for what in range(2):
                    for g in range(4):
                        act.wait_ge(made, 4 * what + g + 1)
                        act.activation((qT, kT)[what][:, g // 2, (g % 2) * GT:(g % 2 + 1) * GT], part(4 * what + g), ACT.Copy,
                                       scale=(float(P) ** -0.5, 1.0)[what]).then_inc(evacuated, 1)
                for g in range(4):
                    act.wait_ge(made, 8 + g + 1)
                    act.copy(V[:, 4 * g:4 * g + 4, :].rearrange("p n d -> p (n d)"), part(g)).then_inc(evacuated, 1)
                act.wait_ge(turned_w, 1)
                act.copy(owT[:, :], part(4)[:, 0:P]).then_inc(evacuated, 1)

        q_taken, scored, maxed, negated, exped = sem("fa_q_taken"), sem("fa_scored"), sem("fa_maxed"), sem("fa_negated"), sem("fa_exped")
        inverted, normed, p_turned, pt_ready = sem("fa_inverted"), sem("fa_normed"), sem("fa_p_turned"), sem("fa_pt_ready")
        y_done, y_ready, o_done, added = sem("fa_y_done"), sem("fa_y_ready"), sem("fa_o_done"), sem("fa_added")
        start_at_one(nc, [scored, exped, pt_ready, y_ready, added, p_turned, y_done])
        s_ps, t_ps, y_ps, o_ps = [part(0, 2), part(2, 2)], part(4, 2), part(6), part(7)
        with nc.Block() as block:
            def tiles(eng, body):
                with eng.Fori(0, NT) as t:
                    for b in range(B):
                        body(b, t, t * B + b)

            @block.gpsimd
            def _(pool):
                with pool.Fori(0, NT) as t:
                    for b in range(B):
                        n = t * B + b
                        pool.wait_ge(scored, t * B + 1)
                        settle(pool, c)
                        pool.tensor_copy(qs[b][:, :], qT[:, b, bass.ds(t * P, P)]).then_inc(q_taken, 1)

            @block.tensor
            def _(pe):
                def score(b, t, n):
                    pe.wait_ge(q_taken, n + 1)
                    pe.wait_ge(exped, t * B + 1)
                    for i in range(2):
                        last = pe.matmul(s_ps[b][:, i * 512:(i + 1) * 512], qs[b][:, :], kT[:, b, i * 512:(i + 1) * 512],
                                         start=True, stop=True)
                    last.then_inc(scored, 1)

                def rest(b, t, n):
                    pe.wait_ge(normed, n + 1)
                    pe.wait_ge(pt_ready, n + 1)
                    for k in range(NT):
                        last = pe.transpose(t_ps[:, k * P:(k + 1) * P], pr[b][:, k * P:(k + 1) * P], c.ident[:, :])
                    last.then_inc(p_turned, 1)
                    pe.wait_ge(pt_ready, n + 1 + 1)
                    pe.wait_ge(y_ready, n + 1)
                    for k in range(NT):
                        last = pe.matmul(y_ps[:, 0:P], V[:, b * NT + k, :], pT[b][:, k * P:(k + 1) * P], start=(k == 0), stop=(k == NT - 1))
                    last.then_inc(y_done, 1)
                    pe.wait_ge(y_ready, n + 1 + 1)
                    pe.wait_ge(added, n + 1)
                    pe.matmul(o_ps[:, 0:P], owT[:, :], yT[b][:, :], start=True, stop=True).then_inc(o_done, 1)

                with pe.Fori(0, NT) as t:
                    for b in range(B):
                        score(b, t, t * B + b)
                    for b in range(B):
                        rest(b, t, t * B + b)

            @block.vector
            def _(dve):
                with dve.Fori(0, NT) as t:
                    for b in range(B):
                        n = t * B + b
                        dve.wait_ge(scored, n + 1 + 1)
                        dve.tensor_reduce(mx[b][:, :], s_ps[b], AX.X, ALU.max).then_inc(maxed, 1)
                        dve.wait_ge(maxed, n + 1)
                        dve.tensor_scalar(mx[b][:, :], mx[b][:, :], -1.0, None, ALU.mult).then_inc(negated, 1)
                    for b in range(B):
                        n = t * B + b
                        dve.wait_ge(exped, n + 1 + 1)
                        dve.reciprocal(sm[b][:, :], sm[b][:, :]).then_inc(inverted, 1)
                        dve.wait_ge(inverted, n + 1)
                        dve.tensor_scalar(pr[b][:, :], pr[b][:, :], sm[b][:, 0:1], None, ALU.mult).then_inc(normed, 1)
                    for b in range(B):
                        n = t * B + b
                        dve.wait_ge(o_done, n + 1)
                        at = PAD + t * P
                        bias = c.cols[:, c.col["L1_attn_out_b"]:c.col["L1_attn_out_b"] + 1]
                        dve.scalar_tensor_tensor(out=c.X[:, b, bass.ds(at, P)], in0=o_ps[:, 0:P], scalar=bias,
                                                 in1=c.X[:, b, bass.ds(at, P)], op0=ALU.add, op1=ALU.add).then_inc(added, 1)

            @block.scalar
            def _(act):
                act.activation(c.scrap[:, :], c.ones[:, 0:1], ACT.Exp).then_inc(turned_w, 1)
                with act.Fori(0, NT) as t:
                    for b in range(B):
                        n = t * B + b
                        act.wait_ge(negated, n + 1)
                        act.wait_ge(p_turned, t * B + 1)
                        act.activation(pr[b][:, :], s_ps[b], ACT.Exp, bias=mx[b][:, 0:1], accum_out=sm[b][:, 0:1]).then_inc(exped, 1)
                    for b in range(B):
                        n = t * B + b
                        act.wait_ge(p_turned, n + 1 + 1)
                        act.wait_ge(y_done, t * B + 1)
                        act.copy(pT[b][:, :], t_ps).then_inc(pt_ready, 1)
                        act.wait_ge(y_done, n + 1 + 1)
                        act.copy(yT[b][:, :], y_ps[:, 0:P]).then_inc(y_ready, 1)


def output_phase(nc, c, src, out):
    with ExitStack() as ctx:
        sb, ps, sem = scope(nc, ctx)
        turned = [ps(f"o_turned{i}", [P, 4, P]) for i in range(4)]
        ot = sb("ot", [P, B * NT, P])
        o_turned, o_copied, stored = sem("o_turned"), sem("o_copied"), sem("stored")
        with nc.Block() as block:
            @block.tensor
            def _(pe):
                for g in range(4):
                    for j in range(4):
                        b, t = g // 2, (g % 2) * 4 + j
                        last = pe.transpose(turned[g][:, j, :], src[:, b, PAD + t * P:PAD + (t + 1) * P], c.ident[:, :])
                    last.then_inc(o_turned, 1)

            @block.vector
            def _(dve):
                for g in range(4):
                    dve.wait_ge(o_turned, g + 1)
                    dve.tensor_copy(ot[:, 4 * g:4 * g + 4, :], turned[g][:, :, :]).then_inc(o_copied, 1)

            @block.sync
            def _(sp):
                for g in range(4):
                    b, t = g // 2, (g % 2) * 4
                    sp.wait_ge(o_copied, g + 1)
                    sp.dma_start(out[b, t * P:(t + 4) * P, :].rearrange("(t p) f -> p t f", p=P),
                                 ot[:, 4 * g:4 * g + 4, :]).then_inc(stored, 16)
                sp.wait_ge(stored, 16 * 4)


def program(nc, names, *aps):
    d = dict(zip(names, aps))
    out = aps[-1]
    with ExitStack() as ctx:
        sb, ps, sem = scope(nc, ctx)
        c = Chip()
        c.d, c.sems = d, {}
        c.settled = sem("settled")
        stage = 5
        c.depth = DEPTH
        c.X, c.xA, c.xB = (sb(x, [P, B, PAD + T + CH]) for x in ("X", "xA", "xB"))
        c.ident, c.identb = sb("ident", [P, P]), sb("identb", [P, P], BF16)
        c.ones, c.scrap = sb("ones", [P, P]), sb("scrap", [P, 1])
        c.cols = sb("cols", [P, P])
        with ExitStack() as ctx2:
            sb, ps, sem = scope(nc, ctx2)
            c.mask = sb("mask", [P, NT, KEYS], BF16)
            c.rope = sb("rope", [P, 4, NT, DH])
            c.qks = sb("qks", [P, 4, DEPTH * DH])
            c.Wqkv, c.Wo = sb("Wqkv", [P, 3 * INNER]), sb("Wo", [P, PAIRS, P])
            c.W1, c.W2 = sb("W1", [P, 2 * FF]), sb("W2", [P, 3, P])
            c.KT = [sb(f"KT{b}", [P, PAIRS, WIN + P]) for b in range(B)]
            load_phase(nc, c, d)
            transformer(nc, c, "a")
            if stage >= 1:
                norm_phase(nc, c, "rn", c.X, c.xA)
                recurrence_phase(nc, c)
                norm_phase(nc, c, "ry", c.xB, c.xA, affine=("L0_attn_gamma", "L0_attn_beta"))
                residual_phase(nc, c, "rres", 1.0)
            if stage >= 2:
                transformer(nc, c, "b")
        if stage >= 3:
            norm_phase(nc, c, "norm_e", c.X, c.xA)
            experts_phase(nc, c, "moe1")
        if stage >= 4:
            norm_phase(nc, c, "norm_f", c.X, c.xA)
            full_attention_phase(nc, c)
        if stage >= 5:
            norm_phase(nc, c, "norm_h", c.X, c.xA)
            experts_phase(nc, c, "moe2")
        output_phase(nc, c, c.X, out)


_INS = ['L0_attn_x', 'L0_attn_Wi', 'L0_attn_bi', 'L0_attn_Wf', 'L0_attn_bf', 'L0_attn_Wg', 'L0_attn_bg', 'L0_attn_Wo',
        'L0_attn_bo', 'L0_attn_Weg', 'L0_attn_beg', 'L0_attn_gamma', 'L0_attn_beta', 'L0_ffn_Wqkv', 'L0_ffn_q_scale',
        'L0_ffn_k_scale', 'L0_ffn_Wo', 'L0_ffn_ln_g', 'L0_ffn_ln_b', 'L0_ffn_W1', 'L0_ffn_b1', 'L0_ffn_W2', 'L0_ffn_b2',
        'L1_attn_weight_qkv', 'L1_attn_out_w', 'L1_attn_out_b', 'L1_ffn_wg1', 'L1_ffn_bg1', 'L1_ffn_wg2', 'L1_ffn_bg2',
        'L1_ffn_We', 'L1_ffn_be']


def kernel(**inputs):
    import concourse.bacc as _bacc
    from concourse.bass_utils import run_bass_kernel_spmd as _run

    nc = _bacc.Bacc("TRN2", target_bir_lowering=False, num_devices=1)
    arrays = {name: np.ascontiguousarray(inputs[name]) for name in _INS}
    arrays["rope"] = rope_tables()
    arrays["mask"] = band_mask()
    args = [nc.dram_tensor(f"in_{k}", a.shape, mybir.dt.from_np(a.dtype), kind="ExternalInput").ap() for k, a in arrays.items()]
    args.append(nc.dram_tensor("out", (B, T, P), F32, kind="ExternalOutput").ap())
    program(nc, list(arrays), *args)
    r = _run(nc, [{f"in_{k}": a for k, a in arrays.items()}], core_ids=[0])
    return r.results[0]["out"]
```

```python
from contextlib import ExitStack

import numpy as np

import concourse.bass as bass
from concourse import mybir

F32 = mybir.dt.float32
F16 = mybir.dt.float16
BF16 = mybir.dt.bfloat16
I32 = mybir.dt.int32
ALU = mybir.AluOpType
ACT = mybir.ActivationFunctionType
AX = mybir.AxisListType

P = 128
B, T = 2, 1024
NT = T // P
DEPTH, HEADS, DH, WIN = 6, 16, 64, 32
PAIRS = HEADS // 2
HALF = PAIRS // 2
NW = P // WIN
KEYS = 2 * WIN
INNER = HEADS * DH
FF = int(P * 4 * 2 / 3)
FFC = [(0, 128), (128, 128), (256, FF - 256)]
PAD = WIN + 1
GT = 512
NG = T // GT
QK_SCALE = 8.0
RSQRT_SEED = 1597463007.0
NEWTON = 12
NEG = -1e30
LV = 9
CH = 16

EXPERTS, TOPK, GH = 20, 2, 32


def rope_tables():
    half = np.arange(0, DH, 2, dtype=np.float32)
    inv_freq = (np.float32(1.0) / np.float32(10000.0) ** (half / np.float32(DH))).astype(np.float32)
    t = np.arange(T, dtype=np.float32)
    freqs = t[:, None] * inv_freq[None, :]
    freqs = np.concatenate([freqs, freqs], -1)
    base = ((half + np.float32(0.4 * DH)) / np.float32(1.4 * DH)).astype(np.float32)
    power = ((t - T // 2) / np.float32(WIN // 2)).astype(np.float32)
    scale = (base[None, :] ** power[:, None]).astype(np.float32)
    scale = np.concatenate([scale, scale], -1)
    sign = np.where(np.arange(DH) < DH // 2, -1, 1).astype(np.float32)
    cos, sin = np.cos(freqs), np.sin(freqs) * sign
    inv = (np.float32(1.0) / scale).astype(np.float32)
    four = np.stack([cos * scale * np.float32(QK_SCALE), sin * scale * np.float32(QK_SCALE), cos * inv, sin * inv])
    return np.ascontiguousarray(four.reshape(4, NT, P, DH).transpose(2, 0, 1, 3)).astype(np.float32)


def band_mask():
    i = (np.arange(P) % WIN)[:, None, None]
    j = np.arange(KEYS)[None, None, :]
    seen = np.broadcast_to((j >= i) & (j <= i + WIN), (P, NT, KEYS)).copy()
    seen[:WIN, 0, :WIN] = False
    return np.where(seen, 0.0, NEG).astype(np.float32)


def rsqrt_steps(dve, done, at, v, y, t, least, add, between={}):
    k = 0

    def step(instruction):
        nonlocal k
        k += 1
        instruction.then_inc(done, 1)
        if k in between:
            between[k]()
        dve.wait_ge(done, at + k)

    step(dve.tensor_scalar(v, v, add, least, ALU.add, ALU.max))
    step(dve.tensor_scalar(y.bitcast(I32), v.bitcast(I32), 1, None, ALU.logical_shift_right))
    step(dve.tensor_scalar(y.bitcast(I32), y.bitcast(I32), -1.0, RSQRT_SEED, ALU.mult, ALU.add))
    for _ in range(3):
        step(dve.tensor_tensor(t, y, y, ALU.mult))
        step(dve.scalar_tensor_tensor(out=t, in0=t, scalar=-0.5, in1=v, op0=ALU.mult, op1=ALU.mult))
        step(dve.scalar_tensor_tensor(out=y, in0=t, scalar=1.5, in1=y, op0=ALU.add, op1=ALU.mult))
    assert k == NEWTON


def is_zero(t):
    return isinstance(t, int) and t == 0


def settle(eng, c):
    eng.sem_inc(c.settled, 1)


def start_at_one(nc, sems):
    with nc.Block() as block:
        @block.sync
        def _(sp):
            for sem in sems:
                sp.sem_inc(sem, 1)


class Chip:
    pass


def scope(nc, ctx):
    def sb(name, shape, dt=F32):
        return ctx.enter_context(nc.sbuf_tensor(name, shape, dt))

    def ps(name, shape, dt=F32):
        return ctx.enter_context(nc.psum_tensor(name, shape, dt))

    held = []

    def sem(name):
        if not held:
            ctx.callback(give_back)
        held.append(nc.alloc_semaphore(name=name))
        return held[-1]

    def give_back():
        nc.clear_and_free_semaphores(held)
        nc.all_engine_barrier()

    return sb, ps, sem


def load_phase(nc, c, d):
    with ExitStack() as ctx:
        sb, ps, sem = scope(nc, ctx)
        xt = sb("xt", [P, B * NT, P])
        rows = sb("rows", [P, P])
        maskf = sb("maskf", [P, NT, KEYS])
        turned = [ps(f"ld_turned{i}", [P, 4, P]) for i in range(4)]
        turned_rows = ps("ld_turned_rows", [P, P])
        x_in, cleared, rows_in, mask_in, rest_in = sem("x_in"), sem("cleared"), sem("rows_in"), sem("mask_in"), sem("rest_in")
        ident_done, x_turned, rows_turned, copied, swapped = (
            sem("ident_done"), sem("x_turned"), sem("rows_turned"), sem("copied"), sem("swapped"))
        single = ["L0_attn_bi", "L0_attn_bf", "L0_attn_bo", "L0_attn_bg", "L0_attn_beg", "L0_attn_gamma", "L0_attn_beta", "L1_attn_out_b"]
        c.col = {name: DEPTH * LV + i for i, name in enumerate(single)}

        with nc.Block() as block:
            @block.gpsimd
            def _(pool):
                pool.memset(c.ident[:, :], 0.0).then_inc(ident_done, 1)
                pool.memset(rows[:, :], 0.0).then_inc(cleared, 1)
                pool.wait_ge(ident_done, 1)
                pool.affine_select(out=c.ident[:, :], in_=c.ident[:, :], compare_op=ALU.not_equal, fill=1.0,
                                   base=0, pattern=[[-1, P]], channel_multiplier=1).then_inc(ident_done, 1)
                pool.wait_ge(ident_done, 2)
                settle(pool, c)
                pool.tensor_copy(c.identb[:, :], c.ident[:, :]).then_inc(copied, 1)
                pool.memset(c.xA[:, :, 0:PAD], 0.0).then_inc(cleared, 1)
                pool.memset(c.xB[:, :, 0:PAD], 0.0).then_inc(cleared, 1)
                pool.memset(c.xA[:, :, PAD + T:], 0.0).then_inc(cleared, 1)
                pool.memset(c.ones[:, :], 1.0).then_inc(cleared, 1)

            @block.sync
            def _(sp):
                for b in range(B):
                    sp.dma_start(xt[:, b * NT:(b + 1) * NT, :],
                                 d["L0_attn_x"][b].rearrange("(t p) f -> p t f", p=P)).then_inc(x_in, 16)
                sp.dma_start(maskf[:, :, :], d["mask"]).then_inc(mask_in, 16)
                sp.dma_start(c.rope[:, :, :, :], d["rope"]).then_inc(rest_in, 16)
                sp.dma_start(c.Wqkv[:, :], d["L0_ffn_Wqkv"][0]).then_inc(rest_in, 16)
                sp.dma_start(c.Wo[:, :, :], d["L0_ffn_Wo"][0].rearrange("(j p) n -> p j n", p=P)).then_inc(rest_in, 16)
                sp.wait_ge(rest_in, 16 * 5)

            @block.scalar
            def _(act):
                act.wait_ge(cleared, 1)
                with nc.allow_non_contiguous_dma(reason="short vectors"):
                    n = 0
                    layered = [("L0_ffn_ln_g", 0, 0, P), ("L0_ffn_ln_b", 1, 0, P), ("L0_ffn_b2", 2, 0, P)]
                    layered += [("L0_ffn_b1", 3 + i, s, w) for i, (s, w) in enumerate(FFC)]
                    layered += [("L0_ffn_b1", 6 + i, FF + s, w) for i, (s, w) in enumerate(FFC)]
                    for name, row, s, w in layered:
                        act.dma_start(rows[row:DEPTH * LV:LV, 0:w], d[name][:, s:s + w]).then_inc(rows_in, 16)
                        n += 1
                    for name in single:
                        act.dma_start(rows[c.col[name]:c.col[name] + 1, :],
                                      d[name].rearrange("(a f) -> a f", a=1)).then_inc(rows_in, 16)
                        n += 1
                    c.n_rows_in = n
                    act.dma_start(c.qks[:, 0, :], d["L0_ffn_q_scale"].rearrange("l f -> (l f)").partition_broadcast(P)).then_inc(rest_in, 16)
                    act.dma_start(c.qks[:, 1, :], d["L0_ffn_k_scale"].rearrange("l f -> (l f)").partition_broadcast(P)).then_inc(rest_in, 16)
                act.wait_ge(mask_in, 16)
                act.copy(c.mask[:, :, :], maskf[:, :, :]).then_inc(copied, 1)
                act.wait_ge(x_turned, 4)
                for g in range(4):
                    b, t = g // 2, (g % 2) * 4
                    act.copy(c.X[:, b, PAD + t * P:PAD + (t + 4) * P], turned[g][:, :, :].rearrange("f t p -> f (t p)")).then_inc(copied, 1)
                act.wait_ge(rows_turned, 1)
                act.copy(c.cols[:, :], turned_rows[:, :]).then_inc(copied, 1)

            @block.vector
            def _(dve):
                dve.wait_ge(rest_in, 16 * 5)
                for i in range(2):
                    halves = [c.qks[:, j, :].rearrange("p (l a d) -> p l a d", a=2, d=DH // 2) for j in (i, 2 + i)]
                    for a in range(2):
                        dve.tensor_copy(halves[1][:, :, a, :], halves[0][:, :, 1 - a, :]).then_inc(swapped, 1)

            @block.tensor
            def _(pe):
                pe.wait_ge(ident_done, 2)
                pe.wait_ge(x_in, 16 * B)
                for g in range(4):
                    for j in range(4):
                        last = pe.transpose(turned[g][:, j, :], xt[:, g * 4 + j, :], c.ident[:, :])
                    last.then_inc(x_turned, 1)
                pe.wait_ge(rows_in, 16 * (9 + len(single)))
                pe.transpose(turned_rows[:, :], rows[:, :], c.ident[:, :]).then_inc(rows_turned, 1)


def norm_phase(nc, c, name, src, dst, affine=None):
    NGR = B * NG
    with ExitStack() as ctx:
        sb, ps, sem = scope(nc, ctx)
        stats = sb(name + "stats", [P, NGR, 4, 6])
        mv = sb(name + "mv", [P, NGR, 4, 2])
        var = sb(name + "var", [P, NGR * 4])
        rstd = sb(name + "rstd", [P, NGR * 4])
        tmp = sb(name + "tmp", [P, NGR * 4])
        xn = sb(name + "xn", [P, NGR, 4, P])
        tok = [ps(f"{name}tok{g}", [P, 4, P]) for g in range(NGR)]
        back = [ps(f"{name}back{g}", [P, 4 * P]) for g in range(NGR)]
        tok_ready, stat, aggr, var_ready, newton = sem(name + "tok_ready"), sem(name + "stat"), sem(name + "aggr"), sem(name + "var_ready"), sem(name + "newton")
        xn_ready, back_ready, out_done = sem(name + "xn_ready"), sem(name + "back_ready"), sem(name + "out_done")
        place = [(g // NG, PAD + (g % NG) * GT) for g in range(NGR)]

        with nc.Block() as block:
            @block.tensor
            def _(pe):
                for g, (b, s) in enumerate(place):
                    for j in range(4):
                        last = pe.transpose(tok[g][:, j, :], src[:, b, s + j * P:s + (j + 1) * P], c.ident[:, :])
                    last.then_inc(tok_ready, 1)
                for g in range(NGR):
                    pe.wait_ge(xn_ready, 4 * (g + 1))
                    for j in range(4):
                        last = pe.transpose(back[g][:, j * P:(j + 1) * P], xn[:, g, j, :], c.ident[:, :])
                    last.then_inc(back_ready, 1)

            @block.vector
            def _(dve):
                for g in range(NGR):
                    dve.wait_ge(tok_ready, g + 1)
                    for j in range(4):
                        dve.bn_stats(stats[:, g, j, :], tok[g][:, j, :]).then_inc(stat, 1)
                for g in range(NGR):
                    dve.wait_ge(stat, 4 * (g + 1))
                    for j in range(4):
                        dve.bn_aggr(mv[:, g, j, :], stats[:, g, j, :]).then_inc(aggr, 1)
                dve.wait_ge(aggr, 4 * NGR)
                dve.tensor_copy(var[:, :], mv[:, :, :, 1].rearrange("p g j -> p (g j)")).then_inc(var_ready, 1)
                dve.wait_ge(var_ready, 1)
                rsqrt_steps(dve, newton, 0, var[:, :], rstd[:, :], tmp[:, :], 0.0, 1e-5)
                for g in range(NGR):
                    for j in range(4):
                        dve.tensor_scalar(xn[:, g, j, :], tok[g][:, j, :], mv[:, g, j, 0:1],
                                          rstd[:, g * 4 + j:g * 4 + j + 1], ALU.subtract, ALU.mult).then_inc(xn_ready, 1)

            @block.scalar
            def _(act):
                for g, (b, s) in enumerate(place):
                    act.wait_ge(back_ready, g + 1)
                    if affine:
                        gain, offset = (c.cols[:, c.col[x]:c.col[x] + 1] for x in affine)
                        act.activation(dst[:, b, s:s + GT], back[g][:, :], ACT.Identity, bias=offset, scale=gain).then_inc(out_done, 1)
                    else:
                        act.copy(dst[:, b, s:s + GT], back[g][:, :]).then_inc(out_done, 1)


def attention_phase(nc, c, layer, nm):
    s = c.sems[nm]
    base = layer * (B * NT)
    qk, vo, sc = c.qk_ps, c.vo_ps, c.sc_ps
    t1, t2, sq, pr = c.t1, c.t2, c.sq, c.probs

    def run(eng, stages):
        def emit(*tiles):
            stages(*(None if x is None else (x[0], x[1], base + 2 * x[1] + x[0], not is_zero(x[1])) for x in tiles))
        emit((0, 0), None, None, None)
        emit((1, 0), (0, 0), None, None)
        emit((0, 1), (1, 0), (0, 0), None)
        emit((1, 1), (0, 1), (1, 0), (0, 0))
        with eng.Fori(2, NT) as t:
            emit((0, t), (1, t - 1), (0, t - 1), (1, t - 2))
            emit((1, t), (0, t), (1, t - 1), (0, t - 1))
        emit(None, (1, NT - 1), (0, NT - 1), (1, NT - 2))
        emit(None, None, (1, NT - 1), (0, NT - 1))
        emit(None, None, None, (1, NT - 1))

    def qview(psum):
        return psum.rearrange("p (h d) -> p h d", d=DH)

    def swapped(psum):
        return psum.rearrange("p (h a d) -> p h a d", a=2, d=DH // 2)[:, :, ::-1, :]

    def quarter(i, half):
        return slice(i * INNER + half * 512, i * INNER + (half + 1) * 512)

    with nc.Block() as block:
        @block.gpsimd
        def _(pool):
            def shifted(dst, src, b, at, width, ready, count):
                pool.tensor_copy(dst[0:64, :], src[0:64, b, bass.ds(at, width)]).then_inc(ready, 1)
                pool.wait_ge(ready, count + 1)
                settle(pool, c)
                pool.tensor_copy(dst[64:P, :], src[64:P, b, bass.ds(at - 1, width)]).then_inc(ready, 1)
                pool.wait_ge(ready, count + 2)
                settle(pool, c)

            def stages(project, turn, attend, finish):
                if project:
                    b, t, n, later = project
                    if later:
                        pool.wait_ge(s.qk_done, 2 * (n - 1))
                        settle(pool, c)
                    shifted(c.xq[b], c.xA, b, PAD + t * P, P, s.xq_ready, 2 * n)
                    if not later:
                        pool.memset(c.KT[b][:, :, 0:WIN], 0.0).then_inc(s.k_moved, 1)
                if turn:
                    b, t, n, later = turn
                    for i in range(2):
                        pool.wait_ge(s.t_ready, 4 * n + 2 * i + 2)
                        part = slice(i * INNER, (i + 1) * INNER)
                        pool.tensor_tensor(t1[:, part], t1[:, part], t2[:, part], ALU.add).then_inc(s.rot_sum, 1)
                    pool.wait_ge(s.newton, NEWTON * (n + 1))
                    for i in range(2):
                        pool.wait_ge(s.rot_sum, 2 * n + i + 1)
                        part = slice(i * INNER, (i + 1) * INNER)
                        pool.tensor_tensor(qview(t1[:, part]), qview(t1[:, part]),
                                           c.rnorm[:, i * HEADS:(i + 1) * HEADS].unsqueeze(2).to_broadcast([P, HEADS, DH]),
                                           ALU.mult).then_inc(s.scaled, 1)
                    if later:
                        pool.wait_ge(s.v_done, 4 * (n - 1))
                        settle(pool, c)
                    shifted(c.xs[b], c.xA, b, PAD - WIN + t * P, WIN + P, s.xs_ready, 2 * n)
                if finish:
                    b, t, n, later = finish
                    pool.wait_ge(s.x_done, n + 1)
                    settle(pool, c)
                    shifted(c.fxs[:, b, bass.ds(t * P, P)], c.xB, b, PAD + t * P, P, s.fxs_ready, 2 * n)
            run(pool, stages)

        @block.tensor
        def _(pe):
            def stages(project, turn, attend, finish):
                def values_by(half, windows):
                    for w in windows:
                        for k in range(half * HALF, (half + 1) * HALF):
                            for par in range(2):
                                rows = slice(64 * par, 64 * par + 64)
                                last = pe.matmul(vo[WIN * w:WIN * w + WIN, par * 512 + k * DH:par * 512 + (k + 1) * DH],
                                                 c.PT[rows, k * P + WIN * w:k * P + WIN * w + WIN],
                                                 c.Vw[rows, w, k * DH:(k + 1) * DH], start=True, stop=True)
                    return last

                def turn_part(i, n):
                    pe.wait_ge(s.scaled, 2 * n + i + 1)
                    for half in range(2):
                        if i == 1:
                            pe.wait_ge(s.kq_ready, 4 * n + half + 1)
                        for k in range(HALF):
                            src = t1[:, quarter(i, half)]
                            last = pe.transpose(sc[:, half * 512 + k * P:half * 512 + (k + 1) * P], src[:, k * P:(k + 1) * P], c.ident[:, :])
                        last.then_inc(s.kq_turned, 1)

                if attend:
                    b, t, n, later = attend
                    pe.wait_ge(s.kq_ready, 4 * n + 4)
                    for h in range(2):
                        pe.matmul(sc[:, h * 512:(h + 1) * 512], c.identb[:, :],
                                  c.mask[:, t, :].unsqueeze(1).to_broadcast([P, 8, KEYS]), start=True, stop=False,
                                  skip_group_check=True)
                    for w in range(NW):
                        for pair in range(PAIRS):
                            for par in range(2):
                                col = par * 512 + pair * KEYS
                                rows = slice(64 * par, 64 * par + 64)
                                last = pe.matmul(sc[WIN * w:WIN * w + WIN, col:col + KEYS],
                                                 c.QT[rows, pair, WIN * w:WIN * w + WIN],
                                                 c.KT[b][rows, pair, WIN * w:WIN * w + KEYS],
                                                 start=False, stop=True, skip_group_check=True)
                    last.then_inc(s.scored, 1)
                if finish:
                    n = finish[2]
                    pe.wait_ge(s.o_normed, n + 1)
                    for k in range(PAIRS):
                        last = pe.transpose(vo[:, k * P:(k + 1) * P], c.On[:, 2 * k:2 * k + 2, :].rearrange("p a d -> p (a d)"),
                                            c.ident[:, :])
                    last.then_inc(s.o_turned, 1)
                if project:
                    b, t, n, later = project
                    pe.wait_ge(s.xq_ready, 2 * n + 2)
                    if later or b:
                        pe.wait_ge(s.t_ready, 4 * n)
                    for i in range(4):
                        last = pe.matmul(qk[:, i * 512:(i + 1) * 512], c.xq[b][:, :], c.Wqkv[:, i * 512:(i + 1) * 512],
                                         start=True, stop=True)
                        if i % 2:
                            last.then_inc(s.qk_done, 1)
                if finish:
                    n = finish[2]
                    pe.wait_ge(s.o_ready, n + 1)
                    for k in range(PAIRS):
                        last = pe.matmul(vo[:, 0:P], c.Wo[:, k, :], c.OT[:, k * P:(k + 1) * P],
                                         start=(k == 0), stop=(k == PAIRS - 1))
                    last.then_inc(s.wo_done, 1)
                if attend:
                    b, t, n, later = attend
                    pe.wait_ge(s.xs_ready, 2 * n + 2)
                    for w in range(NW):
                        if w == 1 and finish:
                            pe.wait_ge(s.x_done, n)
                        if w >= 2:
                            pe.wait_ge(s.v_ready, 4 * n + w - 1)
                        bank = (w + 1) % 2
                        for par in range(2):
                            last = pe.matmul(vo[64 * par:64 * par + 64, bank * 512:(bank + 1) * 512],
                                             c.xs[b][:, WIN * w:WIN * w + KEYS],
                                             c.Wqkv[:, 2 * INNER:3 * INNER].rearrange("p (k a d) -> p a k d", a=2, d=DH)[:, par],
                                             start=True, stop=True)
                        last.then_inc(s.v_done, 1)
                    pe.wait_ge(s.exp_done, n + 1)
                    for k in range(PAIRS):
                        last = pe.transpose(sc[:, k * P:(k + 1) * P], pr[:, 2 * k:2 * k + 2, :].rearrange("p a j -> p (a j)"),
                                            c.ident[:, :])
                        if k % HALF == HALF - 1:
                            last.then_inc(s.p_turned, 1)
                    pe.wait_ge(s.v_ready, 4 * n + 4)
                    pe.wait_ge(s.pt_ready, 2 * n + 1)
                    settle(pe, c)
                    values_by(0, range(NW))
                    pe.wait_ge(s.pt_ready, 2 * n + 2)
                    settle(pe, c)
                if turn:
                    turn_part(0, turn[2])
                if attend:
                    values_by(1, range(NW // 2))
                if turn:
                    turn_part(1, turn[2])
                if attend:
                    values_by(1, range(NW // 2, NW)).then_inc(s.pv_done, 1)
            run(pe, stages)

        @block.vector
        def _(dve):
            def cosine(i, t, n):
                part = slice(i * INNER, (i + 1) * INNER)
                dve.tensor_tensor(qview(t1[:, part]), qview(qk[:, part]),
                                  c.rl[:, 2 * i, bass.ds(t * DH, DH)].unsqueeze(1).to_broadcast([P, HEADS, DH]),
                                  ALU.mult).then_inc(s.t_ready, 1)

            def sine(i, t, n):
                part = slice(i * INNER, (i + 1) * INNER)
                table = c.rl[:, 2 * i + 1, bass.ds(t * DH, DH)].rearrange("p (a d) -> p a d", a=2)
                dve.tensor_tensor(t2[:, part].rearrange("p (h a d) -> p h a d", a=2, d=DH // 2), swapped(qk[:, part]),
                                  table.unsqueeze(1).to_broadcast([P, HEADS, 2, DH // 2]),
                                  ALU.mult).then_inc(s.t_ready, 1)

            def stages(project, turn, attend, finish):
                if attend:
                    b, _, n, later = attend
                    dve.wait_ge(s.scored, n + 1)
                    dve.tensor_reduce(c.mx[:, :], sc.rearrange("p (h j) -> p h j", j=KEYS), AX.X, ALU.max).then_inc(s.max_done, 1)
                    if later or b:
                        dve.wait_ge(s.p_turned, 2 * n)
                    dve.wait_ge(s.max_done, n + 1)
                    dve.tensor_tensor(pr[:, :, :].rearrange("p (k a) j -> p a k j", a=2),
                                      sc.rearrange("p (a k j) -> p a k j", a=2, j=KEYS),
                                      c.mx[:, :].rearrange("p (a k) -> p a k", a=2).unsqueeze(3).to_broadcast([P, 2, PAIRS, KEYS]),
                                      ALU.subtract).then_inc(s.centred, 1)
                if project:
                    n = project[2]
                    for i in range(2):
                        dve.wait_ge(s.sq_done, 2 * n + i + 1)
                        dve.tensor_reduce(c.ssq[:, i * HEADS:(i + 1) * HEADS], qview(sq[:, i * INNER:(i + 1) * INNER]),
                                          AX.X, ALU.add).then_inc(s.ssq_done, 1)
                if finish:
                    b, t, n, _ = finish
                    dve.wait_ge(s.wo_done, n + 1)
                    dve.tensor_tensor(c.xB[:, b, bass.ds(PAD + t * P, P)], vo[:, 0:P],
                                      c.xA[:, b, bass.ds(PAD + t * P, P)], ALU.add).then_inc(s.x_done, 1)

                def row_sums():
                    if attend:
                        n = attend[2]
                        dve.wait_ge(s.exp_done, n + 1)
                        dve.tensor_reduce(c.rsum[:, :], pr[:, :, :], AX.X, ALU.add).then_inc(s.inverted, 1)
                if project:
                    b, t, n, later = project
                    dve.wait_ge(s.ssq_done, 2 * n + 2)
                    if later or b:
                        dve.wait_ge(s.scaled, 2 * n)
                    rsqrt_steps(dve, s.newton, n * NEWTON, c.ssq[:, :], c.rnorm[:, :], c.ntmp[:, :], 1e-24, 0.0,
                                {1: row_sums})
                    if later or b:
                        dve.wait_ge(s.kq_turned, 4 * n - 2)
                    cosine(0, t, n)
                    sine(0, t, n)
                    if later or b:
                        dve.wait_ge(s.kq_turned, 4 * n)
                    cosine(1, t, n)
                else:
                    row_sums()
                if attend:
                    n = attend[2]
                    dve.wait_ge(s.inverted, 2 * n + 1)
                    dve.reciprocal(c.rsum[:, :], c.rsum[:, :]).then_inc(s.inverted, 1)
                    dve.wait_ge(s.inverted, 2 * n + 2)
                    dve.wait_ge(s.pv_done, n + 1)
                    dve.tensor_tensor(c.On[:, :, :].rearrange("p (k a) d -> p a k d", a=2),
                                      vo.rearrange("p (a k d) -> p a k d", a=2, d=DH),
                                      c.rsum[:, :].rearrange("p (k a) -> p a k", a=2).unsqueeze(3).to_broadcast([P, 2, PAIRS, DH]),
                                      ALU.mult).then_inc(s.o_normed, 1)
                if project:
                    sine(1, project[1], project[2])
            for i in range(2):
                scale = c.qks[:, i, bass.ds(layer * DH, DH)]
                dve.tensor_tensor(c.rl[:, 2 * i, :].rearrange("p (t d) -> p t d", d=DH), c.rope[:, 2 * i, :, :],
                                  scale.unsqueeze(1).to_broadcast([P, NT, DH]), ALU.mult).then_inc(s.table, 1)
                other = c.qks[:, 2 + i, bass.ds(layer * DH, DH)]
                dve.tensor_tensor(c.rl[:, 2 * i + 1, :].rearrange("p (t d) -> p t d", d=DH), c.rope[:, 2 * i + 1, :, :],
                                  other.unsqueeze(1).to_broadcast([P, NT, DH]), ALU.mult).then_inc(s.table, 1)
            dve.wait_ge(s.table, 4 * (layer + 1))
            settle(dve, c)
            run(dve, stages)

        @block.scalar
        def _(act):
            def stages(project, turn, attend, finish):
                if finish:
                    b, t, n, later = finish
                    act.wait_ge(s.o_turned, n + 1)
                    if later or b:
                        act.wait_ge(s.wo_done, n)
                    act.copy(c.OT[:, :], vo).then_inc(s.o_ready, 1)
                if attend:
                    n = attend[2]
                    act.wait_ge(s.centred, n + 1)
                    act.activation(pr[:, :, :], pr[:, :, :], ACT.Exp).then_inc(s.exp_done, 1)
                if project:
                    b, t, n, later = project
                    for i in range(2):
                        act.wait_ge(s.qk_done, 2 * n + i + 1)
                        if later or b:
                            act.wait_ge(s.ssq_done, 2 * n)
                        act.activation(sq[:, i * INNER:(i + 1) * INNER], qk[:, i * INNER:(i + 1) * INNER],
                                       ACT.Square).then_inc(s.sq_done, 1)
                if attend:
                    b, t, n, later = attend
                    for w in range(NW):
                        act.wait_ge(s.v_done, 4 * n + w + 1)
                        if later or b:
                            act.wait_ge(s.pv_done, n)
                        bank = (w + 1) % 2
                        act.copy(c.Vw[:, w, :], vo[:, bank * 512:(bank + 1) * 512]).then_inc(s.v_ready, 1)
                    for half in range(2):
                        act.wait_ge(s.p_turned, 2 * n + half + 1)
                        act.copy(c.PT[:, half * 512:(half + 1) * 512], sc[:, half * 512:(half + 1) * 512]).then_inc(s.pt_ready, 1)
                if turn:
                    b, t, n, later = turn
                    if later or b:
                        act.wait_ge(s.scored, n)
                    if later:
                        act.copy(c.KT[b][:, :, 0:WIN], c.KT[b][:, :, P:P + WIN]).then_inc(s.k_moved, 1)
                    for i in range(2):
                        for half in range(2):
                            act.wait_ge(s.kq_turned, 4 * n + 2 * i + half + 1)
                            if i == 0:
                                dst = c.QT[:, half * HALF:(half + 1) * HALF, :]
                            else:
                                if half == 0:
                                    act.wait_ge(s.k_moved, n + 1)
                                dst = c.KT[b][:, half * HALF:(half + 1) * HALF, WIN:WIN + P]
                            act.copy(dst, sc[:, half * 512:(half + 1) * 512].rearrange("p (k m) -> p k m", m=P)).then_inc(s.kq_ready, 1)
            act.activation(c.scrap[:, :], c.ones[:, 0:1], ACT.Exp).then_inc(s.table_load, 1)
            run(act, stages)

        @block.sync
        def _(sp):
            W1, W2 = c.d["L0_ffn_W1"], c.d["L0_ffn_W2"]
            sp.dma_start(c.W1[:, :], W1[bass.ds(layer, 1)].rearrange("l p n -> p (l n)")).then_inc(s.w_in, 16)
            sp.dma_start(c.W2[:, 0:2, :], W2[bass.ds(layer, 1), 0:256, :].rearrange("l (j p) n -> p (l j) n", p=P)).then_inc(s.w_in, 16)
            w = FFC[2][1]
            sp.dma_start(c.W2[0:w, 2, :], W2[bass.ds(layer, 1), 256:FF, :].rearrange("l p n -> p (l n)")).then_inc(s.w_in, 16)
            sp.wait_ge(s.w_in, 16 * 3 * (layer + 1))
            settle(sp, c)


class TransformerSemaphores:
    def __init__(self, sem, nm):
        self.xq_ready, self.centred, self.scaled, self.inverted = (
            sem(nm + "_xq_ready"), sem(nm + "_centred"), sem(nm + "_scaled"), sem(nm + "_inverted"))
        self.xs_ready, self.qk_done, self.sq_done, self.ssq_done = (
            sem(nm + "_xs_ready"), sem(nm + "_qk_done"), sem(nm + "_sq_done"), sem(nm + "_ssq_done"))
        self.newton, self.t_ready, self.rot_sum = (
            sem(nm + "_newton"), sem(nm + "_t_ready"), sem(nm + "_rot_sum"))
        self.kq_turned, self.kq_ready, self.k_moved, self.scored = (
            sem(nm + "_kq_turned"), sem(nm + "_kq_ready"), sem(nm + "_k_moved"), sem(nm + "_scored"))
        self.max_done, self.exp_done = sem(nm + "_max_done"), sem(nm + "_exp_done")
        self.o_normed, self.o_turned, self.p_turned, self.pt_ready = (
            sem(nm + "_o_normed"), sem(nm + "_o_turned"), sem(nm + "_p_turned"), sem(nm + "_pt_ready"))
        self.v_done, self.v_ready, self.pv_done, self.o_ready = (
            sem(nm + "_v_done"), sem(nm + "_v_ready"), sem(nm + "_pv_done"), sem(nm + "_o_ready"))
        self.wo_done, self.x_done, self.table, self.table_load = (
            sem(nm + "_wo_done"), sem(nm + "_x_done"), sem(nm + "_table"), sem(nm + "_table_load"))
        self.w_in = sem(nm + "_w_in")
        self.fxs_ready, self.f_tok, self.f_stat, self.f_aggr = (
            sem(nm + "_fxs_ready"), sem(nm + "_f_tok"), sem(nm + "_f_stat"), sem(nm + "_f_aggr"))
        self.f_var, self.f_newton, self.f_xn, self.f_turned = (
            sem(nm + "_f_var"), sem(nm + "_f_newton"), sem(nm + "_f_xn"), sem(nm + "_f_turned"))
        self.f_xnT, self.f_h, self.f_gelu, self.f_prod = (
            sem(nm + "_f_xnT"), sem(nm + "_f_h"), sem(nm + "_f_gelu"), sem(nm + "_f_prod"))
        self.f_out, self.f_x, self.f_cols, self.f_next = (
            sem(nm + "_f_out"), sem(nm + "_f_x"), sem(nm + "_f_cols"), sem(nm + "_f_next"))
        self.f_load = sem(nm + "_f_load")


def ffn_phase(nc, c, layer, nm):
    s = c.sems[nm]
    NGR, NC = B * NG, len(FFC)
    place = [(g // NG, (g % NG) * GT) for g in range(NGR)]
    rows, pairs = c.row_ps, c.h_ps
    group0, chunk0 = layer * NGR, layer * (NGR * NC)

    with nc.Block() as block:
        @block.tensor
        def _(pe):
            for g, (b, at) in enumerate(place):
                for j in range(4):
                    last = pe.transpose(rows[g][:, j * P:(j + 1) * P], c.fxs[:, b, at + j * P:at + (j + 1) * P], c.ident[:, :])
                last.then_inc(s.f_tok, 1)

            def turn_back(g):
                pe.wait_ge(s.f_xn, 4 * group0 + 4 * g + 4)
                for j in range(4):
                    last = pe.transpose(rows[g][:, j * P:(j + 1) * P], c.fxn[:, g % 2, j, :], c.ident[:, :])
                last.then_inc(s.f_turned, 1)

            def expand(g, i):
                at, w = FFC[i]
                q = NC * g + i
                if q >= 2:
                    pe.wait_ge(s.f_prod, chunk0 + q - 1)
                gate, lin = pairs[q % 2]
                pe.matmul(gate[0:w, :], c.W1[:, FF + at:FF + at + w], c.fxnT[:, g % 2, :], start=True, stop=True).then_inc(s.f_h, 1)
                pe.matmul(lin[0:w, :], c.W1[:, at:at + w], c.fxnT[:, g % 2, :], start=True, stop=True).then_inc(s.f_h, 1)

            def contract(g):
                for i, (at, w) in enumerate(FFC):
                    pe.wait_ge(s.f_prod, chunk0 + NC * g + i + 1)
                    last = pe.matmul(rows[g], c.W2[0:w, i, :], c.fh[0:w, g % 2, i, :], start=(i == 0), stop=(i == NC - 1))
                last.then_inc(s.f_out, 1)

            turn_back(0)
            for g in range(NGR):
                pe.wait_ge(s.f_xnT, group0 + g + 1)
                expand(g, 0)
                if g > 0:
                    contract(g - 1)
                expand(g, 1)
                if g + 1 < NGR:
                    turn_back(g + 1)
                expand(g, 2)
            contract(NGR - 1)

        @block.vector
        def _(dve):
            dve.tensor_copy(c.lcols[:, :], c.cols[:, bass.ds(layer * LV, LV)]).then_inc(s.f_cols, 1)
            dve.wait_ge(s.f_cols, layer + 1)
            settle(dve, c)
            for g in range(NGR):
                dve.wait_ge(s.f_tok, group0 + g + 1)
                settle(dve, c)
                for j in range(4):
                    dve.bn_stats(c.fstat[:, 4 * g + j, :], rows[g][:, j * P:(j + 1) * P]).then_inc(s.f_stat, 1)
            dve.wait_ge(s.f_stat, 4 * group0 + 4 * NGR)
            settle(dve, c)
            for j in range(4 * NGR):
                dve.bn_aggr(c.fmv[:, j, :], c.fstat[:, j, :]).then_inc(s.f_aggr, 1)
            dve.wait_ge(s.f_aggr, 4 * group0 + 4 * NGR)
            dve.tensor_copy(c.fvar[:, :], c.fmv[:, :, 1]).then_inc(s.f_var, 1)
            dve.wait_ge(s.f_var, layer + 1)
            rsqrt_steps(dve, s.f_newton, layer * NEWTON, c.fvar[:, :], c.frstd[:, :], c.ftmp[:, :], 0.0, 1e-5)

            def normalise(g):
                if g >= 2:
                    dve.wait_ge(s.f_turned, group0 + g - 1)
                for j in range(4):
                    n = 4 * g + j
                    dve.tensor_scalar(c.fxn[:, g % 2, j, :], rows[g][:, j * P:(j + 1) * P], c.fmv[:, n, 0:1], c.frstd[:, n:n + 1],
                                      ALU.subtract, ALU.mult).then_inc(s.f_xn, 1)

            def multiply(g, i):
                w, q = FFC[i][1], NC * g + i
                dve.wait_ge(s.f_h, 2 * chunk0 + 2 * q + 2)
                dve.wait_ge(s.f_gelu, chunk0 + q + 1)
                dve.scalar_tensor_tensor(out=c.fh[0:w, g % 2, i, :], in0=pairs[q % 2][1][0:w, :], scalar=c.lcols[0:w, 3 + i:4 + i],
                                         in1=c.fg[0:w, i, :], op0=ALU.add, op1=ALU.mult).then_inc(s.f_prod, 1)

            def finish(g):
                b, at = place[g]
                dve.wait_ge(s.f_out, group0 + g + 1)
                dve.scalar_tensor_tensor(out=c.xA[:, b, PAD + at:PAD + at + GT], in0=rows[g], scalar=c.lcols[:, 2:3],
                                         in1=c.xB[:, b, PAD + at:PAD + at + GT], op0=ALU.add, op1=ALU.add).then_inc(s.f_x, 1)

            normalise(0)
            normalise(1)
            for g in range(NGR):
                multiply(g, 0)
                if g > 0:
                    finish(g - 1)
                multiply(g, 1)
                if g + 2 < NGR:
                    normalise(g + 2)
                multiply(g, 2)
            finish(NGR - 1)

        @block.scalar
        def _(act):
            act.activation(c.scrap[:, :], c.ones[:, 0:1], ACT.Gelu).then_inc(s.f_load, 1)
            act.wait_ge(s.f_cols, layer + 1)

            def scale(g):
                act.wait_ge(s.f_turned, group0 + g + 1)
                if g >= 2:
                    act.wait_ge(s.f_h, 2 * chunk0 + 2 * NC * (g - 1))
                act.activation(c.fxnT[:, g % 2, :], rows[g], ACT.Identity, bias=c.lcols[:, 1:2], scale=c.lcols[:, 0:1]).then_inc(s.f_xnT, 1)

            def gelu(g, i):
                w, q = FFC[i][1], NC * g + i
                act.wait_ge(s.f_h, 2 * chunk0 + 2 * q + 1)
                if g > 0:
                    act.wait_ge(s.f_prod, chunk0 + q - NC + 1)
                act.activation(c.fg[0:w, i, :], pairs[q % 2][0][0:w, :], ACT.Gelu, bias=c.lcols[0:w, 6 + i:7 + i]).then_inc(s.f_gelu, 1)

            scale(0)
            for g in range(NGR):
                gelu(g, 0)
                gelu(g, 1)
                if g + 1 < NGR:
                    scale(g + 1)
                gelu(g, 2)

        @block.sync
        def _(sp):
            nxt = sp.snap((layer + 1) % (DEPTH))
            sp.dma_start(c.Wqkv[:, :], c.d["L0_ffn_Wqkv"][bass.ds(nxt, 1)].rearrange("l p n -> p (l n)")).then_inc(s.f_next, 16)
            sp.dma_start(c.Wo[:, :, :], c.d["L0_ffn_Wo"][bass.ds(nxt, 1)].rearrange("l (j p) n -> p (l j) n", p=P)).then_inc(s.f_next, 16)
            sp.wait_ge(s.f_next, 32 * (layer + 1))
            settle(sp, c)


def residual_phase(nc, c, name, scale):
    with ExitStack() as ctx:
        _, _, sem = scope(nc, ctx)
        done = sem(name)
        with nc.Block() as block:
            @block.vector
            def _(dve):
                for b in range(B):
                    dve.scalar_tensor_tensor(out=c.X[:, b, PAD:PAD + T], in0=c.xA[:, b, PAD:PAD + T], scalar=scale, in1=c.X[:, b, PAD:PAD + T],
                                             op0=ALU.mult, op1=ALU.add).then_inc(done, 1)


def transformer(nc, c, nm, dump=None):
    norm_phase(nc, c, nm + "n", c.X, c.xA)
    with ExitStack() as ctx:
        sb, ps, sem = scope(nc, ctx)
        c.rl = sb("rl" + nm, [P, 4, NT * DH])
        with ExitStack() as low:
            sb, ps, _ = scope(nc, low)
            c.xq = [sb(f"xq{b}" + nm, [P, P]) for b in range(B)]
            c.xs = [sb(f"xs{b}" + nm, [P, WIN + P]) for b in range(B)]
            c.t1, c.t2, c.sq = (sb(x + nm, [P, 2 * INNER]) for x in ("t1", "t2", "sq"))
            c.ssq, c.rnorm, c.ntmp = (sb(x + nm, [P, 2 * HEADS]) for x in ("ssq", "rnorm", "ntmp"))
            c.mx, c.rsum = (sb(x + nm, [P, HEADS]) for x in ("mx", "rsum"))
            c.QT = sb("QT" + nm, [P, PAIRS, P])
            c.Vw = sb("Vw" + nm, [P, NW, PAIRS * DH])
            c.On = sb("On" + nm, [P, HEADS, DH])
            c.probs = sb("probs" + nm, [P, HEADS, KEYS])
            c.PT, c.OT = (sb(x + nm, [P, PAIRS * P]) for x in ("PT", "OT"))
            c.fxs, c.fxnT = sb("fxs" + nm, [P, B, T]), sb("fxnT" + nm, [P, 2, GT])
            c.fxn = sb("fxn" + nm, [P, 2, 4, P])
            c.fg, c.fh = sb("fg" + nm, [P, 3, GT]), sb("fh" + nm, [P, 2, 3, GT])
            c.fstat, c.fmv = sb("fstat" + nm, [P, B * NT, 6]), sb("fmv" + nm, [P, B * NT, 2])
            c.fvar, c.frstd, c.ftmp = (sb(x + nm, [P, B * NT]) for x in ("fvar", "frstd", "ftmp"))
            c.lcols = sb("lcols" + nm, [P, LV])
            bank = ps("banks" + nm, [P, 8 * 512])
            c.qk_ps, c.vo_ps, c.sc_ps = bank[:, 0:2048], bank[:, 2048:3072], bank[:, 3072:4096]
            part = lambda i: bank[:, i * 512:(i + 1) * 512]
            c.row_ps = [part(i) for i in range(4)]
            c.h_ps = [(part(4), part(5)), (part(6), part(7))]
            c.sems[nm] = TransformerSemaphores(sem, nm)
            with nc.Fori(0, c.depth) as layer:
                attention_phase(nc, c, layer, nm)
                ffn_phase(nc, c, layer, nm)
    residual_phase(nc, c, nm + "res", 0.5)


GATES = ("i", "f", "o", "g")
EARLY_TERMS = [(0, 0), (1, 0), (2, 0), (0, 1), (1, 1)]
LAST_TERM = (0, 2)


def recurrence_phase(nc, c):
    with ExitStack() as ctx:
        sb, ps, sem = scope(nc, ctx)
        Wg = sb("Wgates", [P, 4, 2, P])
        Wparts = sb("Wparts", [P, 3, 3, P], BF16)
        wrest = sb("wrest", [P, 3, P])
        bias = sb("gate_bias", [1, 4, P])
        Weg = sb("Weg", [P, P])
        hbuf = [sb(f"hbuf{i}", [P, B, CH]) for i in range(2)]
        hparts, hrest = sb("hparts", [P, 3, B], BF16), sb("hrest", [P, B])
        tg, es, sg, ex, eo = sb("tg", [P, B]), sb("es", [P, 2, B]), sb("sg", [P, 2, B]), sb("ex", [P, B]), sb("eo", [P, B])
        cn, fcn = sb("cn", [P, 2, B]), sb("fcn", [P, 2, B])
        ig, no, rn = sb("ig", [P, B]), sb("no", [P, B]), sb("rn", [P, B])
        g_bank = [ps(f"g_bank{i}", [P, 512]) for i in range(2)]
        s_bank = [ps(f"s_bank{i}", [P, 512]) for i in range(2)]
        o_bank = [ps(f"o_bank{i}", [P, 512]) for i in range(2)]
        e_bank = ps("e_bank", [P, 512])
        w_in, zeroed, w_split = sem("r_w_in"), sem("r_zeroed"), sem("r_w_split")
        table_loaded, g_done, s_done, o_done, e_done = (
            sem("r_table_loaded"), sem("r_g_done"), sem("r_s_done"), sem("r_o_done"), sem("r_e_done"))
        tg_ready, es_ready, ex_ready, eo_ready, h_ready = (
            sem("r_tg_ready"), sem("r_es_ready"), sem("r_ex_ready"), sem("r_eo_ready"), sem("r_h_ready"))
        h_split, sg_done, fcn_done, ig_done, c_done, n_done, no_done, rn_done, y_done = (
            sem("r_" + x) for x in ("h_split", "sg_done", "fcn_done", "ig_done", "c_done", "n_done", "no_done", "rn_done", "y_done"))
        CHUNKS = T // CH
        start_at_one(nc, [h_ready, y_done] + 4 * [h_split])

        with nc.Block() as block:
            @block.sync
            def _(sp):
                for i, g in enumerate(GATES):
                    sp.dma_start(Wg[:, i, :, :], c.d[f"L0_attn_W{g}"].rearrange("(a p) n -> p a n", p=P)).then_inc(w_in, 16)
                    sp.dma_start(bias[:, i, :], c.d[f"L0_attn_b{g}"].rearrange("(a n) -> a n", a=1)).then_inc(w_in, 16)
                sp.dma_start(Weg[:, :], c.d["L0_attn_Weg"]).then_inc(w_in, 16)
                sp.wait_ge(w_in, 16 * 9)

            @block.gpsimd
            def _(pool):
                pool.memset(cn[:, :, :], 0.0).then_inc(zeroed, 1)
                pool.memset(hbuf[1][:, :, :], 0.0).then_inc(zeroed, 1)
                pool.memset(hparts[:, :, :], 0.0).then_inc(zeroed, 1)

            @block.vector
            def _(dve):
                dve.wait_ge(w_in, 16 * 9)
                W = Wg[:, 0:3, 1, :]
                dve.tensor_copy(Wparts[:, :, 0, :], W).then_inc(w_split, 1)
                dve.wait_ge(w_split, 1)
                dve.tensor_tensor(wrest[:, :, :], W, Wparts[:, :, 0, :], ALU.subtract).then_inc(w_split, 1)
                dve.wait_ge(w_split, 2)
                dve.tensor_copy(Wparts[:, :, 1, :], wrest[:, :, :]).then_inc(w_split, 1)
                dve.wait_ge(w_split, 3)
                dve.tensor_tensor(Wparts[:, :, 2, :], wrest[:, :, :], Wparts[:, :, 1, :], ALU.subtract).then_inc(w_split, 1)

        with nc.Block() as block:
            @block.tensor
            def _(pe):
                def project(j, at, which):
                    gate, part = which // 2, which % 2
                    if GATES[gate] in "go":
                        bank = g_bank if GATES[gate] == "g" else o_bank
                        out = bank[j][:, 0:CH * B].rearrange("p (s b) -> p b s", b=B)
                        first = part == 0
                    else:
                        out = s_bank[j][:, 0:CH * 2 * B].rearrange("p (s g b) -> p g b s", g=2, b=B)[:, gate]
                        first = which == 0
                    if part == 0:
                        lhsT, rhs = bias[0:1, gate, :], c.ones[0:1, 0:B * CH].rearrange("p (b s) -> p b s", b=B)
                    else:
                        lhsT, rhs = Wg[:, gate, 0, :], c.xA[:, :, bass.ds(at, CH)]
                    return pe.matmul(out, lhsT, rhs, start=first, stop=False, skip_group_check=True)

                def recur(out, gate, terms):
                    for w_part, h_part in terms:
                        last = pe.matmul(out, Wparts[:, gate, w_part, :], hparts[:, h_part, :], start=False,
                                         stop=(w_part, h_part) == LAST_TERM, skip_group_check=True)
                    return last

                for which in range(8):
                    project(0, PAD, which)
                with pe.Fori(0, CHUNKS // 2) as it:
                    for j in range(2):
                        for s in range(CH):
                            n = it * (2 * CH) + j * CH + s
                            h = hbuf[j][:, :, s - 1] if s else hbuf[1 - j][:, :, CH - 1]
                            i_out, f_out = (s_bank[j][:, (s * 2 + gate) * B:(s * 2 + gate + 1) * B] for gate in range(2))
                            o_out = o_bank[j][:, s * B:(s + 1) * B]
                            pe.wait_ge(h_ready, n + 1)
                            pe.matmul(g_bank[j][:, s * B:(s + 1) * B], Wg[:, 3, 1, :], h, start=False, stop=True,
                                      skip_group_check=True).then_inc(g_done, 1)
                            pe.wait_ge(h_split, 4 * n + 2)
                            recur(i_out, 0, EARLY_TERMS)
                            recur(f_out, 1, EARLY_TERMS)
                            pe.wait_ge(h_split, 4 * n + 4)
                            recur(i_out, 0, [LAST_TERM])
                            recur(f_out, 1, [LAST_TERM]).then_inc(s_done, 1)
                            pe.wait_ge(tg_ready, n + 1)
                            pe.matmul(e_bank[:, 0:B], Weg[:, :], tg[:, :], start=True, stop=True).then_inc(e_done, 1)
                            recur(o_out, 2, EARLY_TERMS + [LAST_TERM]).then_inc(o_done, 1)
                            if s % 2 == 1:
                                project(1 - j, it * (2 * CH) + (PAD + (j + 1) * CH), s // 2)

            @block.scalar
            def _(act):
                act.activation(c.scrap[:, :], c.ones[:, 0:1], ACT.Exp).then_inc(table_loaded, 1)
                with act.Fori(0, CHUNKS // 2) as it:
                    for j in range(2):
                        for s in range(CH):
                            n = it * (2 * CH) + j * CH + s
                            act.wait_ge(g_done, n + 1)
                            act.activation(tg[:, :], g_bank[j][:, s * B:(s + 1) * B], ACT.Tanh).then_inc(tg_ready, 1)
                            act.wait_ge(s_done, n + 1)
                            act.activation(es[:, :, :].rearrange("p g b -> p (g b)"), s_bank[j][:, s * 2 * B:(s + 1) * 2 * B],
                                           ACT.Exp, scale=-1.0).then_inc(es_ready, 1)
                            act.wait_ge(e_done, n + 1)
                            act.activation(ex[:, :], e_bank[:, 0:B], ACT.Exp,
                                           bias=c.cols[:, c.col["L0_attn_beg"]:c.col["L0_attn_beg"] + 1]).then_inc(ex_ready, 1)
                            act.wait_ge(o_done, n + 1)
                            act.activation(eo[:, :], o_bank[j][:, s * B:(s + 1) * B], ACT.Exp, scale=-1.0).then_inc(eo_ready, 1)

            @block.vector
            def _(dve):
                with dve.Fori(0, CHUNKS // 2) as it:
                    for j in range(2):
                        for s in range(CH):
                            n = it * (2 * CH) + j * CH + s
                            if s == CH // 2:
                                dve.wait_ge(y_done, it * 2 + j + 1)
                            dve.wait_ge(es_ready, n + 1)
                            dve.tensor_scalar(sg[:, :, :], es[:, :, :], 1.0, None, ALU.add).then_inc(sg_done, 1)
                            dve.wait_ge(sg_done, 2 * n + 1)
                            dve.reciprocal(sg[:, :, :], sg[:, :, :]).then_inc(sg_done, 1)
                            dve.wait_ge(sg_done, 2 * n + 2)
                            dve.tensor_tensor(fcn[:, :, :], cn[:, :, :], sg[:, 1:2, :].to_broadcast([P, 2, B]), ALU.mult).then_inc(fcn_done, 1)
                            dve.tensor_tensor(ig[:, :], sg[:, 0, :], tg[:, :], ALU.mult).then_inc(ig_done, 1)
                            dve.wait_ge(fcn_done, n + 1)
                            dve.wait_ge(ex_ready, n + 1)
                            for b in range(B):
                                dve.scalar_tensor_tensor(out=cn[:, 1, b:b + 1], in0=ex[:, b:b + 1], scalar=sg[:, 0, b:b + 1],
                                                         in1=fcn[:, 1, b:b + 1], op0=ALU.mult, op1=ALU.add).then_inc(n_done, 1)
                            dve.wait_ge(ig_done, n + 1)
                            dve.tensor_tensor(cn[:, 0, :], ig[:, :], fcn[:, 0, :], ALU.add).then_inc(c_done, 1)
                            dve.wait_ge(eo_ready, n + 1)
                            dve.wait_ge(n_done, 2 * n + 2)
                            dve.scalar_tensor_tensor(out=no[:, :], in0=eo[:, :], scalar=1.0, in1=cn[:, 1, :],
                                                     op0=ALU.add, op1=ALU.mult).then_inc(no_done, 1)
                            dve.wait_ge(no_done, n + 1)
                            dve.reciprocal(rn[:, :], no[:, :]).then_inc(rn_done, 1)
                            dve.wait_ge(rn_done, n + 1)
                            dve.wait_ge(c_done, n + 1)
                            h = hbuf[j][:, :, s]
                            dve.tensor_tensor(h, cn[:, 0, :], rn[:, :], ALU.mult).then_inc(h_ready, 1)
                            dve.tensor_tensor(hparts[:, 0, :], cn[:, 0, :], rn[:, :], ALU.mult).then_inc(h_split, 1)
                            dve.wait_ge(h_ready, n + 1 + 1)
                            dve.wait_ge(h_split, 4 * n + 4 + 1)
                            dve.tensor_tensor(hparts[:, 1, :], h, hparts[:, 0, :], ALU.subtract).then_inc(h_split, 1)
                            dve.tensor_tensor(hrest[:, :], h, hparts[:, 0, :], ALU.subtract).then_inc(h_split, 1)
                            dve.wait_ge(h_split, 4 * n + 4 + 3)
                            dve.tensor_tensor(hparts[:, 2, :], hrest[:, :], hparts[:, 1, :], ALU.subtract).then_inc(h_split, 1)

            @block.gpsimd
            def _(pool):
                with pool.Fori(0, CHUNKS // 2) as it:
                    for j in range(2):
                        pool.wait_ge(h_ready, it * (2 * CH) + (j + 1) * CH + 1)
                        at = it * (2 * CH) + (PAD + j * CH)
                        pool.tensor_tensor(c.xB[:, :, bass.ds(at, CH)], hbuf[j][:, :, :], c.xA[:, :, bass.ds(at, CH)],
                                           ALU.add).then_inc(y_done, 1)


def experts_phase(nc, c, nm):
    E, N16 = EXPERTS, B * NT
    EP = E + 8 - TOPK
    with ExitStack() as ctx:
        sb, ps, sem = scope(nc, ctx)
        wg1, wg2, bg1 = sb("wg1" + nm, [P, GH]), sb("wg2" + nm, [GH, 2 * E]), sb("bg1" + nm, [GH, 1])
        bg2, We, be = sb("bg2" + nm, [P, 2 * E]), sb("We" + nm, [P, E, P]), sb("be" + nm, [E, P])
        hT = sb("hT" + nm, [GH, B, T])
        lg, pb, gates = sb("lg" + nm, [P, N16, E]), sb("pb" + nm, [P, N16, EP]), sb("gates" + nm, [P, N16, EP])
        mx, sm = sb("emx" + nm, [P, N16]), sb("esm" + nm, [P, N16])
        top, drop = sb("top" + nm, [P, N16, 8]), sb("drop" + nm, [P, N16, 8])
        gT = sb("gT" + nm, [E, B, T])
        xt = [sb(f"ext{b}" + nm, [P, P]) for b in range(B)]
        y = [[sb(f"ey{b}{i}" + nm, [P, P]) for i in range(2)] for b in range(B)]
        with ExitStack() as low:
            _, ps, sem = scope(nc, low)
            h_ps = [ps(f"eh{i}" + nm, [P, 512]) for i in range(4)]
            l_ps = ps("el" + nm, [P, 512])
            w_in, small_in, h_done, gelu, logits = (sem(nm + x) for x in ("w_in", "small_in", "h_done", "gelu", "logits"))
            soft, exped, topped = (sem(nm + x) for x in ("soft", "exped", "topped"))
            gt_turned, gt_ready, filled, loaded = sem(nm + "gt_turned"), sem(nm + "gt_ready"), sem(nm + "filled"), sem(nm + "loaded")
            with nc.Block() as block:
                @block.sync
                def _(sp):
                    with nc.allow_non_contiguous_dma(reason="a short vector to a column"):
                        sp.dma_start(bg1[:, :], c.d["L1_ffn_bg1"].rearrange("(p a) -> p a", a=1)).then_inc(small_in, 16)
                    sp.dma_start(wg1[:, :], c.d["L1_ffn_wg1"]).then_inc(small_in, 16)
                    sp.dma_start(wg2[:, :], c.d["L1_ffn_wg2"]).then_inc(small_in, 16)
                    sp.dma_start(bg2[:, :], c.d["L1_ffn_bg2"].partition_broadcast(P)).then_inc(small_in, 16)
                    sp.dma_start(be[:, :], c.d["L1_ffn_be"]).then_inc(small_in, 16)
                    sp.dma_start(We[:, :, :], c.d["L1_ffn_We"].rearrange("e p n -> p e n")).then_inc(w_in, 16)
                    sp.wait_ge(w_in, 16)
                    sp.wait_ge(small_in, 16 * 5)

                @block.gpsimd
                def _(pool):
                    pool.memset(pb[:, :, E:EP], -1.0).then_inc(filled, 1)
                    pool.memset(drop[:, :, TOPK:8], -1.0).then_inc(filled, 1)

                @block.tensor
                def _(pe):
                    pe.wait_ge(small_in, 16 * 5)
                    for g in range(4):
                        pe.matmul(h_ps[g][0:GH, :], wg1[:, :], c.xA[:, g // 2, PAD + (g % 2) * GT:PAD + (g % 2 + 1) * GT],
                                  start=True, stop=True).then_inc(h_done, 1)
                    for n in range(N16):
                        if n % 4 == 0:
                            pe.wait_ge(gelu, n // 4 + 1)
                        last = pe.matmul(l_ps[:, n * E:(n + 1) * E], hT[:, n // NT, (n % NT) * P:(n % NT + 1) * P], wg2[:, 0:E],
                                         start=True, stop=True)
                    last.then_inc(logits, 1)
                    for g in range(4):
                        pe.wait_ge(topped, N16 + 1)
                        for j in range(4):
                            last = pe.transpose(h_ps[g][0:E, j * P:(j + 1) * P], gates[:, 4 * g + j, 0:E], c.ident[:, :])
                        last.then_inc(gt_turned, 1)

                @block.scalar
                def _(act):
                    for g in range(4):
                        act.wait_ge(h_done, g + 1)
                        act.activation(hT[:, g // 2, (g % 2) * GT:(g % 2 + 1) * GT], h_ps[g][0:GH, :], ACT.Gelu, bias=bg1[:, :]).then_inc(gelu, 1)
                    act.wait_ge(soft, 3)
                    act.activation(pb[:, :, 0:E], lg[:, :, :], ACT.Exp).then_inc(exped, 1)
                    for g in range(4):
                        act.wait_ge(gt_turned, g + 1)
                        act.copy(gT[:, g // 2, (g % 2) * GT:(g % 2 + 1) * GT], h_ps[g][0:E, :]).then_inc(gt_ready, 1)

                @block.vector
                def _(dve):
                    k = 0

                    def step(instruction):
                        nonlocal k
                        k += 1
                        instruction.then_inc(soft, 1)
                        dve.wait_ge(soft, k)

                    def wide(a, w=E):
                        return a.unsqueeze(2).to_broadcast([P, N16, w])

                    dve.wait_ge(logits, 1)
                    dve.wait_ge(filled, 2)
                    step(dve.tensor_tensor(lg[:, :, :], l_ps[:, 0:N16 * E].rearrange("p (n e) -> p n e", e=E),
                                           bg2[:, 0:E].unsqueeze(1).to_broadcast([P, N16, E]), ALU.add))
                    step(dve.tensor_reduce(mx[:, :], lg[:, :, :], AX.X, ALU.max))
                    step(dve.tensor_tensor(lg[:, :, :], lg[:, :, :], wide(mx[:, :]), ALU.subtract))
                    dve.wait_ge(exped, 1)
                    step(dve.tensor_reduce(sm[:, :], pb[:, :, 0:E], AX.X, ALU.add))
                    step(dve.reciprocal(sm[:, :], sm[:, :]))
                    step(dve.tensor_tensor(pb[:, :, 0:E], pb[:, :, 0:E], wide(sm[:, :]), ALU.mult))
                    for n in range(N16):
                        last = dve.max(top[:, n, :], pb[:, n, 0:E])
                    step(last)
                    step(dve.tensor_copy(drop[:, :, 0:TOPK], top[:, :, 0:TOPK]))
                    for n in range(N16):
                        dve.match_replace(out=gates[:, n, :], in_to_replace=drop[:, n, :], in_values=pb[:, n, :],
                                          imm_value=0.0).then_inc(topped, 1)
                    dve.wait_ge(topped, N16)
                    dve.tensor_tensor(gates[:, :, 0:E], pb[:, :, 0:E], gates[:, :, 0:E], ALU.subtract).then_inc(topped, 1)

        with ExitStack() as low:
            _, ps, sem = scope(nc, low)
            z_ps, o_ps = ps("ez" + nm, [P, E * P]), ps("eo" + nm, [P, 512])
            x_taken, z_done, y_done, turned, added = (sem(nm + x) for x in ("x_taken", "z_done", "y_done", "turned", "added"))
            start_at_one(nc, [added, y_done])
            with nc.Block() as block:
                def tiles(eng, body):
                    with eng.Fori(0, NT) as t:
                        for b in range(B):
                            body(b, t, t * B + b)

                @block.gpsimd
                def _(pool):
                    def body(b, t, n):
                        pool.wait_ge(added, n + 1)
                        settle(pool, c)
                        pool.tensor_copy(xt[b][:, :], c.xA[:, b, bass.ds(PAD + t * P, P)]).then_inc(x_taken, 1)
                    tiles(pool, body)

                @block.tensor
                def _(pe):
                    def body(b, t, n):
                        pe.wait_ge(x_taken, n + 1)
                        for i in range(5):
                            pe.wait_ge(y_done, n * E + 0 + 1)
                            pe.matmul(z_ps[:, i * 512:(i + 1) * 512], xt[b][:, :],
                                      We[:, 4 * i:4 * i + 4, :].rearrange("p e n -> p (e n)"), start=True, stop=True).then_inc(z_done, 1)
                        pe.wait_ge(y_done, (n + 1) * E + 1)
                        for i in range(2):
                            pe.matmul(o_ps[:, 0:P], y[b][i][:, :], c.ident[:, :], start=(i == 0), stop=False)
                        pe.matmul(o_ps[:, 0:P], be[:, :], gT[:, b, bass.ds(t * P, P)], start=False, stop=True).then_inc(turned, 1)
                    tiles(pe, body)

                @block.vector
                def _(dve):
                    def body(b, t, n):
                        for e in range(E):
                            if e % 4 == 0:
                                dve.wait_ge(z_done, 5 * n + e // 4 + 1)
                            gate = c.gates_now[:, e:e + 1]
                            z = z_ps[:, e * P:(e + 1) * P]
                            acc = y[b][e % 2][:, :]
                            if e == 0:
                                dve.tensor_copy(c.gates_now[:, :], gates[:, bass.ds(b * NT + t, 1), 0:E].rearrange("p n e -> p (n e)")).then_inc(c.gates_sem, 1)
                                dve.wait_ge(c.gates_sem, n + 1)
                            if e < 2:
                                dve.tensor_scalar(acc, z, gate, None, ALU.mult).then_inc(y_done, 1)
                            else:
                                dve.wait_ge(y_done, n * E + e - 1 + 1)
                                dve.scalar_tensor_tensor(out=acc, in0=z, scalar=gate, in1=acc, op0=ALU.mult, op1=ALU.add).then_inc(y_done, 1)
                        dve.wait_ge(turned, n + 1)
                        at = PAD + t * P
                        dve.scalar_tensor_tensor(out=c.X[:, b, bass.ds(at, P)], in0=o_ps[:, 0:P], scalar=0.5,
                                                 in1=c.X[:, b, bass.ds(at, P)], op0=ALU.mult, op1=ALU.add).then_inc(added, 1)
                    c.gates_now = ctx.enter_context(nc.sbuf_tensor("gates_now" + nm, [P, E], F32))
                    c.gates_sem = sem(nm + "gates_taken")
                    tiles(dve, body)


def full_attention_phase(nc, c):
    BAND = P // 4
    with ExitStack() as ctx:
        sb, ps, sem = scope(nc, ctx)
        w, ow, owT = sb("w_qkv", [P, 3 * P]), sb("ow", [P, P]), sb("owT", [P, P])
        xh, wh = sb("xh", [P, B, T], F16), sb("wh", [P, 3 * P], F16)
        qT, kT = sb("qT", [P, B, T]), sb("kT", [P, B, T])
        V = sb("V", [P, B * NT, P])
        qs = [sb(f"qs{b}", [P, P]) for b in range(B)]
        pr = [sb(f"apr{b}", [P, T]) for b in range(B)]
        pT = [sb(f"apT{b}", [P, T]) for b in range(B)]
        yT = [sb(f"ayT{b}", [P, P]) for b in range(B)]
        mx, sm = [sb(f"amx{b}", [P, 1]) for b in range(B)], [sb(f"asm{b}", [P, 1]) for b in range(B)]
        bank = ps("a_banks", [P, 8 * 512])
        part = lambda i, n=1: bank[:, i * 512:(i + n) * 512]
        w_in, rounded, made, evacuated, turned_w = sem("fa_w_in"), sem("fa_rounded"), sem("fa_made"), sem("fa_evacuated"), sem("fa_turned_w")
        with nc.Block() as block:
            @block.sync
            def _(sp):
                sp.dma_start(w[:, :], c.d["L1_attn_weight_qkv"]).then_inc(w_in, 16)
                sp.dma_start(ow[:, :], c.d["L1_attn_out_w"]).then_inc(w_in, 16)

            @block.vector
            def _(dve):
                xa = c.xA[:, :, PAD:PAD + T]
                dve.tensor_copy(xh[:, :, :], xa).then_inc(rounded, 1)
                dve.wait_ge(w_in, 32)
                dve.tensor_copy(wh[:, :], w[:, :]).then_inc(rounded, 1)
                dve.wait_ge(rounded, 2)
                for lo in (0, P - BAND):
                    rows = slice(lo, lo + BAND)
                    dve.tensor_copy(c.xA[rows, :, PAD:PAD + T], xh[rows, :, :]).then_inc(rounded, 1)
                    dve.tensor_copy(w[rows, :], wh[rows, :]).then_inc(rounded, 1)

            @block.tensor
            def _(pe):
                pe.wait_ge(rounded, 6)
                for what in range(2):
                    for g in range(4):
                        pe.matmul(part(4 * what + g), w[:, what * P:(what + 1) * P],
                                  c.xA[:, g // 2, PAD + (g % 2) * GT:PAD + (g % 2 + 1) * GT], start=True, stop=True).then_inc(made, 1)
                for n in range(B * NT):
                    if n % 4 == 0:
                        pe.wait_ge(evacuated, n // 4 + 1)
                    at = PAD + (n % NT) * P
                    last = pe.matmul(part(n // 4)[:, (n % 4) * P:(n % 4 + 1) * P], c.xA[:, n // NT, at:at + P], w[:, 2 * P:3 * P],
                                     start=True, stop=True)
                    if n % 4 == 3:
                        last.then_inc(made, 1)
                pe.wait_ge(evacuated, 8)
                pe.transpose(part(4)[:, 0:P], ow[:, :], c.ident[:, :]).then_inc(turned_w, 1)

            @block.scalar
            def _(act):
                for what in range(2):
                    for g in range(4):
                        act.wait_ge(made, 4 * what + g + 1)
                        act.activation((qT, kT)[what][:, g // 2, (g % 2) * GT:(g % 2 + 1) * GT], part(4 * what + g), ACT.Copy,
                                       scale=(float(P) ** -0.5, 1.0)[what]).then_inc(evacuated, 1)
                for g in range(4):
                    act.wait_ge(made, 8 + g + 1)
                    act.copy(V[:, 4 * g:4 * g + 4, :].rearrange("p n d -> p (n d)"), part(g)).then_inc(evacuated, 1)
                act.wait_ge(turned_w, 1)
                act.copy(owT[:, :], part(4)[:, 0:P]).then_inc(evacuated, 1)

        q_taken, scored, maxed, negated, exped = sem("fa_q_taken"), sem("fa_scored"), sem("fa_maxed"), sem("fa_negated"), sem("fa_exped")
        inverted, normed, p_turned, pt_ready = sem("fa_inverted"), sem("fa_normed"), sem("fa_p_turned"), sem("fa_pt_ready")
        y_done, y_ready, o_done, added = sem("fa_y_done"), sem("fa_y_ready"), sem("fa_o_done"), sem("fa_added")
        start_at_one(nc, [scored, exped, pt_ready, y_ready, added, p_turned, y_done])
        s_ps, t_ps, y_ps, o_ps = [part(0, 2), part(2, 2)], part(4, 2), part(6), part(7)
        with nc.Block() as block:
            def tiles(eng, body):
                with eng.Fori(0, NT) as t:
                    for b in range(B):
                        body(b, t, t * B + b)

            @block.gpsimd
            def _(pool):
                with pool.Fori(0, NT) as t:
                    for b in range(B):
                        n = t * B + b
                        pool.wait_ge(scored, t * B + 1)
                        settle(pool, c)
                        pool.tensor_copy(qs[b][:, :], qT[:, b, bass.ds(t * P, P)]).then_inc(q_taken, 1)

            @block.tensor
            def _(pe):
                def score(b, t, n):
                    pe.wait_ge(q_taken, n + 1)
                    pe.wait_ge(exped, t * B + 1)
                    for i in range(2):
                        last = pe.matmul(s_ps[b][:, i * 512:(i + 1) * 512], qs[b][:, :], kT[:, b, i * 512:(i + 1) * 512],
                                         start=True, stop=True)
                    last.then_inc(scored, 1)

                def rest(b, t, n):
                    pe.wait_ge(normed, n + 1)
                    pe.wait_ge(pt_ready, n + 1)
                    for k in range(NT):
                        last = pe.transpose(t_ps[:, k * P:(k + 1) * P], pr[b][:, k * P:(k + 1) * P], c.ident[:, :])
                    last.then_inc(p_turned, 1)
                    pe.wait_ge(pt_ready, n + 1 + 1)
                    pe.wait_ge(y_ready, n + 1)
                    for k in range(NT):
                        last = pe.matmul(y_ps[:, 0:P], V[:, b * NT + k, :], pT[b][:, k * P:(k + 1) * P], start=(k == 0), stop=(k == NT - 1))
                    last.then_inc(y_done, 1)
                    pe.wait_ge(y_ready, n + 1 + 1)
                    pe.wait_ge(added, n + 1)
                    pe.matmul(o_ps[:, 0:P], owT[:, :], yT[b][:, :], start=True, stop=True).then_inc(o_done, 1)

                with pe.Fori(0, NT) as t:
                    for b in range(B):
                        score(b, t, t * B + b)
                    for b in range(B):
                        rest(b, t, t * B + b)

            @block.vector
            def _(dve):
                with dve.Fori(0, NT) as t:
                    for b in range(B):
                        n = t * B + b
                        dve.wait_ge(scored, n + 1 + 1)
                        dve.tensor_reduce(mx[b][:, :], s_ps[b], AX.X, ALU.max).then_inc(maxed, 1)
                        dve.wait_ge(maxed, n + 1)
                        dve.tensor_scalar(mx[b][:, :], mx[b][:, :], -1.0, None, ALU.mult).then_inc(negated, 1)
                    for b in range(B):
                        n = t * B + b
                        dve.wait_ge(exped, n + 1 + 1)
                        dve.reciprocal(sm[b][:, :], sm[b][:, :]).then_inc(inverted, 1)
                        dve.wait_ge(inverted, n + 1)
                        dve.tensor_scalar(pr[b][:, :], pr[b][:, :], sm[b][:, 0:1], None, ALU.mult).then_inc(normed, 1)
                    for b in range(B):
                        n = t * B + b
                        dve.wait_ge(o_done, n + 1)
                        at = PAD + t * P
                        bias = c.cols[:, c.col["L1_attn_out_b"]:c.col["L1_attn_out_b"] + 1]
                        dve.scalar_tensor_tensor(out=c.X[:, b, bass.ds(at, P)], in0=o_ps[:, 0:P], scalar=bias,
                                                 in1=c.X[:, b, bass.ds(at, P)], op0=ALU.add, op1=ALU.add).then_inc(added, 1)

            @block.scalar
            def _(act):
                act.activation(c.scrap[:, :], c.ones[:, 0:1], ACT.Exp).then_inc(turned_w, 1)
                with act.Fori(0, NT) as t:
                    for b in range(B):
                        n = t * B + b
                        act.wait_ge(negated, n + 1)
                        act.wait_ge(p_turned, t * B + 1)
                        act.activation(pr[b][:, :], s_ps[b], ACT.Exp, bias=mx[b][:, 0:1], accum_out=sm[b][:, 0:1]).then_inc(exped, 1)
                    for b in range(B):
                        n = t * B + b
                        act.wait_ge(p_turned, n + 1 + 1)
                        act.wait_ge(y_done, t * B + 1)
                        act.copy(pT[b][:, :], t_ps).then_inc(pt_ready, 1)
                        act.wait_ge(y_done, n + 1 + 1)
                        act.copy(yT[b][:, :], y_ps[:, 0:P]).then_inc(y_ready, 1)


def output_phase(nc, c, src, out):
    with ExitStack() as ctx:
        sb, ps, sem = scope(nc, ctx)
        turned = [ps(f"o_turned{i}", [P, 4, P]) for i in range(4)]
        ot = sb("ot", [P, B * NT, P])
        o_turned, o_copied, stored = sem("o_turned"), sem("o_copied"), sem("stored")
        with nc.Block() as block:
            @block.tensor
            def _(pe):
                for g in range(4):
                    for j in range(4):
                        b, t = g // 2, (g % 2) * 4 + j
                        last = pe.transpose(turned[g][:, j, :], src[:, b, PAD + t * P:PAD + (t + 1) * P], c.ident[:, :])
                    last.then_inc(o_turned, 1)

            @block.vector
            def _(dve):
                for g in range(4):
                    dve.wait_ge(o_turned, g + 1)
                    dve.tensor_copy(ot[:, 4 * g:4 * g + 4, :], turned[g][:, :, :]).then_inc(o_copied, 1)

            @block.sync
            def _(sp):
                for g in range(4):
                    b, t = g // 2, (g % 2) * 4
                    sp.wait_ge(o_copied, g + 1)
                    sp.dma_start(out[b, t * P:(t + 4) * P, :].rearrange("(t p) f -> p t f", p=P),
                                 ot[:, 4 * g:4 * g + 4, :]).then_inc(stored, 16)
                sp.wait_ge(stored, 16 * 4)


def program(nc, names, *aps):
    d = dict(zip(names, aps))
    out = aps[-1]
    with ExitStack() as ctx:
        sb, ps, sem = scope(nc, ctx)
        c = Chip()
        c.d, c.sems = d, {}
        c.settled = sem("settled")
        stage = 5
        c.depth = DEPTH
        c.X, c.xA, c.xB = (sb(x, [P, B, PAD + T + CH]) for x in ("X", "xA", "xB"))
        c.ident, c.identb = sb("ident", [P, P]), sb("identb", [P, P], BF16)
        c.ones, c.scrap = sb("ones", [P, P]), sb("scrap", [P, 1])
        c.cols = sb("cols", [P, P])
        with ExitStack() as ctx2:
            sb, ps, sem = scope(nc, ctx2)
            c.mask = sb("mask", [P, NT, KEYS], BF16)
            c.rope = sb("rope", [P, 4, NT, DH])
            c.qks = sb("qks", [P, 4, DEPTH * DH])
            c.Wqkv, c.Wo = sb("Wqkv", [P, 3 * INNER]), sb("Wo", [P, PAIRS, P])
            c.W1, c.W2 = sb("W1", [P, 2 * FF]), sb("W2", [P, 3, P])
            c.KT = [sb(f"KT{b}", [P, PAIRS, WIN + P]) for b in range(B)]
            load_phase(nc, c, d)
            transformer(nc, c, "a")
            if stage >= 1:
                norm_phase(nc, c, "rn", c.X, c.xA)
                recurrence_phase(nc, c)
                norm_phase(nc, c, "ry", c.xB, c.xA, affine=("L0_attn_gamma", "L0_attn_beta"))
                residual_phase(nc, c, "rres", 1.0)
            if stage >= 2:
                transformer(nc, c, "b")
        if stage >= 3:
            norm_phase(nc, c, "norm_e", c.X, c.xA)
            experts_phase(nc, c, "moe1")
        if stage >= 4:
            norm_phase(nc, c, "norm_f", c.X, c.xA)
            full_attention_phase(nc, c)
        if stage >= 5:
            norm_phase(nc, c, "norm_h", c.X, c.xA)
            experts_phase(nc, c, "moe2")
        output_phase(nc, c, c.X, out)


_INS = ['L0_attn_x', 'L0_attn_Wi', 'L0_attn_bi', 'L0_attn_Wf', 'L0_attn_bf', 'L0_attn_Wg', 'L0_attn_bg', 'L0_attn_Wo',
        'L0_attn_bo', 'L0_attn_Weg', 'L0_attn_beg', 'L0_attn_gamma', 'L0_attn_beta', 'L0_ffn_Wqkv', 'L0_ffn_q_scale',
        'L0_ffn_k_scale', 'L0_ffn_Wo', 'L0_ffn_ln_g', 'L0_ffn_ln_b', 'L0_ffn_W1', 'L0_ffn_b1', 'L0_ffn_W2', 'L0_ffn_b2',
        'L1_attn_weight_qkv', 'L1_attn_out_w', 'L1_attn_out_b', 'L1_ffn_wg1', 'L1_ffn_bg1', 'L1_ffn_wg2', 'L1_ffn_bg2',
        'L1_ffn_We', 'L1_ffn_be']


def kernel(**inputs):
    import concourse.bacc as _bacc
    from concourse.bass_utils import run_bass_kernel_spmd as _run

    nc = _bacc.Bacc("TRN2", target_bir_lowering=False, num_devices=1)
    arrays = {name: np.ascontiguousarray(inputs[name]) for name in _INS}
    arrays["rope"] = rope_tables()
    arrays["mask"] = band_mask()
    args = [nc.dram_tensor(f"in_{k}", a.shape, mybir.dt.from_np(a.dtype), kind="ExternalInput").ap() for k, a in arrays.items()]
    args.append(nc.dram_tensor("out", (B, T, P), F32, kind="ExternalOutput").ap())
    program(nc, list(arrays), *args)
    r = _run(nc, [{f"in_{k}": a for k, a in arrays.items()}], core_ids=[0])
    return r.results[0]["out"]
```

```python
from contextlib import ExitStack

import numpy as np

import concourse.bass as bass
from concourse import mybir

F32 = mybir.dt.float32
F16 = mybir.dt.float16
BF16 = mybir.dt.bfloat16
I32 = mybir.dt.int32
ALU = mybir.AluOpType
ACT = mybir.ActivationFunctionType
AX = mybir.AxisListType

P = 128
B, T = 2, 1024
NT = T // P
DEPTH, HEADS, DH, WIN = 6, 16, 64, 32
PAIRS = HEADS // 2
HALF = PAIRS // 2
NW = P // WIN
KEYS = 2 * WIN
INNER = HEADS * DH
FF = int(P * 4 * 2 / 3)
FFC = [(0, 128), (128, 128), (256, FF - 256)]
PAD = WIN + 1
GT = 512
NG = T // GT
QK_SCALE = 8.0
RSQRT_SEED = 1597463007.0
NEWTON = 12
NEG = -1e30
LV = 9
CH = 16
ROUND = 8 * CH

EXPERTS, TOPK, GH = 20, 2, 32


def rope_tables():
    half = np.arange(0, DH, 2, dtype=np.float32)
    inv_freq = (np.float32(1.0) / np.float32(10000.0) ** (half / np.float32(DH))).astype(np.float32)
    t = np.arange(T, dtype=np.float32)
    freqs = t[:, None] * inv_freq[None, :]
    freqs = np.concatenate([freqs, freqs], -1)
    base = ((half + np.float32(0.4 * DH)) / np.float32(1.4 * DH)).astype(np.float32)
    power = ((t - T // 2) / np.float32(WIN // 2)).astype(np.float32)
    scale = (base[None, :] ** power[:, None]).astype(np.float32)
    scale = np.concatenate([scale, scale], -1)
    sign = np.where(np.arange(DH) < DH // 2, -1, 1).astype(np.float32)
    cos, sin = np.cos(freqs), np.sin(freqs) * sign
    inv = (np.float32(1.0) / scale).astype(np.float32)
    four = np.stack([cos * scale * np.float32(QK_SCALE), sin * scale * np.float32(QK_SCALE), cos * inv, sin * inv])
    return np.ascontiguousarray(four.reshape(4, NT, P, DH).transpose(2, 0, 1, 3)).astype(np.float32)


def band_mask():
    i = (np.arange(P) % WIN)[:, None, None]
    j = np.arange(KEYS)[None, None, :]
    seen = np.broadcast_to((j >= i) & (j <= i + WIN), (P, NT, KEYS)).copy()
    seen[:WIN, 0, :WIN] = False
    return np.where(seen, 0.0, NEG).astype(np.float32)


def rsqrt_steps(dve, done, at, v, y, t, least, add, between={}):
    k = 0

    def step(instruction):
        nonlocal k
        k += 1
        instruction.then_inc(done, 1)
        if k in between:
            between[k]()
        dve.wait_ge(done, at + k)

    step(dve.tensor_scalar(v, v, add, least, ALU.add, ALU.max))
    step(dve.tensor_scalar(y.bitcast(I32), v.bitcast(I32), 1, None, ALU.logical_shift_right))
    step(dve.tensor_scalar(y.bitcast(I32), y.bitcast(I32), -1.0, RSQRT_SEED, ALU.mult, ALU.add))
    for _ in range(3):
        step(dve.tensor_tensor(t, y, y, ALU.mult))
        step(dve.scalar_tensor_tensor(out=t, in0=t, scalar=-0.5, in1=v, op0=ALU.mult, op1=ALU.mult))
        step(dve.scalar_tensor_tensor(out=y, in0=t, scalar=1.5, in1=y, op0=ALU.add, op1=ALU.mult))
    assert k == NEWTON


def is_zero(t):
    return isinstance(t, int) and t == 0


def settle(eng, c):
    eng.sem_inc(c.settled, 1)


def start_at_one(nc, sems):
    with nc.Block() as block:
        @block.sync
        def _(sp):
            for sem in sems:
                sp.sem_inc(sem, 1)


class Chip:
    pass


def scope(nc, ctx):
    def sb(name, shape, dt=F32):
        return ctx.enter_context(nc.sbuf_tensor(name, shape, dt))

    def ps(name, shape, dt=F32):
        return ctx.enter_context(nc.psum_tensor(name, shape, dt))

    held = []

    def sem(name):
        if not held:
            ctx.callback(give_back)
        held.append(nc.alloc_semaphore(name=name))
        return held[-1]

    def give_back():
        nc.clear_and_free_semaphores(held)
        nc.all_engine_barrier()

    return sb, ps, sem


def load_phase(nc, c, d):
    with ExitStack() as ctx:
        sb, ps, sem = scope(nc, ctx)
        xt = sb("xt", [P, B * NT, P])
        rows = sb("rows", [P, P])
        maskf = sb("maskf", [P, NT, KEYS])
        turned = [ps(f"ld_turned{i}", [P, 4, P]) for i in range(4)]
        turned_rows = ps("ld_turned_rows", [P, P])
        x_in, cleared, rows_in, mask_in, rest_in = sem("x_in"), sem("cleared"), sem("rows_in"), sem("mask_in"), sem("rest_in")
        ident_done, x_turned, rows_turned, copied, swapped = (
            sem("ident_done"), sem("x_turned"), sem("rows_turned"), sem("copied"), sem("swapped"))
        single = ["L0_attn_bi", "L0_attn_bf", "L0_attn_bo", "L0_attn_bg", "L0_attn_beg", "L0_attn_gamma", "L0_attn_beta", "L1_attn_out_b"]
        c.col = {name: DEPTH * LV + i for i, name in enumerate(single)}

        with nc.Block() as block:
            @block.gpsimd
            def _(pool):
                pool.memset(c.ident[:, :], 0.0).then_inc(ident_done, 1)
                pool.memset(rows[:, :], 0.0).then_inc(cleared, 1)
                pool.wait_ge(ident_done, 1)
                pool.affine_select(out=c.ident[:, :], in_=c.ident[:, :], compare_op=ALU.not_equal, fill=1.0,
                                   base=0, pattern=[[-1, P]], channel_multiplier=1).then_inc(ident_done, 1)
                pool.wait_ge(ident_done, 2)
                settle(pool, c)
                pool.tensor_copy(c.identb[:, :], c.ident[:, :]).then_inc(copied, 1)
                pool.memset(c.xA[:, :, 0:PAD], 0.0).then_inc(cleared, 1)
                pool.memset(c.xB[:, :, 0:PAD], 0.0).then_inc(cleared, 1)
                pool.memset(c.xA[:, :, PAD + T:], 0.0).then_inc(cleared, 1)
                pool.memset(c.ones[:, :], 1.0).then_inc(cleared, 1)

            @block.sync
            def _(sp):
                for b in range(B):
                    sp.dma_start(xt[:, b * NT:(b + 1) * NT, :],
                                 d["L0_attn_x"][b].rearrange("(t p) f -> p t f", p=P)).then_inc(x_in, 16)
                sp.dma_start(maskf[:, :, :], d["mask"]).then_inc(mask_in, 16)
                sp.dma_start(c.rope[:, :, :, :], d["rope"]).then_inc(rest_in, 16)
                sp.dma_start(c.Wqkv[:, :], d["L0_ffn_Wqkv"][0]).then_inc(rest_in, 16)
                sp.dma_start(c.Wo[:, :, :], d["L0_ffn_Wo"][0].rearrange("(j p) n -> p j n", p=P)).then_inc(rest_in, 16)
                sp.wait_ge(rest_in, 16 * 5)

            @block.scalar
            def _(act):
                act.wait_ge(cleared, 1)
                with nc.allow_non_contiguous_dma(reason="short vectors"):
                    layered = [("L0_ffn_ln_g", 0, 0, P), ("L0_ffn_ln_b", 1, 0, P), ("L0_ffn_b2", 2, 0, P)]
                    layered += [("L0_ffn_b1", 3 + i, s, w) for i, (s, w) in enumerate(FFC)]
                    layered += [("L0_ffn_b1", 6 + i, FF + s, w) for i, (s, w) in enumerate(FFC)]
                    for name, row, s, w in layered:
                        act.dma_start(rows[row:DEPTH * LV:LV, 0:w], d[name][:, s:s + w]).then_inc(rows_in, 16)
                    for name in single:
                        act.dma_start(rows[c.col[name]:c.col[name] + 1, :],
                                      d[name].rearrange("(a f) -> a f", a=1)).then_inc(rows_in, 16)
                    act.dma_start(c.qks[:, 0, :], d["L0_ffn_q_scale"].rearrange("l f -> (l f)").partition_broadcast(P)).then_inc(rest_in, 16)
                    act.dma_start(c.qks[:, 1, :], d["L0_ffn_k_scale"].rearrange("l f -> (l f)").partition_broadcast(P)).then_inc(rest_in, 16)
                act.wait_ge(mask_in, 16)
                act.copy(c.mask[:, :, :], maskf[:, :, :]).then_inc(copied, 1)
                act.wait_ge(x_turned, 4)
                for g in range(4):
                    b, t = g // 2, (g % 2) * 4
                    act.copy(c.X[:, b, PAD + t * P:PAD + (t + 4) * P], turned[g][:, :, :].rearrange("f t p -> f (t p)")).then_inc(copied, 1)
                act.wait_ge(rows_turned, 1)
                act.copy(c.cols[:, :], turned_rows[:, :]).then_inc(copied, 1)

            @block.vector
            def _(dve):
                dve.wait_ge(rest_in, 16 * 5)
                for i in range(2):
                    halves = [c.qks[:, j, :].rearrange("p (l a d) -> p l a d", a=2, d=DH // 2) for j in (i, 2 + i)]
                    for a in range(2):
                        dve.tensor_copy(halves[1][:, :, a, :], halves[0][:, :, 1 - a, :]).then_inc(swapped, 1)

            @block.tensor
            def _(pe):
                pe.wait_ge(ident_done, 2)
                pe.wait_ge(x_in, 16 * B)
                for g in range(4):
                    for j in range(4):
                        last = pe.transpose(turned[g][:, j, :], xt[:, g * 4 + j, :], c.ident[:, :])
                    last.then_inc(x_turned, 1)
                pe.wait_ge(rows_in, 16 * (9 + len(single)))
                pe.transpose(turned_rows[:, :], rows[:, :], c.ident[:, :]).then_inc(rows_turned, 1)


def norm_phase(nc, c, name, src, dst, affine=None):
    NGR = B * NG
    with ExitStack() as ctx:
        sb, ps, sem = scope(nc, ctx)
        stats = sb(name + "stats", [P, NGR, 4, 6])
        mv = sb(name + "mv", [P, NGR, 4, 2])
        var = sb(name + "var", [P, NGR * 4])
        rstd = sb(name + "rstd", [P, NGR * 4])
        tmp = sb(name + "tmp", [P, NGR * 4])
        xn = sb(name + "xn", [P, NGR, 4, P])
        tok = [ps(f"{name}tok{g}", [P, 4, P]) for g in range(NGR)]
        back = [ps(f"{name}back{g}", [P, 4 * P]) for g in range(NGR)]
        tok_ready, stat, aggr, var_ready, newton = sem(name + "tok_ready"), sem(name + "stat"), sem(name + "aggr"), sem(name + "var_ready"), sem(name + "newton")
        xn_ready, back_ready, out_done = sem(name + "xn_ready"), sem(name + "back_ready"), sem(name + "out_done")
        place = [(g // NG, PAD + (g % NG) * GT) for g in range(NGR)]

        with nc.Block() as block:
            @block.tensor
            def _(pe):
                for g, (b, s) in enumerate(place):
                    for j in range(4):
                        last = pe.transpose(tok[g][:, j, :], src[:, b, s + j * P:s + (j + 1) * P], c.ident[:, :])
                    last.then_inc(tok_ready, 1)
                for g in range(NGR):
                    pe.wait_ge(xn_ready, 4 * (g + 1))
                    for j in range(4):
                        last = pe.transpose(back[g][:, j * P:(j + 1) * P], xn[:, g, j, :], c.ident[:, :])
                    last.then_inc(back_ready, 1)

            @block.vector
            def _(dve):
                for g in range(NGR):
                    dve.wait_ge(tok_ready, g + 1)
                    for j in range(4):
                        dve.bn_stats(stats[:, g, j, :], tok[g][:, j, :]).then_inc(stat, 1)
                for g in range(NGR):
                    dve.wait_ge(stat, 4 * (g + 1))
                    for j in range(4):
                        dve.bn_aggr(mv[:, g, j, :], stats[:, g, j, :]).then_inc(aggr, 1)
                dve.wait_ge(aggr, 4 * NGR)
                dve.tensor_copy(var[:, :], mv[:, :, :, 1].rearrange("p g j -> p (g j)")).then_inc(var_ready, 1)
                dve.wait_ge(var_ready, 1)
                rsqrt_steps(dve, newton, 0, var[:, :], rstd[:, :], tmp[:, :], 0.0, 1e-5)
                for g in range(NGR):
                    for j in range(4):
                        dve.tensor_scalar(xn[:, g, j, :], tok[g][:, j, :], mv[:, g, j, 0:1],
                                          rstd[:, g * 4 + j:g * 4 + j + 1], ALU.subtract, ALU.mult).then_inc(xn_ready, 1)

            @block.scalar
            def _(act):
                for g, (b, s) in enumerate(place):
                    act.wait_ge(back_ready, g + 1)
                    if affine:
                        gain, offset = (c.cols[:, c.col[x]:c.col[x] + 1] for x in affine)
                        act.activation(dst[:, b, s:s + GT], back[g][:, :], ACT.Identity, bias=offset, scale=gain).then_inc(out_done, 1)
                    else:
                        act.copy(dst[:, b, s:s + GT], back[g][:, :]).then_inc(out_done, 1)


def layer_phase(nc, c, layer, nm):
    s = c.sems[nm]
    base = layer * (B * NT)
    f = FeedForward(c, s, layer)
    qk, vo, sc = c.qk_ps, c.vo_ps, c.sc_ps
    t1, t2, sq, pr = c.t1, c.t2, c.sq, c.probs

    def run(eng, stages, before_last=lambda: None):
        def emit(*tiles):
            stages(*(None if x is None else (x[0], x[1], base + 2 * x[1] + x[0], not is_zero(x[1])) for x in tiles))
        emit((0, 0), None, None, None)
        emit((1, 0), (0, 0), None, None)
        emit((0, 1), (1, 0), (0, 0), None)
        emit((1, 1), (0, 1), (1, 0), (0, 0))
        with eng.Fori(2, NT) as t:
            emit((0, t), (1, t - 1), (0, t - 1), (1, t - 2))
            emit((1, t), (0, t), (1, t - 1), (0, t - 1))
        emit(None, (1, NT - 1), (0, NT - 1), (1, NT - 2))
        before_last()
        emit(None, None, (1, NT - 1), (0, NT - 1))
        emit(None, None, None, (1, NT - 1))

    def qview(psum):
        return psum.rearrange("p (h d) -> p h d", d=DH)

    def swapped(psum):
        return psum.rearrange("p (h a d) -> p h a d", a=2, d=DH // 2)[:, :, ::-1, :]

    def quarter(i, half):
        return slice(i * INNER + half * 512, i * INNER + (half + 1) * 512)

    with nc.Block() as block:
        @block.gpsimd
        def _(pool):
            def shifted(dst, src, b, at, width, ready, count):
                pool.tensor_copy(dst[0:64, :], src[0:64, b, bass.ds(at, width)]).then_inc(ready, 1)
                pool.wait_ge(ready, count + 1)
                settle(pool, c)
                pool.tensor_copy(dst[64:P, :], src[64:P, b, bass.ds(at - 1, width)]).then_inc(ready, 1)
                pool.wait_ge(ready, count + 2)
                settle(pool, c)

            def stages(project, turn, attend, finish):
                if project:
                    b, t, n, later = project
                    if later:
                        pool.wait_ge(s.qk_done, 2 * (n - 1))
                        settle(pool, c)
                    shifted(c.xq[b], c.xA, b, PAD + t * P, P, s.xq_ready, 2 * n)
                    if not later:
                        pool.memset(c.KT[b][:, :, 0:WIN], 0.0).then_inc(s.k_moved, 1)
                if turn:
                    b, t, n, later = turn
                    for i in range(2):
                        pool.wait_ge(s.t_ready, 4 * n + 2 * i + 2)
                        part = slice(i * INNER, (i + 1) * INNER)
                        pool.tensor_tensor(t1[:, part], t1[:, part], t2[:, part], ALU.add).then_inc(s.rot_sum, 1)
                    pool.wait_ge(s.newton, NEWTON * (n + 1))
                    for i in range(2):
                        pool.wait_ge(s.rot_sum, 2 * n + i + 1)
                        part = slice(i * INNER, (i + 1) * INNER)
                        pool.tensor_tensor(qview(t1[:, part]), qview(t1[:, part]),
                                           c.rnorm[:, i * HEADS:(i + 1) * HEADS].unsqueeze(2).to_broadcast([P, HEADS, DH]),
                                           ALU.mult).then_inc(s.scaled, 1)
                    if later:
                        pool.wait_ge(s.v_done, 4 * (n - 1))
                        settle(pool, c)
                    shifted(c.xs[b], c.xA, b, PAD - WIN + t * P, WIN + P, s.xs_ready, 2 * n)
                if finish:
                    b, t, n, later = finish
                    pool.wait_ge(s.x_done, n + 1)
                    settle(pool, c)
                    shifted(c.fxs[:, b, bass.ds(t * P, P)], c.xB, b, PAD + t * P, P, s.fxs_ready, 2 * n)
            run(pool, stages)

        @block.tensor
        def _(pe):
            def stages(project, turn, attend, finish):
                def values_by(half):
                    for w in range(NW):
                        for k in range(half * HALF, (half + 1) * HALF):
                            for par in range(2):
                                rows = slice(64 * par, 64 * par + 64)
                                last = pe.matmul(vo[WIN * w:WIN * w + WIN, par * 512 + k * DH:par * 512 + (k + 1) * DH],
                                                 c.PT[rows, k * P + WIN * w:k * P + WIN * w + WIN],
                                                 c.Vw[rows, w, k * DH:(k + 1) * DH], start=True, stop=True)
                    return last

                def turn_part(i, n):
                    pe.wait_ge(s.scaled, 2 * n + i + 1)
                    for half in range(2):
                        if i == 1:
                            pe.wait_ge(s.kq_ready, 4 * n + half + 1)
                        for k in range(HALF):
                            src = t1[:, quarter(i, half)]
                            last = pe.transpose(sc[:, half * 512 + k * P:half * 512 + (k + 1) * P], src[:, k * P:(k + 1) * P], c.ident[:, :])
                        last.then_inc(s.kq_turned, 1)

                if attend:
                    b, t, n, later = attend
                    pe.wait_ge(s.kq_ready, 4 * n + 4)
                    for h in range(2):
                        pe.matmul(sc[:, h * 512:(h + 1) * 512], c.identb[:, :],
                                  c.mask[:, t, :].unsqueeze(1).to_broadcast([P, 8, KEYS]), start=True, stop=False,
                                  skip_group_check=True)
                    for w in range(NW):
                        for pair in range(PAIRS):
                            for par in range(2):
                                col = par * 512 + pair * KEYS
                                rows = slice(64 * par, 64 * par + 64)
                                last = pe.matmul(sc[WIN * w:WIN * w + WIN, col:col + KEYS],
                                                 c.QT[rows, pair, WIN * w:WIN * w + WIN],
                                                 c.KT[b][rows, pair, WIN * w:WIN * w + KEYS],
                                                 start=False, stop=True, skip_group_check=True)
                    last.then_inc(s.scored, 1)
                if finish:
                    n = finish[2]
                    pe.wait_ge(s.o_normed, n + 1)
                    for k in range(PAIRS):
                        last = pe.transpose(vo[:, k * P:(k + 1) * P], c.On[:, 2 * k:2 * k + 2, :].rearrange("p a d -> p (a d)"),
                                            c.ident[:, :])
                    last.then_inc(s.o_turned, 1)
                    if not attend:
                        f.turn_back(pe, 1)
                if project:
                    b, t, n, later = project
                    pe.wait_ge(s.xq_ready, 2 * n + 2)
                    if later or b:
                        pe.wait_ge(s.t_ready, 4 * n)
                    for i in range(4):
                        last = pe.matmul(qk[:, i * 512:(i + 1) * 512], c.xq[b][:, :], c.Wqkv[:, i * 512:(i + 1) * 512],
                                         start=True, stop=True)
                        if i % 2:
                            last.then_inc(s.qk_done, 1)
                if finish:
                    n = finish[2]
                    pe.wait_ge(s.o_ready, n + 1)
                    for k in range(PAIRS):
                        last = pe.matmul(vo[:, 0:P], c.Wo[:, k, :], c.OT[:, k * P:(k + 1) * P],
                                         start=(k == 0), stop=(k == PAIRS - 1))
                    last.then_inc(s.wo_done, 1)
                if attend:
                    b, t, n, later = attend
                    pe.wait_ge(s.xs_ready, 2 * n + 2)
                    for w in range(NW):
                        if w == 1 and finish:
                            pe.wait_ge(s.x_done, n)
                        if w >= 2:
                            pe.wait_ge(s.v_ready, 4 * n + w - 1)
                        bank = (w + 1) % 2
                        for par in range(2):
                            last = pe.matmul(vo[64 * par:64 * par + 64, bank * 512:(bank + 1) * 512],
                                             c.xs[b][:, WIN * w:WIN * w + KEYS],
                                             c.Wqkv[:, 2 * INNER:3 * INNER].rearrange("p (k a d) -> p a k d", a=2, d=DH)[:, par],
                                             start=True, stop=True)
                        last.then_inc(s.v_done, 1)
                        if w == 1:
                            pe.wait_ge(s.exp_done, n + 1)
                        if 1 <= w < NW - 1:
                            for k in range((w - 1) * HALF, w * HALF):
                                last = pe.transpose(sc[:, k * P:(k + 1) * P], pr[:, 2 * k:2 * k + 2, :].rearrange("p a j -> p (a j)"),
                                                    c.ident[:, :])
                            last.then_inc(s.p_turned, 1)
                    if not turn:
                        f.turn_back(pe, 0)
                if turn:
                    if attend:
                        pe.wait_ge(s.pt_ready, 2 * attend[2] + 2)
                    turn_part(0, turn[2])
                if attend:
                    pe.wait_ge(s.v_ready, 4 * n + 4)
                    pe.wait_ge(s.pt_ready, 2 * n + 2)
                    settle(pe, c)
                    values_by(0)
                if turn:
                    turn_part(1, turn[2])
                if attend:
                    values_by(1).then_inc(s.pv_done, 1)
                    if not turn:
                        pe.wait_ge(s.w_in, 16 * 3 * (layer + 1))
                        pe.wait_ge(s.f_xnT, f.group0 + 1)
                        f.expand(pe, 0, 0)
            run(pe, stages, lambda: f.turn_rows(pe, (0, 1)))
            f.tensor(pe)

        @block.vector
        def _(dve):
            def cosine(i, t, n):
                part = slice(i * INNER, (i + 1) * INNER)
                dve.tensor_tensor(qview(t1[:, part]), qview(qk[:, part]),
                                  c.rl[:, 2 * i, bass.ds(t * DH, DH)].unsqueeze(1).to_broadcast([P, HEADS, DH]),
                                  ALU.mult).then_inc(s.t_ready, 1)

            def sine(i, t, n):
                part = slice(i * INNER, (i + 1) * INNER)
                table = c.rl[:, 2 * i + 1, bass.ds(t * DH, DH)].rearrange("p (a d) -> p a d", a=2)
                dve.tensor_tensor(t2[:, part].rearrange("p (h a d) -> p h a d", a=2, d=DH // 2), swapped(qk[:, part]),
                                  table.unsqueeze(1).to_broadcast([P, HEADS, 2, DH // 2]),
                                  ALU.mult).then_inc(s.t_ready, 1)

            def residual(tile):
                if tile:
                    b, t, n, _ = tile
                    dve.wait_ge(s.wo_done, n + 1)
                    dve.tensor_tensor(c.xB[:, b, bass.ds(PAD + t * P, P)], vo[:, 0:P],
                                      c.xA[:, b, bass.ds(PAD + t * P, P)], ALU.add).then_inc(s.x_done, 1)

            def stages(project, turn, attend, finish):
                if attend:
                    b, _, n, later = attend
                    dve.wait_ge(s.scored, n + 1)
                    dve.tensor_reduce(c.mx[:, :], sc.rearrange("p (h j) -> p h j", j=KEYS), AX.X, ALU.max).then_inc(s.max_done, 1)
                    if later or b:
                        dve.wait_ge(s.p_turned, 2 * n)
                    dve.wait_ge(s.max_done, n + 1)
                    dve.tensor_tensor(pr[:, :, :].rearrange("p (k a) j -> p a k j", a=2),
                                      sc.rearrange("p (a k j) -> p a k j", a=2, j=KEYS),
                                      c.mx[:, :].rearrange("p (a k) -> p a k", a=2).unsqueeze(3).to_broadcast([P, 2, PAIRS, KEYS]),
                                      ALU.subtract).then_inc(s.centred, 1)
                first = project and not turn
                if project:
                    n = project[2]
                    for i in range(2):
                        dve.wait_ge(s.sq_done, 2 * n + i + 1)
                        if first and i == 0:
                            cosine(0, project[1], n)
                            sine(0, project[1], n)
                        dve.tensor_reduce(c.ssq[:, i * HEADS:(i + 1) * HEADS], qview(sq[:, i * INNER:(i + 1) * INNER]),
                                          AX.X, ALU.add).then_inc(s.ssq_done, 1)
                        if i == 0:
                            residual(finish)

                if not project:
                    residual(finish)

                def row_sums():
                    if attend:
                        n = attend[2]
                        dve.wait_ge(s.exp_done, n + 1)
                        dve.tensor_reduce(c.rsum[:, :], pr[:, :, :], AX.X, ALU.add).then_inc(s.inverted, 1)
                if project:
                    b, t, n, later = project
                    dve.wait_ge(s.ssq_done, 2 * n + 2)
                    if later or b:
                        dve.wait_ge(s.scaled, 2 * n)
                    rsqrt_steps(dve, s.newton, n * NEWTON, c.ssq[:, :], c.rnorm[:, :], c.ntmp[:, :], 1e-24, 0.0,
                                {1: lambda: cosine(1, t, n), 2: lambda: sine(1, t, n)} if first else {1: row_sums})
                    if not first:
                        dve.wait_ge(s.kq_turned, 4 * n - 2)
                        cosine(0, t, n)
                        sine(0, t, n)
                        dve.wait_ge(s.kq_turned, 4 * n)
                        cosine(1, t, n)
                else:
                    row_sums()
                if attend:
                    n = attend[2]
                    dve.wait_ge(s.inverted, 2 * n + 1)
                    dve.reciprocal(c.rsum[:, :], c.rsum[:, :]).then_inc(s.inverted, 1)
                    if not turn:
                        f.normalise(dve, 0)
                        f.normalise(dve, 1)
                    dve.wait_ge(s.inverted, 2 * n + 2)
                    dve.wait_ge(s.pv_done, n + 1)
                    dve.tensor_tensor(c.On[:, :, :].rearrange("p (k a) d -> p a k d", a=2),
                                      vo.rearrange("p (a k d) -> p a k d", a=2, d=DH),
                                      c.rsum[:, :].rearrange("p (k a) -> p a k", a=2).unsqueeze(3).to_broadcast([P, 2, PAIRS, DH]),
                                      ALU.mult).then_inc(s.o_normed, 1)
                if project and not first:
                    sine(1, project[1], project[2])
            for i in range(2):
                scale = c.qks[:, i, bass.ds(layer * DH, DH)]
                dve.tensor_tensor(c.rl[:, 2 * i, :].rearrange("p (t d) -> p t d", d=DH), c.rope[:, 2 * i, :, :],
                                  scale.unsqueeze(1).to_broadcast([P, NT, DH]), ALU.mult).then_inc(s.table, 1)
                other = c.qks[:, 2 + i, bass.ds(layer * DH, DH)]
                dve.tensor_tensor(c.rl[:, 2 * i + 1, :].rearrange("p (t d) -> p t d", d=DH), c.rope[:, 2 * i + 1, :, :],
                                  other.unsqueeze(1).to_broadcast([P, NT, DH]), ALU.mult).then_inc(s.table, 1)
            dve.tensor_copy(c.lcols[:, :], c.cols[:, bass.ds(layer * LV, LV)]).then_inc(s.f_cols, 1)
            dve.wait_ge(s.table, 4 * (layer + 1))
            settle(dve, c)
            dve.wait_ge(s.f_cols, layer + 1)
            settle(dve, c)
            run(dve, stages, lambda: f.statistics(dve, (0, 1)))
            f.vector(dve)

        @block.scalar
        def _(act):
            def stages(project, turn, attend, finish):
                if finish:
                    b, t, n, later = finish
                    act.wait_ge(s.o_turned, n + 1)
                    if later or b:
                        act.wait_ge(s.wo_done, n)
                    act.copy(c.OT[:, :], vo).then_inc(s.o_ready, 1)
                if attend:
                    n = attend[2]
                    act.wait_ge(s.centred, n + 1)
                    act.activation(pr[:, :, :], pr[:, :, :], ACT.Exp).then_inc(s.exp_done, 1)
                if project:
                    b, t, n, later = project
                    for i in range(2):
                        act.wait_ge(s.qk_done, 2 * n + i + 1)
                        if later or b:
                            act.wait_ge(s.ssq_done, 2 * n)
                        act.activation(sq[:, i * INNER:(i + 1) * INNER], qk[:, i * INNER:(i + 1) * INNER],
                                       ACT.Square).then_inc(s.sq_done, 1)
                if attend:
                    b, t, n, later = attend
                    for w in range(NW):
                        act.wait_ge(s.v_done, 4 * n + w + 1)
                        if later or b:
                            act.wait_ge(s.pv_done, n)
                        bank = (w + 1) % 2
                        act.copy(c.Vw[:, w, :], vo[:, bank * 512:(bank + 1) * 512]).then_inc(s.v_ready, 1)
                        if 1 <= w < NW - 1:
                            half = w - 1
                            act.wait_ge(s.p_turned, 2 * n + half + 1)
                            act.copy(c.PT[:, half * 512:(half + 1) * 512], sc[:, half * 512:(half + 1) * 512]).then_inc(s.pt_ready, 1)
                    if not turn:
                        act.activation(c.scrap[:, :], c.ones[:, 0:1], ACT.Gelu).then_inc(s.f_load, 1)
                        act.wait_ge(s.f_cols, layer + 1)
                        f.scale(act, 0)
                if turn:
                    b, t, n, later = turn
                    if later or b:
                        act.wait_ge(s.scored, n)
                    if later:
                        act.copy(c.KT[b][:, :, 0:WIN], c.KT[b][:, :, P:P + WIN]).then_inc(s.k_moved, 1)
                    for i in range(2):
                        for half in range(2):
                            act.wait_ge(s.kq_turned, 4 * n + 2 * i + half + 1)
                            if i == 0:
                                dst = c.QT[:, half * HALF:(half + 1) * HALF, :]
                            else:
                                if half == 0:
                                    act.wait_ge(s.k_moved, n + 1)
                                dst = c.KT[b][:, half * HALF:(half + 1) * HALF, WIN:WIN + P]
                            act.copy(dst, sc[:, half * 512:(half + 1) * 512].rearrange("p (k m) -> p k m", m=P)).then_inc(s.kq_ready, 1)
            act.activation(c.scrap[:, :], c.ones[:, 0:1], ACT.Exp).then_inc(s.table_load, 1)
            run(act, stages)
            f.scalar(act)

        @block.sync
        def _(sp):
            W1, W2 = c.d["L0_ffn_W1"], c.d["L0_ffn_W2"]
            sp.dma_start(c.W1[:, :], W1[bass.ds(layer, 1)].rearrange("l p n -> p (l n)")).then_inc(s.w_in, 16)
            sp.dma_start(c.W2[:, 0:2, :], W2[bass.ds(layer, 1), 0:256, :].rearrange("l (j p) n -> p (l j) n", p=P)).then_inc(s.w_in, 16)
            w = FFC[2][1]
            sp.dma_start(c.W2[0:w, 2, :], W2[bass.ds(layer, 1), 256:FF, :].rearrange("l p n -> p (l n)")).then_inc(s.w_in, 16)
            nxt = sp.snap((layer + 1) % (DEPTH))
            sp.wait_ge(s.v_done, NW * (base + B * NT))
            settle(sp, c)
            sp.wait_ge(s.wo_done, base + B * NT)
            settle(sp, c)
            sp.dma_start(c.Wqkv[:, :], c.d["L0_ffn_Wqkv"][bass.ds(nxt, 1)].rearrange("l p n -> p (l n)")).then_inc(s.f_next, 16)
            sp.dma_start(c.Wo[:, :, :], c.d["L0_ffn_Wo"][bass.ds(nxt, 1)].rearrange("l (j p) n -> p (l j) n", p=P)).then_inc(s.f_next, 16)
            sp.wait_ge(s.w_in, 16 * 3 * (layer + 1))
            settle(sp, c)
            sp.wait_ge(s.f_next, 32 * (layer + 1))
            settle(sp, c)


class TransformerSemaphores:
    def __init__(self, sem, nm):
        self.xq_ready, self.centred, self.scaled, self.inverted = (
            sem(nm + "_xq_ready"), sem(nm + "_centred"), sem(nm + "_scaled"), sem(nm + "_inverted"))
        self.xs_ready, self.qk_done, self.sq_done, self.ssq_done = (
            sem(nm + "_xs_ready"), sem(nm + "_qk_done"), sem(nm + "_sq_done"), sem(nm + "_ssq_done"))
        self.newton, self.t_ready, self.rot_sum = (
            sem(nm + "_newton"), sem(nm + "_t_ready"), sem(nm + "_rot_sum"))
        self.kq_turned, self.kq_ready, self.k_moved, self.scored = (
            sem(nm + "_kq_turned"), sem(nm + "_kq_ready"), sem(nm + "_k_moved"), sem(nm + "_scored"))
        self.max_done, self.exp_done = sem(nm + "_max_done"), sem(nm + "_exp_done")
        self.o_normed, self.o_turned, self.p_turned, self.pt_ready = (
            sem(nm + "_o_normed"), sem(nm + "_o_turned"), sem(nm + "_p_turned"), sem(nm + "_pt_ready"))
        self.v_done, self.v_ready, self.pv_done, self.o_ready = (
            sem(nm + "_v_done"), sem(nm + "_v_ready"), sem(nm + "_pv_done"), sem(nm + "_o_ready"))
        self.wo_done, self.x_done, self.table, self.table_load = (
            sem(nm + "_wo_done"), sem(nm + "_x_done"), sem(nm + "_table"), sem(nm + "_table_load"))
        self.w_in = sem(nm + "_w_in")
        self.fxs_ready, self.f_tok, self.f_stat, self.f_aggr = (
            sem(nm + "_fxs_ready"), sem(nm + "_f_tok"), sem(nm + "_f_stat"), sem(nm + "_f_aggr"))
        self.f_var, self.f_newton, self.f_xn, self.f_turned = (
            sem(nm + "_f_var"), sem(nm + "_f_newton"), sem(nm + "_f_xn"), sem(nm + "_f_turned"))
        self.f_xnT, self.f_h, self.f_gelu, self.f_prod = (
            sem(nm + "_f_xnT"), sem(nm + "_f_h"), sem(nm + "_f_gelu"), sem(nm + "_f_prod"))
        self.f_out, self.f_x, self.f_cols, self.f_next = (
            sem(nm + "_f_out"), sem(nm + "_f_x"), sem(nm + "_f_cols"), sem(nm + "_f_next"))
        self.f_load = sem(nm + "_f_load")


class FeedForward:
    PLACE = [(b, g * GT) for g in range(NG) for b in range(B)]
    NC = len(FFC)

    def __init__(self, c, s, layer):
        self.c, self.s, self.layer = c, s, layer
        self.tiles = (layer + 1) * (B * NT)
        self.group0 = layer * len(self.PLACE)
        self.chunk0 = layer * (len(self.PLACE) * self.NC)


    def turn_rows(self, pe, groups):
        c, s = self.c, self.s
        pe.wait_ge(s.t_ready, 4 * self.tiles)
        for g in groups:
            b, at = self.PLACE[g]
            pe.wait_ge(s.fxs_ready, 2 * self.tiles - (2 * B * NT // NG) * (1 - g // B))
            for j in range(4):
                last = pe.transpose(c.row_ps[g][:, j * P:(j + 1) * P], c.fxs[:, b, at + j * P:at + (j + 1) * P], c.ident[:, :])
            last.then_inc(s.f_tok, 1)

    def turn_back(self, pe, g):
        c, s = self.c, self.s
        pe.wait_ge(s.f_xn, 4 * self.group0 + 4 * g + 4)
        for j in range(4):
            last = pe.transpose(c.row_ps[g][:, j * P:(j + 1) * P], c.fxn[:, g % 2, j, :], c.ident[:, :])
        last.then_inc(s.f_turned, 1)

    def expand(self, pe, g, i):
        c, s = self.c, self.s
        at, w = FFC[i]
        q = self.NC * g + i
        if q >= 2:
            pe.wait_ge(s.f_prod, self.chunk0 + q - 1)
        gate, lin = c.h_ps[q % 2]
        pe.matmul(gate[0:w, :], c.W1[:, FF + at:FF + at + w], c.fxnT[:, g % 2, :], start=True, stop=True).then_inc(s.f_h, 1)
        pe.matmul(lin[0:w, :], c.W1[:, at:at + w], c.fxnT[:, g % 2, :], start=True, stop=True).then_inc(s.f_h, 1)

    def contract(self, pe, g):
        c, s, NC = self.c, self.s, self.NC
        for i, (at, w) in enumerate(FFC):
            pe.wait_ge(s.f_prod, self.chunk0 + NC * g + i + 1)
            last = pe.matmul(c.row_ps[g], c.W2[0:w, i, :], c.fh[0:w, g % 2, i, :], start=(i == 0), stop=(i == NC - 1))
        last.then_inc(s.f_out, 1)

    def tensor(self, pe):
        s, NGR = self.s, len(self.PLACE)
        pe.wait_ge(s.x_done, self.tiles)
        for g in range(NGR):
            if g > 0:
                pe.wait_ge(s.f_xnT, self.group0 + g + 1)
                self.expand(pe, g, 0)
                self.contract(pe, g - 1)
            self.expand(pe, g, 1)
            if g == 0:
                self.turn_rows(pe, (2, 3))
            elif g + 1 < NGR:
                self.turn_back(pe, g + 1)
            self.expand(pe, g, 2)
        self.contract(pe, NGR - 1)


    def statistics(self, dve, groups, between={}):
        c, s = self.c, self.s
        half = groups[0] // 2
        part = slice(8 * half, 8 * half + 8)
        for g in groups:
            dve.wait_ge(s.f_tok, self.group0 + g + 1)
            settle(dve, c)
            for j in range(4):
                dve.bn_stats(c.fstat[:, 4 * g + j, :], c.row_ps[g][:, j * P:(j + 1) * P]).then_inc(s.f_stat, 1)
        dve.wait_ge(s.f_stat, 4 * self.group0 + 4 * groups[1] + 4)
        settle(dve, c)
        for j in range(part.start, part.stop):
            dve.bn_aggr(c.fmv[:, j, :], c.fstat[:, j, :]).then_inc(s.f_aggr, 1)
        dve.wait_ge(s.f_aggr, 4 * self.group0 + 4 * groups[1] + 4)
        dve.tensor_copy(c.fvar[:, part], c.fmv[:, part, 1]).then_inc(s.f_var, 1)
        dve.wait_ge(s.f_var, 2 * self.layer + half + 1)
        rsqrt_steps(dve, s.f_newton, (2 * self.layer + half) * NEWTON, c.fvar[:, part], c.frstd[:, part], c.ftmp[:, part],
                    0.0, 1e-5, between)

    def normalise(self, dve, g):
        c, s = self.c, self.s
        if g >= 2:
            dve.wait_ge(s.f_turned, self.group0 + g - 1)
        for j in range(4):
            n = 4 * g + j
            dve.tensor_scalar(c.fxn[:, g % 2, j, :], c.row_ps[g][:, j * P:(j + 1) * P], c.fmv[:, n, 0:1], c.frstd[:, n:n + 1],
                              ALU.subtract, ALU.mult).then_inc(s.f_xn, 1)

    def vector(self, dve):
        c, s, NC, NGR = self.c, self.s, self.NC, len(self.PLACE)

        def multiply(g, i):
            w, q = FFC[i][1], NC * g + i
            dve.wait_ge(s.f_h, 2 * self.chunk0 + 2 * q + 2)
            dve.wait_ge(s.f_gelu, self.chunk0 + q + 1)
            dve.scalar_tensor_tensor(out=c.fh[0:w, g % 2, i, :], in0=c.h_ps[q % 2][1][0:w, :], scalar=c.lcols[0:w, 3 + i:4 + i],
                                     in1=c.fg[0:w, i, :], op0=ALU.add, op1=ALU.mult).then_inc(s.f_prod, 1)

        def finish(g):
            b, at = self.PLACE[g]
            dve.wait_ge(s.f_out, self.group0 + g + 1)
            dve.scalar_tensor_tensor(out=c.xA[:, b, PAD + at:PAD + at + GT], in0=c.row_ps[g], scalar=c.lcols[:, 2:3],
                                     in1=c.xB[:, b, PAD + at:PAD + at + GT], op0=ALU.add, op1=ALU.add).then_inc(s.f_x, 1)

        multiply(0, 0)
        multiply(0, 1)
        self.statistics(dve, (2, 3), {1: lambda: multiply(0, 2), 5: lambda: multiply(1, 0)})
        self.normalise(dve, 2)
        finish(0)
        multiply(1, 1)
        multiply(1, 2)
        for g in range(2, NGR):
            multiply(g, 0)
            if g + 1 < NGR:
                self.normalise(dve, g + 1)
            finish(g - 1)
            multiply(g, 1)
            multiply(g, 2)
        finish(NGR - 1)


    def scale(self, act, g):
        c, s = self.c, self.s
        act.wait_ge(s.f_turned, self.group0 + g + 1)
        if g >= 2:
            act.wait_ge(s.f_h, 2 * self.chunk0 + 2 * self.NC * (g - 1))
        act.activation(c.fxnT[:, g % 2, :], c.row_ps[g], ACT.Identity, bias=c.lcols[:, 1:2], scale=c.lcols[:, 0:1]).then_inc(s.f_xnT, 1)

    def scalar(self, act):
        c, s, NC, NGR = self.c, self.s, self.NC, len(self.PLACE)

        def gelu(g, i):
            w, q = FFC[i][1], NC * g + i
            act.wait_ge(s.f_h, 2 * self.chunk0 + 2 * q + 1)
            if g > 0:
                act.wait_ge(s.f_prod, self.chunk0 + q - NC + 1)
            act.activation(c.fg[0:w, i, :], c.h_ps[q % 2][0][0:w, :], ACT.Gelu, bias=c.lcols[0:w, 6 + i:7 + i]).then_inc(s.f_gelu, 1)

        for g in range(NGR):
            gelu(g, 0)
            if g == 0:
                self.scale(act, 1)
            gelu(g, 1)
            if 0 < g < NGR - 1:
                self.scale(act, g + 1)
            gelu(g, 2)


def residual_phase(nc, c, name, scale):
    with ExitStack() as ctx:
        _, _, sem = scope(nc, ctx)
        done = sem(name)
        with nc.Block() as block:
            @block.vector
            def _(dve):
                for b in range(B):
                    dve.scalar_tensor_tensor(out=c.X[:, b, PAD:PAD + T], in0=c.xA[:, b, PAD:PAD + T], scalar=scale, in1=c.X[:, b, PAD:PAD + T],
                                             op0=ALU.mult, op1=ALU.add).then_inc(done, 1)


def transformer(nc, c, nm, dump=None):
    norm_phase(nc, c, nm + "n", c.X, c.xA)
    with ExitStack() as ctx:
        sb, ps, sem = scope(nc, ctx)
        c.rl = sb("rl" + nm, [P, 4, NT * DH])
        with ExitStack() as low:
            sb, ps, _ = scope(nc, low)
            c.xq = [sb(f"xq{b}" + nm, [P, P]) for b in range(B)]
            c.xs = [sb(f"xs{b}" + nm, [P, WIN + P]) for b in range(B)]
            c.t1, c.t2, c.sq = (sb(x + nm, [P, 2 * INNER]) for x in ("t1", "t2", "sq"))
            c.ssq, c.rnorm, c.ntmp = (sb(x + nm, [P, 2 * HEADS]) for x in ("ssq", "rnorm", "ntmp"))
            c.mx, c.rsum = (sb(x + nm, [P, HEADS]) for x in ("mx", "rsum"))
            c.QT = sb("QT" + nm, [P, PAIRS, P])
            c.Vw = sb("Vw" + nm, [P, NW, PAIRS * DH])
            c.On = sb("On" + nm, [P, HEADS, DH])
            c.probs = sb("probs" + nm, [P, HEADS, KEYS])
            c.PT, c.OT = (sb(x + nm, [P, PAIRS * P]) for x in ("PT", "OT"))
            c.fxs, c.fxnT = sb("fxs" + nm, [P, B, T]), sb("fxnT" + nm, [P, 2, GT])
            c.fxn = sb("fxn" + nm, [P, 2, 4, P])
            c.fg, c.fh = sb("fg" + nm, [P, 3, GT]), sb("fh" + nm, [P, 2, 3, GT])
            c.fstat, c.fmv = sb("fstat" + nm, [P, B * NT, 6]), sb("fmv" + nm, [P, B * NT, 2])
            c.fvar, c.frstd, c.ftmp = (sb(x + nm, [P, B * NT]) for x in ("fvar", "frstd", "ftmp"))
            c.lcols = sb("lcols" + nm, [P, LV])
            bank = ps("banks" + nm, [P, 8 * 512])
            c.qk_ps, c.vo_ps, c.sc_ps = bank[:, 0:2048], bank[:, 2048:3072], bank[:, 3072:4096]
            part = lambda i: bank[:, i * 512:(i + 1) * 512]
            c.row_ps = [part(i) for i in range(4)]
            c.h_ps = [(part(6), part(7)), (part(4), part(5))]
            c.sems[nm] = TransformerSemaphores(sem, nm)
            with nc.Fori(0, c.depth) as layer:
                layer_phase(nc, c, layer, nm)
    residual_phase(nc, c, nm + "res", 0.5)


GATES = ("i", "f", "o", "g")
EARLY_TERMS = [(0, 0), (1, 0), (2, 0), (0, 1), (1, 1)]
LAST_TERM = (0, 2)
MOST = 1e37


def recurrence_phase(nc, c):
    with ExitStack() as ctx:
        sb, ps, sem = scope(nc, ctx)
        Wg = sb("Wgates", [P, 4, 2, P])
        Wparts = sb("Wparts", [P, 3, 3, P], BF16)
        wrest = sb("wrest", [P, 3, P])
        bias = sb("gate_bias", [1, 5, P])
        Weg = sb("Weg", [P, P])
        hbuf = [sb(f"hbuf{i}", [P, B, CH]) for i in range(2)]
        hparts, hrest = sb("hparts", [P, 3, B], BF16), sb("hrest", [P, B])
        tg, es, sg, ex, eo = sb("tg", [P, B]), sb("es", [P, 2, B]), sb("sg", [P, 2, B]), sb("ex", [P, B]), sb("eo", [P, B])
        cn, fcn = sb("cn", [P, 2, B]), sb("fcn", [P, 2, B])
        so, nso, iso, fno = sb("so", [P, B]), sb("nso", [P, B]), sb("iso", [P, B]), sb("fno", [P, B])
        ig, no, rn = sb("ig", [P, B]), sb("no", [P, B]), sb("rn", [P, B])
        g_bank = [ps(f"g_bank{i}", [P, 512]) for i in range(2)]
        s_bank = [ps(f"s_bank{i}", [P, 512]) for i in range(2)]
        o_bank = [ps(f"o_bank{i}", [P, 512]) for i in range(2)]
        e_bank = [ps(f"e_bank{i}", [P, 512]) for i in range(2)]
        w_in, zeroed, w_split, table_loaded = sem("r_w_in"), sem("r_zeroed"), sem("r_w_split"), sem("r_table_loaded")
        counted = [sem("r_" + x) for x in (
            "g_done", "s_done", "o_done", "e_done", "tg_ready", "es_ready", "ex_ready", "eo_ready", "h_ready",
            "h_first", "h_split", "rest_done", "so_done", "nso_done", "sg_done", "fno_done", "ig_done", "n_done", "no_done", "rn_done", "y_done")]
        (g_done, s_done, o_done, e_done, tg_ready, es_ready, ex_ready, eo_ready, h_ready,
         h_first, h_split, rest_done, so_done, nso_done, sg_done, fno_done, ig_done, n_done, no_done, rn_done, y_done) = counted

        with nc.Block() as block:
            @block.sync
            def _(sp):
                for i, g in enumerate(GATES):
                    sp.dma_start(Wg[:, i, :, :], c.d[f"L0_attn_W{g}"].rearrange("(a p) n -> p a n", p=P)).then_inc(w_in, 16)
                    sp.dma_start(bias[:, i, :], c.d[f"L0_attn_b{g}"].rearrange("(a n) -> a n", a=1)).then_inc(w_in, 16)
                sp.dma_start(bias[:, 4, :], c.d["L0_attn_beg"].rearrange("(a n) -> a n", a=1)).then_inc(w_in, 16)
                sp.dma_start(Weg[:, :], c.d["L0_attn_Weg"]).then_inc(w_in, 16)
                sp.wait_ge(w_in, 16 * 10)

            @block.gpsimd
            def _(pool):
                pool.memset(cn[:, :, :], 0.0).then_inc(zeroed, 1)
                pool.memset(hbuf[1][:, :, :], 0.0).then_inc(zeroed, 1)
                pool.memset(hparts[:, :, :], 0.0).then_inc(zeroed, 1)

            @block.vector
            def _(dve):
                dve.wait_ge(w_in, 16 * 10)
                W = Wg[:, 0:3, 1, :]
                dve.tensor_copy(Wparts[:, :, 0, :], W).then_inc(w_split, 1)
                dve.wait_ge(w_split, 1)
                dve.tensor_tensor(wrest[:, :, :], W, Wparts[:, :, 0, :], ALU.subtract).then_inc(w_split, 1)
                dve.wait_ge(w_split, 2)
                dve.tensor_copy(Wparts[:, :, 1, :], wrest[:, :, :]).then_inc(w_split, 1)
                dve.wait_ge(w_split, 3)
                dve.tensor_tensor(Wparts[:, :, 2, :], wrest[:, :, :], Wparts[:, :, 1, :], ALU.subtract).then_inc(w_split, 1)

        def tensor_steps(pe, it, first_round):
            def project(j, at, which):
                gate, part = which // 2, which % 2
                if gate != 0 and gate != 1:
                    bank = {2: o_bank, 3: g_bank, 4: e_bank}[gate]
                    out = bank[j][:, 0:CH * B].rearrange("p (s b) -> p b s", b=B)
                    first = part == 0
                else:
                    out = s_bank[j][:, 0:CH * 2 * B].rearrange("p (s g b) -> p g b s", g=2, b=B)[:, gate]
                    first = which == 0
                if part == 0:
                    lhsT, rhs = bias[0:1, gate, :], c.ones[0:1, 0:B * CH].rearrange("p (b s) -> p b s", b=B)
                else:
                    lhsT, rhs = Wg[:, gate, 0, :], c.xA[:, :, bass.ds(at, CH)]
                return pe.matmul(out, lhsT, rhs, start=first, stop=False, skip_group_check=True)

            def recur(out, gate, terms):
                for w_part, h_part in terms:
                    last = pe.matmul(out, Wparts[:, gate, w_part, :], hparts[:, h_part, :], start=False,
                                     stop=(w_part, h_part) == LAST_TERM, skip_group_check=True)
                return last

            if first_round:
                for which in range(9):
                    project(0, PAD, which)
                return
            for n in range(ROUND):
                k, s = divmod(n, CH)
                j = k % 2
                h = hbuf[j][:, :, s - 1] if s else hbuf[1 - j][:, :, CH - 1]
                i_out, f_out = (s_bank[j][:, (s * 2 + gate) * B:(s * 2 + gate + 1) * B] for gate in range(2))
                o_out = o_bank[j][:, s * B:(s + 1) * B]
                if n:
                    pe.wait_ge(h_ready, n)
                pe.matmul(g_bank[j][:, s * B:(s + 1) * B], Wg[:, 3, 1, :], h, start=False, stop=True,
                          skip_group_check=True).then_inc(g_done, 1)
                if n:
                    pe.wait_ge(h_split, 2 * n - 1)
                recur(i_out, 0, EARLY_TERMS)
                recur(f_out, 1, EARLY_TERMS)
                if n:
                    pe.wait_ge(h_split, 2 * n)
                recur(i_out, 0, [LAST_TERM])
                recur(f_out, 1, [LAST_TERM]).then_inc(s_done, 1)
                recur(o_out, 2, EARLY_TERMS + [LAST_TERM]).then_inc(o_done, 1)
                pe.wait_ge(tg_ready, n + 1)
                pe.matmul(e_bank[j][:, s * B:(s + 1) * B], Weg[:, :], tg[:, :], start=False, stop=True,
                          skip_group_check=True).then_inc(e_done, 1)
                if s % 2 == 1:
                    project(1 - j, it * ROUND + (PAD + (k + 1) * CH), s // 2)
                if s == 0:
                    project(1 - j, 0, 8)

        with nc.Block() as block:
            @block.tensor
            def _(pe):
                tensor_steps(pe, 0, True)

            @block.scalar
            def _(act):
                act.activation(c.scrap[:, :], c.ones[:, 0:1], ACT.Exp).then_inc(table_loaded, 1)

        with nc.Fori(0, T // ROUND) as it:
            with nc.Block() as block:
                @block.tensor
                def _(pe):
                    tensor_steps(pe, it, False)

                @block.scalar
                def _(act):
                    for n in range(ROUND):
                        k, s = divmod(n, CH)
                        j = k % 2
                        act.wait_ge(g_done, n + 1)
                        act.activation(tg[:, :], g_bank[j][:, s * B:(s + 1) * B], ACT.Tanh).then_inc(tg_ready, 1)
                        act.wait_ge(s_done, n + 1)
                        act.activation(es[:, :, :].rearrange("p g b -> p (g b)"), s_bank[j][:, s * 2 * B:(s + 1) * 2 * B],
                                       ACT.Exp, scale=-1.0).then_inc(es_ready, 1)
                        act.wait_ge(o_done, n + 1)
                        act.activation(eo[:, :], o_bank[j][:, s * B:(s + 1) * B], ACT.Exp, scale=-1.0).then_inc(eo_ready, 1)
                        if n:
                            act.wait_ge(n_done, n)
                        act.wait_ge(e_done, n + 1)
                        act.activation(ex[:, :], e_bank[j][:, s * B:(s + 1) * B], ACT.Exp).then_inc(ex_ready, 1)

                @block.vector
                def _(dve):
                    for n in range(ROUND):
                        k, s = divmod(n, CH)
                        j = k % 2
                        if s == 0 and k >= 2:
                            dve.wait_ge(y_done, k - 1)
                        dve.wait_ge(es_ready, n + 1)
                        dve.tensor_scalar(sg[:, :, :], es[:, :, :], 1.0, None, ALU.add).then_inc(sg_done, 1)
                        dve.wait_ge(eo_ready, n + 1)
                        dve.tensor_scalar(so[:, :], eo[:, :], MOST, 1.0, ALU.min, ALU.add).then_inc(so_done, 1)
                        dve.wait_ge(sg_done, 2 * n + 1)
                        dve.reciprocal(sg[:, :, :], sg[:, :, :]).then_inc(sg_done, 1)
                        dve.wait_ge(so_done, n + 1)
                        dve.tensor_tensor(nso[:, :], cn[:, 1, :], so[:, :], ALU.mult).then_inc(nso_done, 1)
                        dve.wait_ge(sg_done, 2 * n + 2)
                        dve.tensor_tensor(iso[:, :], sg[:, 0, :], so[:, :], ALU.mult)
                        dve.wait_ge(nso_done, n + 1)
                        dve.tensor_tensor(fno[:, :], nso[:, :], sg[:, 1, :], ALU.mult).then_inc(fno_done, 1)
                        dve.tensor_tensor(fcn[:, :, :], cn[:, :, :], sg[:, 1:2, :].to_broadcast([P, 2, B]), ALU.mult)
                        dve.tensor_tensor(ig[:, :], sg[:, 0, :], tg[:, :], ALU.mult).then_inc(ig_done, 1)
                        dve.wait_ge(fno_done, n + 1)
                        dve.wait_ge(ex_ready, n + 1)
                        for b in range(B):
                            last = dve.scalar_tensor_tensor(out=no[:, b:b + 1], in0=ex[:, b:b + 1], scalar=iso[:, b:b + 1],
                                                            in1=fno[:, b:b + 1], op0=ALU.mult, op1=ALU.add)
                        last.then_inc(no_done, 1)
                        dve.wait_ge(ig_done, n + 1)
                        dve.tensor_tensor(cn[:, 0, :], ig[:, :], fcn[:, 0, :], ALU.add)
                        dve.wait_ge(no_done, n + 1)
                        dve.reciprocal(rn[:, :], no[:, :]).then_inc(rn_done, 1)
                        dve.wait_ge(rn_done, n + 1)
                        h = hbuf[j][:, :, s]
                        dve.tensor_tensor(h, cn[:, 0, :], rn[:, :], ALU.mult).then_inc(h_ready, 1)
                        dve.tensor_tensor(hparts[:, 0, :], cn[:, 0, :], rn[:, :], ALU.mult).then_inc(h_first, 1)
                        dve.wait_ge(h_first, n + 1)
                        dve.tensor_tensor(hparts[:, 1, :], h, hparts[:, 0, :], ALU.subtract).then_inc(h_split, 1)
                        dve.tensor_tensor(hrest[:, :], h, hparts[:, 0, :], ALU.subtract).then_inc(rest_done, 1)
                        dve.wait_ge(rest_done, n + 1)
                        dve.tensor_tensor(hparts[:, 2, :], hrest[:, :], hparts[:, 1, :], ALU.subtract).then_inc(h_split, 1)
                        for b in range(B):
                            last = dve.scalar_tensor_tensor(out=cn[:, 1, b:b + 1], in0=ex[:, b:b + 1], scalar=sg[:, 0, b:b + 1],
                                                            in1=fcn[:, 1, b:b + 1], op0=ALU.mult, op1=ALU.add)
                        last.then_inc(n_done, 1)
                        dve.wait_ge(n_done, n + 1)

                @block.gpsimd
                def _(pool):
                    for k in range(ROUND // CH):
                        pool.wait_ge(h_ready, (k + 1) * CH)
                        at = it * ROUND + (PAD + k * CH)
                        pool.tensor_tensor(c.xB[:, :, bass.ds(at, CH)], hbuf[k % 2][:, :, :], c.xA[:, :, bass.ds(at, CH)],
                                           ALU.add).then_inc(y_done, 1)
            for semaphore in counted:
                nc.gpsimd.sem_clear(semaphore)
            nc.all_engine_barrier()


def experts_phase(nc, c, nm):
    E, N16 = EXPERTS, B * NT
    EP = E + 8 - TOPK
    with ExitStack() as ctx:
        sb, ps, sem = scope(nc, ctx)
        wg1, wg2, bg1 = sb("wg1" + nm, [P, GH]), sb("wg2" + nm, [GH, 2 * E]), sb("bg1" + nm, [GH, 1])
        bg2, We, be = sb("bg2" + nm, [P, 2 * E]), sb("We" + nm, [P, E, P]), sb("be" + nm, [E, P])
        hT = sb("hT" + nm, [GH, B, T])
        lg, pb, gates = sb("lg" + nm, [P, N16, E]), sb("pb" + nm, [P, N16, EP]), sb("gates" + nm, [P, N16, EP])
        mx, sm = sb("emx" + nm, [P, N16]), sb("esm" + nm, [P, N16])
        top, drop = sb("top" + nm, [P, N16, 8]), sb("drop" + nm, [P, N16, 8])
        gT = sb("gT" + nm, [E, B, T])
        xt = [sb(f"ext{b}" + nm, [P, P]) for b in range(B)]
        y = [[sb(f"ey{b}{i}" + nm, [P, P]) for i in range(2)] for b in range(B)]
        gates_now = [sb(f"gates_now{b}" + nm, [P, E]) for b in range(B)]
        with ExitStack() as low:
            _, ps, sem = scope(nc, low)
            h_ps = [ps(f"eh{i}" + nm, [P, 512]) for i in range(4)]
            l_ps = ps("el" + nm, [P, 512])
            w_in, small_in, h_done, gelu, logits = (sem(nm + x) for x in ("w_in", "small_in", "h_done", "gelu", "logits"))
            soft, exped, topped = (sem(nm + x) for x in ("soft", "exped", "topped"))
            gt_turned, gt_ready, filled, loaded = sem(nm + "gt_turned"), sem(nm + "gt_ready"), sem(nm + "filled"), sem(nm + "loaded")
            with nc.Block() as block:
                @block.sync
                def _(sp):
                    with nc.allow_non_contiguous_dma(reason="a short vector to a column"):
                        sp.dma_start(bg1[:, :], c.d["L1_ffn_bg1"].rearrange("(p a) -> p a", a=1)).then_inc(small_in, 16)
                    sp.dma_start(wg1[:, :], c.d["L1_ffn_wg1"]).then_inc(small_in, 16)
                    sp.dma_start(wg2[:, :], c.d["L1_ffn_wg2"]).then_inc(small_in, 16)
                    sp.dma_start(bg2[:, :], c.d["L1_ffn_bg2"].partition_broadcast(P)).then_inc(small_in, 16)
                    sp.dma_start(be[:, :], c.d["L1_ffn_be"]).then_inc(small_in, 16)
                    sp.dma_start(We[:, :, :], c.d["L1_ffn_We"].rearrange("e p n -> p e n")).then_inc(w_in, 16)
                    sp.wait_ge(w_in, 16)
                    sp.wait_ge(small_in, 16 * 5)

                @block.gpsimd
                def _(pool):
                    pool.memset(pb[:, :, E:EP], -1.0).then_inc(filled, 1)
                    pool.memset(drop[:, :, TOPK:8], -1.0).then_inc(filled, 1)

                @block.tensor
                def _(pe):
                    pe.wait_ge(small_in, 16 * 5)
                    for g in range(4):
                        pe.matmul(h_ps[g][0:GH, :], wg1[:, :], c.xA[:, g // 2, PAD + (g % 2) * GT:PAD + (g % 2 + 1) * GT],
                                  start=True, stop=True).then_inc(h_done, 1)
                    for n in range(N16):
                        if n % 4 == 0:
                            pe.wait_ge(gelu, n // 4 + 1)
                        last = pe.matmul(l_ps[:, n * E:(n + 1) * E], hT[:, n // NT, (n % NT) * P:(n % NT + 1) * P], wg2[:, 0:E],
                                         start=True, stop=True)
                    last.then_inc(logits, 1)
                    for g in range(4):
                        pe.wait_ge(topped, N16 + 1)
                        for j in range(4):
                            last = pe.transpose(h_ps[g][0:E, j * P:(j + 1) * P], gates[:, 4 * g + j, 0:E], c.ident[:, :])
                        last.then_inc(gt_turned, 1)

                @block.scalar
                def _(act):
                    for g in range(4):
                        act.wait_ge(h_done, g + 1)
                        act.activation(hT[:, g // 2, (g % 2) * GT:(g % 2 + 1) * GT], h_ps[g][0:GH, :], ACT.Gelu, bias=bg1[:, :]).then_inc(gelu, 1)
                    act.wait_ge(soft, 3)
                    act.activation(pb[:, :, 0:E], lg[:, :, :], ACT.Exp).then_inc(exped, 1)
                    for g in range(4):
                        act.wait_ge(gt_turned, g + 1)
                        act.copy(gT[:, g // 2, (g % 2) * GT:(g % 2 + 1) * GT], h_ps[g][0:E, :]).then_inc(gt_ready, 1)

                @block.vector
                def _(dve):
                    k = 0

                    def step(instruction):
                        nonlocal k
                        k += 1
                        instruction.then_inc(soft, 1)
                        dve.wait_ge(soft, k)

                    def wide(a, w=E):
                        return a.unsqueeze(2).to_broadcast([P, N16, w])

                    dve.wait_ge(logits, 1)
                    dve.wait_ge(filled, 2)
                    step(dve.tensor_tensor(lg[:, :, :], l_ps[:, 0:N16 * E].rearrange("p (n e) -> p n e", e=E),
                                           bg2[:, 0:E].unsqueeze(1).to_broadcast([P, N16, E]), ALU.add))
                    step(dve.tensor_reduce(mx[:, :], lg[:, :, :], AX.X, ALU.max))
                    step(dve.tensor_tensor(lg[:, :, :], lg[:, :, :], wide(mx[:, :]), ALU.subtract))
                    dve.wait_ge(exped, 1)
                    step(dve.tensor_reduce(sm[:, :], pb[:, :, 0:E], AX.X, ALU.add))
                    step(dve.reciprocal(sm[:, :], sm[:, :]))
                    step(dve.tensor_tensor(pb[:, :, 0:E], pb[:, :, 0:E], wide(sm[:, :]), ALU.mult))
                    for n in range(N16):
                        last = dve.max(top[:, n, :], pb[:, n, 0:E])
                    step(last)
                    step(dve.tensor_copy(drop[:, :, 0:TOPK], top[:, :, 0:TOPK]))
                    for n in range(N16):
                        dve.match_replace(out=gates[:, n, :], in_to_replace=drop[:, n, :], in_values=pb[:, n, :],
                                          imm_value=0.0).then_inc(topped, 1)
                    dve.wait_ge(topped, N16)
                    dve.tensor_tensor(gates[:, :, 0:E], pb[:, :, 0:E], gates[:, :, 0:E], ALU.subtract).then_inc(topped, 1)

        with ExitStack() as low:
            _, ps, sem = scope(nc, low)
            z_ps, o_ps = ps("ez" + nm, [P, E * P]), ps("eo" + nm, [P, 512])
            x_taken, z_done, gates_taken, y_done, turned, added = (
                sem(nm + x) for x in ("x_taken", "z_done", "gates_taken", "y_done", "turned", "added"))
            Z, BANKS = 4, E // 4
            start_at_one(nc, [added] + 2 * BANKS * [z_done] + E * [y_done])
            with nc.Block() as block:
                def tiles(eng, body, last):
                    def number(b, t):
                        return b, t, t * B + b
                    body(*number(0, 0), None)
                    body(*number(1, 0), number(0, 0))
                    with eng.Fori(1, NT) as t:
                        body(*number(0, t), number(1, t - 1))
                        body(*number(1, t), number(0, t))
                    last(*number(1, NT - 1))

                @block.gpsimd
                def _(pool):
                    def body(b, t, n, before):
                        pool.wait_ge(z_done, BANKS * n + BANKS)
                        settle(pool, c)
                        pool.tensor_copy(xt[b][:, :], c.xA[:, b, bass.ds(PAD + t * P, P)]).then_inc(x_taken, 1)
                    tiles(pool, body, lambda b, t, n: None)

                @block.tensor
                def _(pe):
                    def output(b, t, n):
                        pe.wait_ge(y_done, (n + 1) * E + E)
                        pe.wait_ge(added, n + 1)
                        for i in range(2):
                            pe.matmul(o_ps[:, 0:P], y[b][i][:, :], c.ident[:, :], start=(i == 0), stop=False)
                        pe.matmul(o_ps[:, 0:P], be[:, :], gT[:, b, bass.ds(t * P, P)], start=False, stop=True).then_inc(turned, 1)

                    def body(b, t, n, before):
                        pe.wait_ge(x_taken, n + 1)
                        for i in range(BANKS):
                            if i == 2 and before:
                                output(*before)
                            pe.wait_ge(y_done, n * E + Z * (i + 1))
                            pe.matmul(z_ps[:, i * 512:(i + 1) * 512], xt[b][:, :],
                                      We[:, Z * i:Z * i + Z, :].rearrange("p e n -> p (e n)"), start=True, stop=True).then_inc(z_done, 1)
                    tiles(pe, body, output)

                @block.vector
                def _(dve):
                    def add(b, t, n):
                        dve.wait_ge(turned, n + 1)
                        at = PAD + t * P
                        dve.scalar_tensor_tensor(out=c.X[:, b, bass.ds(at, P)], in0=o_ps[:, 0:P], scalar=0.5,
                                                 in1=c.X[:, b, bass.ds(at, P)], op0=ALU.mult, op1=ALU.add).then_inc(added, 1)

                    def body(b, t, n, before):
                        dve.tensor_copy(gates_now[b][:, :], gates[:, bass.ds(b * NT + t, 1), 0:E].rearrange("p n e -> p (n e)")).then_inc(gates_taken, 1)
                        dve.wait_ge(gates_taken, n + 1)
                        for e in range(E):
                            if e % Z == 0:
                                dve.wait_ge(z_done, BANKS * n + e // Z + 1 + 2 * BANKS)
                            if e == 3 * Z and before:
                                add(*before)
                            gate, z, acc = gates_now[b][:, e:e + 1], z_ps[:, e * P:(e + 1) * P], y[b][e % 2][:, :]
                            if e < 2:
                                dve.tensor_scalar(acc, z, gate, None, ALU.mult).then_inc(y_done, 1)
                            else:
                                dve.wait_ge(y_done, n * E + e - 1 + E)
                                dve.scalar_tensor_tensor(out=acc, in0=z, scalar=gate, in1=acc, op0=ALU.mult, op1=ALU.add).then_inc(y_done, 1)
                    tiles(dve, body, add)


def full_attention_phase(nc, c):
    BAND = P // 4
    with ExitStack() as ctx:
        sb, ps, sem = scope(nc, ctx)
        w, ow, owT = sb("w_qkv", [P, 3 * P]), sb("ow", [P, P]), sb("owT", [P, P])
        xh, wh = sb("xh", [P, B, T], F16), sb("wh", [P, 3 * P], F16)
        qT, kT = sb("qT", [P, B, T]), sb("kT", [P, B, T])
        V = sb("V", [P, B * NT, P])
        qs = [sb(f"qs{b}", [P, P]) for b in range(B)]
        pr = [sb(f"apr{b}", [P, T]) for b in range(B)]
        pT = [sb(f"apT{b}", [P, T]) for b in range(B)]
        yT = [sb(f"ayT{b}", [P, P]) for b in range(B)]
        mx, sm = [sb(f"amx{b}", [P, 1]) for b in range(B)], [sb(f"asm{b}", [P, 1]) for b in range(B)]
        bank = ps("a_banks", [P, 8 * 512])
        part = lambda i, n=1: bank[:, i * 512:(i + n) * 512]
        w_in, rounded, made, evacuated, turned_w = sem("fa_w_in"), sem("fa_rounded"), sem("fa_made"), sem("fa_evacuated"), sem("fa_turned_w")
        with nc.Block() as block:
            @block.sync
            def _(sp):
                sp.dma_start(w[:, :], c.d["L1_attn_weight_qkv"]).then_inc(w_in, 16)
                sp.dma_start(ow[:, :], c.d["L1_attn_out_w"]).then_inc(w_in, 16)

            @block.vector
            def _(dve):
                xa = c.xA[:, :, PAD:PAD + T]
                dve.tensor_copy(xh[:, :, :], xa).then_inc(rounded, 1)
                dve.wait_ge(w_in, 32)
                dve.tensor_copy(wh[:, :], w[:, :]).then_inc(rounded, 1)
                dve.wait_ge(rounded, 2)
                for lo in (0, P - BAND):
                    rows = slice(lo, lo + BAND)
                    dve.tensor_copy(c.xA[rows, :, PAD:PAD + T], xh[rows, :, :]).then_inc(rounded, 1)
                    dve.tensor_copy(w[rows, :], wh[rows, :]).then_inc(rounded, 1)

            @block.tensor
            def _(pe):
                pe.wait_ge(rounded, 6)
                for what in range(2):
                    for g in range(4):
                        pe.matmul(part(4 * what + g), w[:, what * P:(what + 1) * P],
                                  c.xA[:, g // 2, PAD + (g % 2) * GT:PAD + (g % 2 + 1) * GT], start=True, stop=True).then_inc(made, 1)
                for n in range(B * NT):
                    if n % 4 == 0:
                        pe.wait_ge(evacuated, n // 4 + 1)
                    at = PAD + (n % NT) * P
                    last = pe.matmul(part(n // 4)[:, (n % 4) * P:(n % 4 + 1) * P], c.xA[:, n // NT, at:at + P], w[:, 2 * P:3 * P],
                                     start=True, stop=True)
                    if n % 4 == 3:
                        last.then_inc(made, 1)
                pe.wait_ge(evacuated, 8)
                pe.transpose(part(4)[:, 0:P], ow[:, :], c.ident[:, :]).then_inc(turned_w, 1)

            @block.scalar
            def _(act):
                for what in range(2):
                    for g in range(4):
                        act.wait_ge(made, 4 * what + g + 1)
                        act.activation((qT, kT)[what][:, g // 2, (g % 2) * GT:(g % 2 + 1) * GT], part(4 * what + g), ACT.Copy,
                                       scale=(float(P) ** -0.5, 1.0)[what]).then_inc(evacuated, 1)
                for g in range(4):
                    act.wait_ge(made, 8 + g + 1)
                    act.copy(V[:, 4 * g:4 * g + 4, :].rearrange("p n d -> p (n d)"), part(g)).then_inc(evacuated, 1)
                act.wait_ge(turned_w, 1)
                act.copy(owT[:, :], part(4)[:, 0:P]).then_inc(evacuated, 1)

        q_taken, scored, maxed, negated, exped = sem("fa_q_taken"), sem("fa_scored"), sem("fa_maxed"), sem("fa_negated"), sem("fa_exped")
        inverted, normed, p_turned, pt_ready = sem("fa_inverted"), sem("fa_normed"), sem("fa_p_turned"), sem("fa_pt_ready")
        y_done, y_ready, o_done, added = sem("fa_y_done"), sem("fa_y_ready"), sem("fa_o_done"), sem("fa_added")
        start_at_one(nc, [scored, exped, pt_ready, y_ready, added, p_turned, y_done])
        s_ps, t_ps, y_ps, o_ps = [part(0, 2), part(2, 2)], part(4, 2), part(6), part(7)
        with nc.Block() as block:
            def rounds(eng, begin, rest):
                for b in range(B):
                    begin(b, 0, b)
                with eng.Fori(0, NT - 1) as t:
                    rest(t, True)
                rest(NT - 1, False)

            @block.gpsimd
            def _(pool):
                with pool.Fori(0, NT) as t:
                    for b in range(B):
                        n = t * B + b
                        pool.wait_ge(scored, t * B + 1)
                        settle(pool, c)
                        pool.tensor_copy(qs[b][:, :], qT[:, b, bass.ds(t * P, P)]).then_inc(q_taken, 1)

            @block.tensor
            def _(pe):
                def score(b, t, n):
                    pe.wait_ge(q_taken, n + 1)
                    if not is_zero(t):
                        pe.wait_ge(exped, n)
                    for i in range(2):
                        last = pe.matmul(s_ps[b][:, i * 512:(i + 1) * 512], qs[b][:, :], kT[:, b, i * 512:(i + 1) * 512],
                                         start=True, stop=True)
                    last.then_inc(scored, 1)

                def turn(b, t, n):
                    pe.wait_ge(normed, n + 1)
                    pe.wait_ge(pt_ready, n + 1)
                    for k in range(NT):
                        last = pe.transpose(t_ps[:, k * P:(k + 1) * P], pr[b][:, k * P:(k + 1) * P], c.ident[:, :])
                    last.then_inc(p_turned, 1)

                def attend(b, t, n):
                    pe.wait_ge(pt_ready, n + 1 + 1)
                    pe.wait_ge(y_ready, n + 1)
                    for k in range(NT):
                        last = pe.matmul(y_ps[:, 0:P], V[:, b * NT + k, :], pT[b][:, k * P:(k + 1) * P], start=(k == 0), stop=(k == NT - 1))
                    last.then_inc(y_done, 1)

                def output(b, t, n):
                    pe.wait_ge(y_ready, n + 1 + 1)
                    pe.wait_ge(added, n + 1)
                    pe.matmul(o_ps[:, 0:P], owT[:, :], yT[b][:, :], start=True, stop=True).then_inc(o_done, 1)

                def rest(t, more):
                    for b in range(B):
                        turn(b, t, t * B + b)
                        if b:
                            output(b - 1, t, t * B + b - 1)
                        if more:
                            score(b, t + 1, (t + 1) * B + b)
                        attend(b, t, t * B + b)
                    output(B - 1, t, t * B + B - 1)
                rounds(pe, score, rest)

            @block.vector
            def _(dve):
                def largest(b, t, n):
                    dve.wait_ge(scored, n + 1 + 1)
                    dve.tensor_reduce(mx[b][:, :], s_ps[b], AX.X, ALU.max).then_inc(maxed, 1)
                    dve.wait_ge(maxed, n + 1)
                    dve.tensor_scalar(mx[b][:, :], mx[b][:, :], -1.0, None, ALU.mult).then_inc(negated, 1)

                def rest(t, more):
                    for b in range(B):
                        n = t * B + b
                        dve.wait_ge(exped, n + 1 + 1)
                        dve.reciprocal(sm[b][:, :], sm[b][:, :]).then_inc(inverted, 1)
                        dve.wait_ge(inverted, n + 1)
                        dve.tensor_scalar(pr[b][:, :], pr[b][:, :], sm[b][:, 0:1], None, ALU.mult).then_inc(normed, 1)
                    for b in range(B):
                        n = t * B + b
                        if more:
                            largest(b, t + 1, n + B)
                        dve.wait_ge(o_done, n + 1)
                        at = t * P + PAD
                        bias = c.cols[:, c.col["L1_attn_out_b"]:c.col["L1_attn_out_b"] + 1]
                        dve.scalar_tensor_tensor(out=c.X[:, b, bass.ds(at, P)], in0=o_ps[:, 0:P], scalar=bias,
                                                 in1=c.X[:, b, bass.ds(at, P)], op0=ALU.add, op1=ALU.add).then_inc(added, 1)
                rounds(dve, largest, rest)

            @block.scalar
            def _(act):
                act.activation(c.scrap[:, :], c.ones[:, 0:1], ACT.Exp).then_inc(turned_w, 1)

                def exponent(b, t, n):
                    act.wait_ge(negated, n + 1)
                    if not is_zero(t):
                        act.wait_ge(p_turned, n)
                    act.activation(pr[b][:, :], s_ps[b], ACT.Exp, bias=mx[b][:, 0:1], accum_out=sm[b][:, 0:1]).then_inc(exped, 1)

                def rest(t, more):
                    for b in range(B):
                        n = t * B + b
                        act.wait_ge(p_turned, n + 1 + 1)
                        act.wait_ge(y_done, t * B + 1)
                        act.copy(pT[b][:, :], t_ps).then_inc(pt_ready, 1)
                        if more:
                            exponent(b, t + 1, n + B)
                        act.wait_ge(y_done, n + 1 + 1)
                        act.copy(yT[b][:, :], y_ps[:, 0:P]).then_inc(y_ready, 1)
                rounds(act, exponent, rest)


def output_phase(nc, c, src, out):
    with ExitStack() as ctx:
        sb, ps, sem = scope(nc, ctx)
        turned = [ps(f"o_turned{i}", [P, 4, P]) for i in range(4)]
        ot = sb("ot", [P, B * NT, P])
        o_turned, o_copied, stored = sem("o_turned"), sem("o_copied"), sem("stored")
        with nc.Block() as block:
            @block.tensor
            def _(pe):
                for g in range(4):
                    for j in range(4):
                        b, t = g // 2, (g % 2) * 4 + j
                        last = pe.transpose(turned[g][:, j, :], src[:, b, PAD + t * P:PAD + (t + 1) * P], c.ident[:, :])
                    last.then_inc(o_turned, 1)

            @block.vector
            def _(dve):
                for g in range(4):
                    dve.wait_ge(o_turned, g + 1)
                    dve.tensor_copy(ot[:, 4 * g:4 * g + 4, :], turned[g][:, :, :]).then_inc(o_copied, 1)

            @block.sync
            def _(sp):
                for g in range(4):
                    b, t = g // 2, (g % 2) * 4
                    sp.wait_ge(o_copied, g + 1)
                    sp.dma_start(out[b, t * P:(t + 4) * P, :].rearrange("(t p) f -> p t f", p=P),
                                 ot[:, 4 * g:4 * g + 4, :]).then_inc(stored, 16)
                sp.wait_ge(stored, 16 * 4)


def program(nc, names, *aps):
    d = dict(zip(names, aps))
    out = aps[-1]
    with ExitStack() as ctx:
        sb, ps, sem = scope(nc, ctx)
        c = Chip()
        c.d, c.sems = d, {}
        c.settled = sem("settled")
        stage = 5
        c.depth = DEPTH
        c.X, c.xA, c.xB = (sb(x, [P, B, PAD + T + CH]) for x in ("X", "xA", "xB"))
        c.ident, c.identb = sb("ident", [P, P]), sb("identb", [P, P], BF16)
        c.ones, c.scrap = sb("ones", [P, P]), sb("scrap", [P, 1])
        c.cols = sb("cols", [P, P])
        with ExitStack() as ctx2:
            sb, ps, sem = scope(nc, ctx2)
            c.mask = sb("mask", [P, NT, KEYS], BF16)
            c.rope = sb("rope", [P, 4, NT, DH])
            c.qks = sb("qks", [P, 4, DEPTH * DH])
            c.Wqkv, c.Wo = sb("Wqkv", [P, 3 * INNER]), sb("Wo", [P, PAIRS, P])
            c.W1, c.W2 = sb("W1", [P, 2 * FF]), sb("W2", [P, 3, P])
            c.KT = [sb(f"KT{b}", [P, PAIRS, WIN + P]) for b in range(B)]
            load_phase(nc, c, d)
            transformer(nc, c, "a")
            if stage >= 1:
                norm_phase(nc, c, "rn", c.X, c.xA)
                recurrence_phase(nc, c)
                norm_phase(nc, c, "ry", c.xB, c.xA, affine=("L0_attn_gamma", "L0_attn_beta"))
                residual_phase(nc, c, "rres", 1.0)
            if stage >= 2:
                transformer(nc, c, "b")
        if stage >= 3:
            norm_phase(nc, c, "norm_e", c.X, c.xA)
            experts_phase(nc, c, "moe1")
        if stage >= 4:
            norm_phase(nc, c, "norm_f", c.X, c.xA)
            full_attention_phase(nc, c)
        if stage >= 5:
            norm_phase(nc, c, "norm_h", c.X, c.xA)
            experts_phase(nc, c, "moe2")
        output_phase(nc, c, c.X, out)


_INS = ['L0_attn_x', 'L0_attn_Wi', 'L0_attn_bi', 'L0_attn_Wf', 'L0_attn_bf', 'L0_attn_Wg', 'L0_attn_bg', 'L0_attn_Wo',
        'L0_attn_bo', 'L0_attn_Weg', 'L0_attn_beg', 'L0_attn_gamma', 'L0_attn_beta', 'L0_ffn_Wqkv', 'L0_ffn_q_scale',
        'L0_ffn_k_scale', 'L0_ffn_Wo', 'L0_ffn_ln_g', 'L0_ffn_ln_b', 'L0_ffn_W1', 'L0_ffn_b1', 'L0_ffn_W2', 'L0_ffn_b2',
        'L1_attn_weight_qkv', 'L1_attn_out_w', 'L1_attn_out_b', 'L1_ffn_wg1', 'L1_ffn_bg1', 'L1_ffn_wg2', 'L1_ffn_bg2',
        'L1_ffn_We', 'L1_ffn_be']


def kernel(**inputs):
    import concourse.bacc as _bacc
    from concourse.bass_utils import run_bass_kernel_spmd as _run

    nc = _bacc.Bacc("TRN2", target_bir_lowering=False, num_devices=1)
    arrays = {name: np.ascontiguousarray(inputs[name]) for name in _INS}
    arrays["rope"] = rope_tables()
    arrays["mask"] = band_mask()
    args = [nc.dram_tensor(f"in_{k}", a.shape, mybir.dt.from_np(a.dtype), kind="ExternalInput").ap() for k, a in arrays.items()]
    args.append(nc.dram_tensor("out", (B, T, P), F32, kind="ExternalOutput").ap())
    program(nc, list(arrays), *args)
    r = _run(nc, [{f"in_{k}": a for k, a in arrays.items()}], core_ids=[0])
    return r.results[0]["out"]
```
